# Optimizing a Trainium2 kernel written in Bass

```python
import numpy as np
import jax
import jax.numpy as jnp

def _softmax(x, axis=-1):
    return jax.nn.softmax(x, axis=axis)
def _gelu(x):
    return jax.nn.gelu(x, approximate=True)
def _silu(x):
    return jax.nn.silu(x)
def _sigmoid(x):
    return jax.nn.sigmoid(x)
def _layernorm(x, axis=-1, eps=1e-5):
    m = jnp.mean(x, axis=axis, keepdims=True)
    v = jnp.var(x, axis=axis, keepdims=True)
    return (x - m) / jnp.sqrt(v + eps)
def _scatter_add(tgt, idx, src, axis=0):
    return tgt.at[idx].add(src)
def _segment_sum(src, seg, n):
    return jax.ops.segment_sum(src, seg, n)

kernel_name = 'mk_conv_attn_hybrid_d4_conv_nhwc128_f8d5cb'

def setup_inputs(seed: int = 0):
    np.random.seed(seed)
    _w = jnp.asarray
    def _rec_inputs():
        import jax
        import jax.numpy as jnp
        _gk = jax.random.key(seed)
        x = -0.0005207 + 1.001 * jax.random.normal(jax.random.fold_in(_gk, 1), (4, 64, 64, 128), jnp.float32)
        return x
    x = _rec_inputs()
    def _L0_conv_setup():
        import jax, jax.numpy as jnp
        import numpy as np
        from jax import lax
        D_MODEL, D_INNER, D_STATE, DT_RANK, KDIR = (64, 128, 16, 4, 4)

        def _silu(x):
            return x * jax.nn.sigmoid(x)

        def _conv1x1(x, w):
            return jnp.einsum('bhwc,oc->bhwo', x, w)

        def _bn(x, g, b):
            return x * g + b

        def _conv3x3(x, w, b):
            y = lax.conv_general_dilated(x, w, (1, 1), 'SAME', dimension_numbers=('NHWC', 'HWIO', 'NHWC'))
            return y + b

        def _ss2d(x, in_proj_w, dw_w, dw_b, x_proj_w, dt_w, dt_b, A_logs, Ds, ln_g, ln_b, out_proj_w):
            B, H, W, _ = x.shape
            L = H * W
            xz = jnp.einsum('bhwd,ed->bhwe', x, in_proj_w)
            xh, z = jnp.split(xz, 2, axis=-1)
            xh = lax.conv_general_dilated(xh, dw_w, (1, 1), 'SAME', dimension_numbers=('NHWC', 'HWIO', 'NHWC'), feature_group_count=D_INNER) + dw_b
            xh = _silu(xh)
            x1 = xh.transpose(0, 3, 1, 2).reshape(B, D_INNER, L)
            x2 = xh.transpose(0, 3, 2, 1).reshape(B, D_INNER, L)
            xs = jnp.stack([x1, x2, x1[:, :, ::-1], x2[:, :, ::-1]], axis=1)
            x_dbl = jnp.einsum('bkdl,kcd->bkcl', xs, x_proj_w)
            dts = jnp.einsum('bkrl,kdr->bkdl', x_dbl[:, :, :DT_RANK], dt_w) + dt_b[None, :, :, None]
            Bs = x_dbl[:, :, DT_RANK:DT_RANK + D_STATE]
            Cs = x_dbl[:, :, DT_RANK + D_STATE:]
            delta = jax.nn.softplus(dts)
            A = -jnp.exp(A_logs).reshape(KDIR, D_INNER, D_STATE)
            Dk = Ds.reshape(KDIR, D_INNER)

            def step(h, inp):
                d, u, b, c = inp
                dA = jnp.exp(d[..., None] * A)
                h = dA * h + (d * u)[..., None] * b[:, :, None, :]
                y = jnp.sum(h * c[:, :, None, :], axis=-1)
                return (h, y)
            h0 = jnp.zeros((B, KDIR, D_INNER, D_STATE), xh.dtype)
            seq = (delta.transpose(3, 0, 1, 2), xs.transpose(3, 0, 1, 2), Bs.transpose(3, 0, 1, 2), Cs.transpose(3, 0, 1, 2))
            _, ys = lax.scan(step, h0, seq)
            y = ys.transpose(1, 2, 3, 0) + Dk[None, :, :, None] * xs
            wh = y[:, 1].reshape(B, D_INNER, W, H).transpose(0, 1, 3, 2).reshape(B, D_INNER, L)
            iwh = y[:, 3, :, ::-1].reshape(B, D_INNER, W, H).transpose(0, 1, 3, 2).reshape(B, D_INNER, L)
            yc = y[:, 0] + y[:, 2, :, ::-1] + wh + iwh
            yc = yc.transpose(0, 2, 1).reshape(B, H, W, D_INNER)
            mu = yc.mean(-1, keepdims=True)
            var = yc.var(-1, keepdims=True)
            yc = (yc - mu) / jnp.sqrt(var + 1e-05) * ln_g + ln_b
            yc = yc * _silu(z)
            return jnp.einsum('bhwe,de->bhwd', yc, out_proj_w)

        def _forward(x, cv1_w, cv1_g, cv1_b, in_proj_w, dw_w, dw_b, x_proj_w, dt_w, dt_b, A_logs, Ds, ln_g, ln_b, out_proj_w, cv2_w, cv2_g, cv2_b, bn0_g, bn0_b, c1_w, c1_b, bn1_g, bn1_b, c2_w, c2_b, bn2_g, bn2_b, c3_w, c3_b, cv_w, cv_g, cv_b, cv3_w, cv3_g, cv3_b):
            left, right = jnp.split(x, 2, axis=-1)
            right = _silu(_bn(_conv1x1(right, cv1_w), cv1_g, cv1_b))
            xr = _ss2d(right, in_proj_w, dw_w, dw_b, x_proj_w, dt_w, dt_b, A_logs, Ds, ln_g, ln_b, out_proj_w)
            l = _silu(_bn(_conv1x1(left, cv2_w), cv2_g, cv2_b))
            l = _bn(l, bn0_g, bn0_b)
            l = jax.nn.relu(_bn(_conv3x3(l, c1_w, c1_b), bn1_g, bn1_b))
            l = jax.nn.relu(_bn(_conv3x3(l, c2_w, c2_b), bn2_g, bn2_b))
            l = jax.nn.relu(_conv1x1(l, c3_w) + c3_b)
            xr = _silu(_bn(_conv1x1(xr, cv_w), cv_g, cv_b))
            out = jnp.concatenate([l, xr], axis=-1)
            out = _silu(_bn(_conv1x1(out, cv3_w), cv3_g, cv3_b))
            B, H, W, C = out.shape
            out = out.reshape(B, H, W, 2, C // 2).swapaxes(-1, -2).reshape(B, H, W, C)
            return out + x
        ks = iter(jax.random.split(jax.random.key(seed), 64))

        def rn(shape, s):
            return jax.random.normal(next(ks), shape, jnp.float32) * s
        D, DI, N, R, Kd = (D_MODEL, D_INNER, D_STATE, DT_RANK, KDIR)
        inp = {}
        inp['x'] = jax.random.normal(next(ks), (4, 64, 64, 128), jnp.float32)
        inp['cv1_w'] = rn((D, D), 0.1)
        inp['cv1_g'] = 1.0 + rn((D,), 0.05)
        inp['cv1_b'] = rn((D,), 0.05)
        inp['in_proj_w'] = rn((2 * DI, D), 0.08)
        inp['dw_w'] = rn((3, 3, 1, DI), 0.1)
        inp['dw_b'] = rn((DI,), 0.05)
        inp['x_proj_w'] = rn((Kd, R + 2 * N, DI), 0.08)
        inp['dt_w'] = rn((Kd, DI, R), 0.1)
        inp['dt_b'] = rn((Kd, DI), 0.1)
        inp['A_logs'] = jnp.tile(jnp.log(jnp.arange(1.0, N + 1.0, dtype=jnp.float32)), (Kd * DI, 1))
        inp['Ds'] = jnp.ones((Kd * DI,), jnp.float32)
        inp['ln_g'] = jnp.ones((DI,), jnp.float32)
        inp['ln_b'] = jnp.zeros((DI,), jnp.float32)
        inp['out_proj_w'] = rn((D, DI), 0.08)
        inp['cv2_w'] = rn((D, D), 0.1)
        inp['cv2_g'] = 1.0 + rn((D,), 0.05)
        inp['cv2_b'] = rn((D,), 0.05)
        inp['bn0_g'] = 1.0 + rn((D,), 0.05)
        inp['bn0_b'] = rn((D,), 0.05)
        inp['c1_w'] = rn((3, 3, D, D), 0.06)
        inp['c1_b'] = rn((D,), 0.05)
        inp['bn1_g'] = 1.0 + rn((D,), 0.05)
        inp['bn1_b'] = rn((D,), 0.05)
        inp['c2_w'] = rn((3, 3, D, D), 0.06)
        inp['c2_b'] = rn((D,), 0.05)
        inp['bn2_g'] = 1.0 + rn((D,), 0.05)
        inp['bn2_b'] = rn((D,), 0.05)
        inp['c3_w'] = rn((D, D), 0.1)
        inp['c3_b'] = rn((D,), 0.05)
        inp['cv_w'] = rn((D, D), 0.1)
        inp['cv_g'] = 1.0 + rn((D,), 0.05)
        inp['cv_b'] = rn((D,), 0.05)
        inp['cv3_w'] = rn((2 * D, 2 * D), 0.08)
        inp['cv3_g'] = 1.0 + rn((2 * D,), 0.05)
        inp['cv3_b'] = rn((2 * D,), 0.05)
        return inp
    _L0_conv_all = _L0_conv_setup()
    _L0_conv_in = {k: v for k, v in _L0_conv_all.items() if k in ('cv1_w', 'cv1_g', 'cv1_b', 'in_proj_w', 'dw_w', 'dw_b', 'x_proj_w', 'dt_w', 'dt_b', 'A_logs', 'Ds', 'ln_g', 'ln_b', 'out_proj_w', 'cv2_w', 'cv2_g', 'cv2_b', 'bn0_g', 'bn0_b', 'c1_w', 'c1_b', 'bn1_g', 'bn1_b', 'c2_w', 'c2_b', 'bn2_g', 'bn2_b', 'c3_w', 'c3_b', 'cv_w', 'cv_g', 'cv_b', 'cv3_w', 'cv3_g', 'cv3_b', )}
    del _L0_conv_all

    def _L1_conv_setup():
        import jax, jax.numpy as jnp
        import numpy as np
        C = 128
        EPS = 1e-05

        def _ln(x, g, b):
            m = jnp.mean(x, axis=-1, keepdims=True)
            v = jnp.mean((x - m) ** 2, axis=-1, keepdims=True)
            return (x - m) * jax.lax.rsqrt(v + EPS) * g + b
        key = jax.random.key(seed)
        ks = jax.random.split(key, 10)
        B, N = (1, 384)
        s = 1.0 / np.sqrt(C)
        inp = {'z': jax.random.normal(ks[0], (B, N, N, C), dtype=jnp.float32), 'ln1_g': jnp.ones((C,), jnp.float32), 'ln1_b': jnp.zeros((C,), jnp.float32), 'ln2_g': jnp.ones((C,), jnp.float32), 'ln2_b': jnp.zeros((C,), jnp.float32), 'Wa': jax.random.uniform(ks[1], (C, C), jnp.float32, -s, s), 'ba': jnp.zeros((C,), jnp.float32), 'Wga': jax.random.uniform(ks[2], (C, C), jnp.float32, -s, s), 'bga': jnp.zeros((C,), jnp.float32), 'Wb': jax.random.uniform(ks[3], (C, C), jnp.float32, -s, s), 'bb': jnp.zeros((C,), jnp.float32), 'Wgb': jax.random.uniform(ks[4], (C, C), jnp.float32, -s, s), 'bgb': jnp.zeros((C,), jnp.float32), 'Wg': jax.random.uniform(ks[5], (C, C), jnp.float32, -s, s), 'bg': jnp.zeros((C,), jnp.float32), 'Wo': jax.random.uniform(ks[6], (C, C), jnp.float32, -s, s), 'bo': jnp.zeros((C,), jnp.float32)}
        return inp
    _L1_conv_all = _L1_conv_setup()
    _L1_conv_in = {k: v for k, v in _L1_conv_all.items() if k in ('ln1_g', 'ln1_b', 'ln2_g', 'ln2_b', 'Wa', 'ba', 'Wga', 'bga', 'Wb', 'bb', 'Wgb', 'bgb', 'Wg', 'bg', 'Wo', 'bo', )}
    del _L1_conv_all

    def _L2_attn_setup():
        import jax, jax.numpy as jnp
        import numpy as np
        B, L, C, H = (8, 16384, 128, 4)
        EPS = 1e-05
        key = jax.random.key(seed)
        k1, k2, k3, k4 = jax.random.split(key, 4)
        return {'x': jax.random.normal(k1, (B, L, C), dtype=jnp.float32), 'W_qkv': jax.random.normal(k2, (3 * C, C), dtype=jnp.float32) * C ** (-0.5), 'W_out': jax.random.normal(k3, (C, C), dtype=jnp.float32) * C ** (-0.5), 'b_out': jax.random.normal(k4, (C,), dtype=jnp.float32) * 0.01, 'gn_w': jnp.ones((C,), dtype=jnp.float32), 'gn_b': jnp.zeros((C,), dtype=jnp.float32)}
    _L2_attn_all = _L2_attn_setup()
    _L2_attn_in = {k: v for k, v in _L2_attn_all.items() if k in ('W_qkv', 'W_out', 'b_out', 'gn_w', 'gn_b', )}
    del _L2_attn_all

    def _L2_ffn_setup():
        import jax, jax.numpy as jnp
        import numpy as np
        B, N, D, C, E, K = (8, 8192, 128, 128, 8, 2)
        key = jax.random.key(seed)
        k0, k1, k2 = jax.random.split(key, 3)
        x = jax.random.normal(k0, (B, N, D), dtype=jnp.float32)
        router_w = jax.random.normal(k1, (D, E), dtype=jnp.float32) * 0.05
        router_b = jnp.zeros((E,), dtype=jnp.float32)
        expert_w = jax.random.normal(k2, (E, D, C), dtype=jnp.float32) * (1.0 / np.sqrt(D))
        expert_b = jnp.zeros((E, C), dtype=jnp.float32)
        return {'x': x, 'router_w': router_w, 'router_b': router_b, 'expert_w': expert_w, 'expert_b': expert_b}
    _L2_ffn_all = _L2_ffn_setup()
    _L2_ffn_in = {k: v for k, v in _L2_ffn_all.items() if k in ('router_w', 'router_b', 'expert_w', 'expert_b', )}
    del _L2_ffn_all

    def _L3_attn_setup():
        import jax, jax.numpy as jnp
        import numpy as np
        HEADS = 8
        DIM = 128
        key = jax.random.key(seed)
        k1, k2, k3 = jax.random.split(key, 3)
        b, t, d, h = (4, 4096, DIM, HEADS)
        x = jax.random.normal(k1, (b, t, d), dtype=jnp.float32)
        W_kv = jax.random.normal(k2, (h * d * 2, d), dtype=jnp.float32) * (1.0 / np.sqrt(d))
        q_proj = jax.random.normal(k3, (h, d), dtype=jnp.float32) * (1.0 / np.sqrt(d))
        return {'x': x, 'W_kv': W_kv, 'q_proj': q_proj}
    _L3_attn_all = _L3_attn_setup()
    _L3_attn_in = {k: v for k, v in _L3_attn_all.items() if k in ('W_kv', 'q_proj', )}
    del _L3_attn_all

    def _L3_ffn_setup():
        import jax, jax.numpy as jnp
        import numpy as np
        B, S, D, E, H, O, K = (512, 2048, 128, 64, 512, 128, 8)
        key = jax.random.key(seed)
        k0, k1, k2, k3 = jax.random.split(key, 4)
        x = jax.random.normal(k0, (B, S, D), dtype=jnp.float32)
        gate_w = jax.random.normal(k1, (E, D), dtype=jnp.float32) * (1.0 / np.sqrt(D))
        gate_b = jnp.zeros((E,), dtype=jnp.float32)
        weight1 = jax.random.uniform(k2, (E, D + 1, H), dtype=jnp.float32, minval=-1.0, maxval=1.0) * (1.0 / np.sqrt(D + 1))
        weight2 = jax.random.uniform(k3, (E, H + 1, O), dtype=jnp.float32, minval=-1.0, maxval=1.0) * (1.0 / np.sqrt(H + 1))
        return {'x': x, 'gate_w': gate_w, 'gate_b': gate_b, 'weight1': weight1, 'weight2': weight2}
    _L3_ffn_all = _L3_ffn_setup()
    _L3_ffn_in = {k: v for k, v in _L3_ffn_all.items() if k in ('gate_w', 'gate_b', 'weight1', 'weight2', )}
    del _L3_ffn_all

    return {
        "x": x,
        "L0_conv_cv1_w": _L0_conv_in["cv1_w"],
        "L0_conv_cv1_g": _L0_conv_in["cv1_g"],
        "L0_conv_cv1_b": _L0_conv_in["cv1_b"],
        "L0_conv_in_proj_w": _L0_conv_in["in_proj_w"],
        "L0_conv_dw_w": _L0_conv_in["dw_w"],
        "L0_conv_dw_b": _L0_conv_in["dw_b"],
        "L0_conv_x_proj_w": _L0_conv_in["x_proj_w"],
        "L0_conv_dt_w": _L0_conv_in["dt_w"],
        "L0_conv_dt_b": _L0_conv_in["dt_b"],
        "L0_conv_A_logs": _L0_conv_in["A_logs"],
        "L0_conv_Ds": _L0_conv_in["Ds"],
        "L0_conv_ln_g": _L0_conv_in["ln_g"],
        "L0_conv_ln_b": _L0_conv_in["ln_b"],
        "L0_conv_out_proj_w": _L0_conv_in["out_proj_w"],
        "L0_conv_cv2_w": _L0_conv_in["cv2_w"],
        "L0_conv_cv2_g": _L0_conv_in["cv2_g"],
        "L0_conv_cv2_b": _L0_conv_in["cv2_b"],
        "L0_conv_bn0_g": _L0_conv_in["bn0_g"],
        "L0_conv_bn0_b": _L0_conv_in["bn0_b"],
        "L0_conv_c1_w": _L0_conv_in["c1_w"],
        "L0_conv_c1_b": _L0_conv_in["c1_b"],
        "L0_conv_bn1_g": _L0_conv_in["bn1_g"],
        "L0_conv_bn1_b": _L0_conv_in["bn1_b"],
        "L0_conv_c2_w": _L0_conv_in["c2_w"],
        "L0_conv_c2_b": _L0_conv_in["c2_b"],
        "L0_conv_bn2_g": _L0_conv_in["bn2_g"],
        "L0_conv_bn2_b": _L0_conv_in["bn2_b"],
        "L0_conv_c3_w": _L0_conv_in["c3_w"],
        "L0_conv_c3_b": _L0_conv_in["c3_b"],
        "L0_conv_cv_w": _L0_conv_in["cv_w"],
        "L0_conv_cv_g": _L0_conv_in["cv_g"],
        "L0_conv_cv_b": _L0_conv_in["cv_b"],
        "L0_conv_cv3_w": _L0_conv_in["cv3_w"],
        "L0_conv_cv3_g": _L0_conv_in["cv3_g"],
        "L0_conv_cv3_b": _L0_conv_in["cv3_b"],
        "L1_conv_ln1_g": _L1_conv_in["ln1_g"],
        "L1_conv_ln1_b": _L1_conv_in["ln1_b"],
        "L1_conv_ln2_g": _L1_conv_in["ln2_g"],
        "L1_conv_ln2_b": _L1_conv_in["ln2_b"],
        "L1_conv_Wa": _L1_conv_in["Wa"],
        "L1_conv_ba": _L1_conv_in["ba"],
        "L1_conv_Wga": _L1_conv_in["Wga"],
        "L1_conv_bga": _L1_conv_in["bga"],
        "L1_conv_Wb": _L1_conv_in["Wb"],
        "L1_conv_bb": _L1_conv_in["bb"],
        "L1_conv_Wgb": _L1_conv_in["Wgb"],
        "L1_conv_bgb": _L1_conv_in["bgb"],
        "L1_conv_Wg": _L1_conv_in["Wg"],
        "L1_conv_bg": _L1_conv_in["bg"],
        "L1_conv_Wo": _L1_conv_in["Wo"],
        "L1_conv_bo": _L1_conv_in["bo"],
        "L2_attn_W_qkv": _L2_attn_in["W_qkv"],
        "L2_attn_W_out": _L2_attn_in["W_out"],
        "L2_attn_b_out": _L2_attn_in["b_out"],
        "L2_attn_gn_w": _L2_attn_in["gn_w"],
        "L2_attn_gn_b": _L2_attn_in["gn_b"],
        "L2_ffn_router_w": _L2_ffn_in["router_w"],
        "L2_ffn_router_b": _L2_ffn_in["router_b"],
        "L2_ffn_expert_w": _L2_ffn_in["expert_w"],
        "L2_ffn_expert_b": _L2_ffn_in["expert_b"],
        "L3_attn_W_kv": _L3_attn_in["W_kv"],
        "L3_attn_q_proj": _L3_attn_in["q_proj"],
        "L3_ffn_gate_w": _L3_ffn_in["gate_w"],
        "L3_ffn_gate_b": _L3_ffn_in["gate_b"],
        "L3_ffn_weight1": _L3_ffn_in["weight1"],
        "L3_ffn_weight2": _L3_ffn_in["weight2"],
    }

def reference(x, L0_conv_cv1_w, L0_conv_cv1_g, L0_conv_cv1_b, L0_conv_in_proj_w, L0_conv_dw_w, L0_conv_dw_b, L0_conv_x_proj_w, L0_conv_dt_w, L0_conv_dt_b, L0_conv_A_logs, L0_conv_Ds, L0_conv_ln_g, L0_conv_ln_b, L0_conv_out_proj_w, L0_conv_cv2_w, L0_conv_cv2_g, L0_conv_cv2_b, L0_conv_bn0_g, L0_conv_bn0_b, L0_conv_c1_w, L0_conv_c1_b, L0_conv_bn1_g, L0_conv_bn1_b, L0_conv_c2_w, L0_conv_c2_b, L0_conv_bn2_g, L0_conv_bn2_b, L0_conv_c3_w, L0_conv_c3_b, L0_conv_cv_w, L0_conv_cv_g, L0_conv_cv_b, L0_conv_cv3_w, L0_conv_cv3_g, L0_conv_cv3_b, L1_conv_ln1_g, L1_conv_ln1_b, L1_conv_ln2_g, L1_conv_ln2_b, L1_conv_Wa, L1_conv_ba, L1_conv_Wga, L1_conv_bga, L1_conv_Wb, L1_conv_bb, L1_conv_Wgb, L1_conv_bgb, L1_conv_Wg, L1_conv_bg, L1_conv_Wo, L1_conv_bo, L2_attn_W_qkv, L2_attn_W_out, L2_attn_b_out, L2_attn_gn_w, L2_attn_gn_b, L2_ffn_router_w, L2_ffn_router_b, L2_ffn_expert_w, L2_ffn_expert_b, L3_attn_W_kv, L3_attn_q_proj, L3_ffn_gate_w, L3_ffn_gate_b, L3_ffn_weight1, L3_ffn_weight2):
    import jax
    import jax.numpy as jnp
    def _L0_conv_ref(x, cv1_w, cv1_g, cv1_b, in_proj_w, dw_w, dw_b, x_proj_w, dt_w, dt_b, A_logs, Ds, ln_g, ln_b, out_proj_w, cv2_w, cv2_g, cv2_b, bn0_g, bn0_b, c1_w, c1_b, bn1_g, bn1_b, c2_w, c2_b, bn2_g, bn2_b, c3_w, c3_b, cv_w, cv_g, cv_b, cv3_w, cv3_g, cv3_b):
        import jax, jax.numpy as jnp
        import numpy as np
        from jax import lax
        D_MODEL, D_INNER, D_STATE, DT_RANK, KDIR = (64, 128, 16, 4, 4)

        def _silu(x):
            return x * jax.nn.sigmoid(x)

        def _conv1x1(x, w):
            return jnp.einsum('bhwc,oc->bhwo', x, w)

        def _bn(x, g, b):
            return x * g + b

        def _conv3x3(x, w, b):
            y = lax.conv_general_dilated(x, w, (1, 1), 'SAME', dimension_numbers=('NHWC', 'HWIO', 'NHWC'))
            return y + b

        def _ss2d(x, in_proj_w, dw_w, dw_b, x_proj_w, dt_w, dt_b, A_logs, Ds, ln_g, ln_b, out_proj_w):
            B, H, W, _ = x.shape
            L = H * W
            xz = jnp.einsum('bhwd,ed->bhwe', x, in_proj_w)
            xh, z = jnp.split(xz, 2, axis=-1)
            xh = lax.conv_general_dilated(xh, dw_w, (1, 1), 'SAME', dimension_numbers=('NHWC', 'HWIO', 'NHWC'), feature_group_count=D_INNER) + dw_b
            xh = _silu(xh)
            x1 = xh.transpose(0, 3, 1, 2).reshape(B, D_INNER, L)
            x2 = xh.transpose(0, 3, 2, 1).reshape(B, D_INNER, L)
            xs = jnp.stack([x1, x2, x1[:, :, ::-1], x2[:, :, ::-1]], axis=1)
            x_dbl = jnp.einsum('bkdl,kcd->bkcl', xs, x_proj_w)
            dts = jnp.einsum('bkrl,kdr->bkdl', x_dbl[:, :, :DT_RANK], dt_w) + dt_b[None, :, :, None]
            Bs = x_dbl[:, :, DT_RANK:DT_RANK + D_STATE]
            Cs = x_dbl[:, :, DT_RANK + D_STATE:]
            delta = jax.nn.softplus(dts)
            A = -jnp.exp(A_logs).reshape(KDIR, D_INNER, D_STATE)
            Dk = Ds.reshape(KDIR, D_INNER)

            def step(h, inp):
                d, u, b, c = inp
                dA = jnp.exp(d[..., None] * A)
                h = dA * h + (d * u)[..., None] * b[:, :, None, :]
                y = jnp.sum(h * c[:, :, None, :], axis=-1)
                return (h, y)
            h0 = jnp.zeros((B, KDIR, D_INNER, D_STATE), xh.dtype)
            seq = (delta.transpose(3, 0, 1, 2), xs.transpose(3, 0, 1, 2), Bs.transpose(3, 0, 1, 2), Cs.transpose(3, 0, 1, 2))
            _, ys = lax.scan(step, h0, seq)
            y = ys.transpose(1, 2, 3, 0) + Dk[None, :, :, None] * xs
            wh = y[:, 1].reshape(B, D_INNER, W, H).transpose(0, 1, 3, 2).reshape(B, D_INNER, L)
            iwh = y[:, 3, :, ::-1].reshape(B, D_INNER, W, H).transpose(0, 1, 3, 2).reshape(B, D_INNER, L)
            yc = y[:, 0] + y[:, 2, :, ::-1] + wh + iwh
            yc = yc.transpose(0, 2, 1).reshape(B, H, W, D_INNER)
            mu = yc.mean(-1, keepdims=True)
            var = yc.var(-1, keepdims=True)
            yc = (yc - mu) / jnp.sqrt(var + 1e-05) * ln_g + ln_b
            yc = yc * _silu(z)
            return jnp.einsum('bhwe,de->bhwd', yc, out_proj_w)

        def _forward(x, cv1_w, cv1_g, cv1_b, in_proj_w, dw_w, dw_b, x_proj_w, dt_w, dt_b, A_logs, Ds, ln_g, ln_b, out_proj_w, cv2_w, cv2_g, cv2_b, bn0_g, bn0_b, c1_w, c1_b, bn1_g, bn1_b, c2_w, c2_b, bn2_g, bn2_b, c3_w, c3_b, cv_w, cv_g, cv_b, cv3_w, cv3_g, cv3_b):
            left, right = jnp.split(x, 2, axis=-1)
            right = _silu(_bn(_conv1x1(right, cv1_w), cv1_g, cv1_b))
            xr = _ss2d(right, in_proj_w, dw_w, dw_b, x_proj_w, dt_w, dt_b, A_logs, Ds, ln_g, ln_b, out_proj_w)
            l = _silu(_bn(_conv1x1(left, cv2_w), cv2_g, cv2_b))
            l = _bn(l, bn0_g, bn0_b)
            l = jax.nn.relu(_bn(_conv3x3(l, c1_w, c1_b), bn1_g, bn1_b))
            l = jax.nn.relu(_bn(_conv3x3(l, c2_w, c2_b), bn2_g, bn2_b))
            l = jax.nn.relu(_conv1x1(l, c3_w) + c3_b)
            xr = _silu(_bn(_conv1x1(xr, cv_w), cv_g, cv_b))
            out = jnp.concatenate([l, xr], axis=-1)
            out = _silu(_bn(_conv1x1(out, cv3_w), cv3_g, cv3_b))
            B, H, W, C = out.shape
            out = out.reshape(B, H, W, 2, C // 2).swapaxes(-1, -2).reshape(B, H, W, C)
            return out + x
        return _forward(x, cv1_w, cv1_g, cv1_b, in_proj_w, dw_w, dw_b, x_proj_w, dt_w, dt_b, A_logs, Ds, ln_g, ln_b, out_proj_w, cv2_w, cv2_g, cv2_b, bn0_g, bn0_b, c1_w, c1_b, bn1_g, bn1_b, c2_w, c2_b, bn2_g, bn2_b, c3_w, c3_b, cv_w, cv_g, cv_b, cv3_w, cv3_g, cv3_b)

    def _L1_conv_ref(z, ln1_g, ln1_b, ln2_g, ln2_b, Wa, ba, Wga, bga, Wb, bb, Wgb, bgb, Wg, bg, Wo, bo):
        import jax, jax.numpy as jnp
        import numpy as np
        C = 128
        EPS = 1e-05

        def _ln(x, g, b):
            m = jnp.mean(x, axis=-1, keepdims=True)
            v = jnp.mean((x - m) ** 2, axis=-1, keepdims=True)
            return (x - m) * jax.lax.rsqrt(v + EPS) * g + b
        zn = _ln(z, ln1_g, ln1_b)
        a = (zn @ Wa + ba) * jax.nn.sigmoid(zn @ Wga + bga)
        b = (zn @ Wb + bb) * jax.nn.sigmoid(zn @ Wgb + bgb)
        gate = jax.nn.sigmoid(zn @ Wg + bg)
        o = jnp.einsum('bikc,bjkc->bijc', a, b)
        return gate * (_ln(o, ln2_g, ln2_b) @ Wo + bo)

    def _L2_attn_ref(x, W_qkv, W_out, b_out, gn_w, gn_b):
        import jax, jax.numpy as jnp
        import numpy as np
        B, L, C, H = (8, 16384, 128, 4)
        EPS = 1e-05
        b, l, c = x.shape
        h = H
        d = c // h
        scale = d ** (-0.5)
        xc = jnp.swapaxes(x, 1, 2)
        qkv = jnp.einsum('oc,bcl->bol', W_qkv, xc)
        q, k, v = jnp.split(qkv, 3, axis=1)
        q = q.reshape(b, h, d, l)
        k = k.reshape(b, h, d, l)
        v = v.reshape(b, h, d, l)
        q = jax.nn.softmax(q, axis=2) * scale
        k = jax.nn.softmax(k, axis=3)
        context = jnp.einsum('bhcj,bhdj->bhcd', k, v)
        out = jnp.einsum('bhcd,bhdi->bhci', context, q)
        out = out.reshape(b, h * d, l)
        out = jnp.einsum('oc,bcl->bol', W_out, out) + b_out[None, :, None]
        mean = jnp.mean(out, axis=(1, 2), keepdims=True)
        var = jnp.var(out, axis=(1, 2), keepdims=True)
        out = (out - mean) * jax.lax.rsqrt(var + EPS)
        out = out * gn_w[None, :, None] + gn_b[None, :, None]
        return jnp.swapaxes(out, 1, 2)

    def _L2_ffn_ref(x, router_w, router_b, expert_w, expert_b):
        import jax, jax.numpy as jnp
        import numpy as np
        B, N, D, C, E, K = (8, 8192, 128, 128, 8, 2)
        router_probs = jax.nn.softmax(x @ router_w + router_b, axis=-1)
        top_p, top_i = jax.lax.top_k(router_probs, K)
        top_p = top_p / jnp.sum(top_p, axis=-1, keepdims=True)
        expert_out = jnp.einsum('bnd,edc->bnec', x, expert_w) + expert_b
        gathered = jnp.take_along_axis(expert_out, top_i[..., None], axis=2)
        return jnp.einsum('bnk,bnkc->bnc', top_p, gathered)

    def _L3_attn_ref(x, W_kv, q_proj):
        import jax, jax.numpy as jnp
        import numpy as np
        HEADS = 8
        DIM = 128
        b, t, d = x.shape
        h = q_proj.shape[0]
        kv = jnp.einsum('btd,ed->bte', x, W_kv).reshape(b, t, h, d, 2)
        kv = jax.nn.silu(kv)
        k, v = (kv[..., 0], kv[..., 1])
        s = jnp.einsum('hd,bthd->bth', q_proj, k)
        m_A = jax.lax.cummax(s, axis=1)
        exp_scores = jnp.exp(s - m_A)
        u_A = jnp.cumsum(exp_scores, axis=1)
        w_A = jnp.cumsum(exp_scores[..., None] * v, axis=1)
        output = w_A / u_A[..., None]
        return output.mean(axis=2)

    def _L3_ffn_ref(x, gate_w, gate_b, weight1, weight2):
        import jax, jax.numpy as jnp
        import numpy as np
        B, S, D, E, H, O, K = (512, 2048, 128, 64, 512, 128, 8)
        Bn, Sn, Dn = x.shape
        logits = jnp.einsum('bsd,ed->bse', x, gate_w) + gate_b
        probs = jax.nn.softmax(logits, axis=1)
        vals, idx = jax.lax.top_k(probs.transpose(0, 2, 1), K)
        topv = vals.transpose(0, 2, 1)
        topi = idx.transpose(0, 2, 1)
        flat_idx = topi.reshape(Bn, K * E)
        gathered = jnp.take_along_axis(x, flat_idx[:, :, None], axis=1)
        gathered = gathered.reshape(Bn, K, E, Dn)
        pooled = jnp.einsum('bked,bke->bed', gathered, topv)
        ones = jnp.ones((E, Bn, 1), dtype=x.dtype)
        h = jnp.concatenate([pooled.transpose(1, 0, 2), ones], axis=-1)
        h = jax.nn.gelu(jnp.einsum('ebd,edh->ebh', h, weight1), approximate=False)
        h = jnp.concatenate([h, ones], axis=-1)
        out = jnp.einsum('ebh,eho->ebo', h, weight2)
        out = out.transpose(1, 0, 2)
        weighted = jnp.einsum('beo,bke->bkeo', out, topv).reshape(Bn, K * E, O)
        outputs = jnp.zeros((Bn, Sn, O), dtype=x.dtype)
        outputs = outputs.at[jnp.arange(Bn)[:, None], flat_idx].add(weighted)
        return outputs

    def _gn(v, G=32, eps=1e-5):
        B_, H_, W_, C_ = v.shape
        g = v.reshape(B_, H_, W_, G, C_ // G)
        m = jnp.mean(g, axis=(1, 2, 4), keepdims=True)
        s = jnp.var(g, axis=(1, 2, 4), keepdims=True)
        return ((g - m) / jnp.sqrt(s + eps)).reshape(v.shape)

    def _ln_c(v, eps=1e-6):
        m = jnp.mean(v, axis=-1, keepdims=True)
        s = jnp.var(v, axis=-1, keepdims=True)
        return (v - m) / jnp.sqrt(s + eps)

    def _ln_t(v, eps=1e-5):
        m = jnp.mean(v, axis=-1, keepdims=True)
        s = jnp.var(v, axis=-1, keepdims=True)
        return (v - m) / jnp.sqrt(s + eps)

    def _to_tokens(v):
        B_, H_, W_, C_ = v.shape
        return v.reshape(B_, H_ * W_, C_)
    def _from_tokens(t, like):
        return t.reshape(like.shape)

    x = _L0_conv_ref(x, L0_conv_cv1_w, L0_conv_cv1_g, L0_conv_cv1_b, L0_conv_in_proj_w, L0_conv_dw_w, L0_conv_dw_b, L0_conv_x_proj_w, L0_conv_dt_w, L0_conv_dt_b, L0_conv_A_logs, L0_conv_Ds, L0_conv_ln_g, L0_conv_ln_b, L0_conv_out_proj_w, L0_conv_cv2_w, L0_conv_cv2_g, L0_conv_cv2_b, L0_conv_bn0_g, L0_conv_bn0_b, L0_conv_c1_w, L0_conv_c1_b, L0_conv_bn1_g, L0_conv_bn1_b, L0_conv_c2_w, L0_conv_c2_b, L0_conv_bn2_g, L0_conv_bn2_b, L0_conv_c3_w, L0_conv_c3_b, L0_conv_cv_w, L0_conv_cv_g, L0_conv_cv_b, L0_conv_cv3_w, L0_conv_cv3_g, L0_conv_cv3_b)
    x = x + _L1_conv_ref(_gn(x), L1_conv_ln1_g, L1_conv_ln1_b, L1_conv_ln2_g, L1_conv_ln2_b, L1_conv_Wa, L1_conv_ba, L1_conv_Wga, L1_conv_bga, L1_conv_Wb, L1_conv_bb, L1_conv_Wgb, L1_conv_bgb, L1_conv_Wg, L1_conv_bg, L1_conv_Wo, L1_conv_bo)
    t = _to_tokens(x)
    t = t + _L2_attn_ref(_ln_t(t), L2_attn_W_qkv, L2_attn_W_out, L2_attn_b_out, L2_attn_gn_w, L2_attn_gn_b)
    t = t + _L2_ffn_ref(_ln_t(t), L2_ffn_router_w, L2_ffn_router_b, L2_ffn_expert_w, L2_ffn_expert_b)
    t = t + _L3_attn_ref(_ln_t(t), L3_attn_W_kv, L3_attn_q_proj)
    t = t + _L3_ffn_ref(_ln_t(t), L3_ffn_gate_w, L3_ffn_gate_b, L3_ffn_weight1, L3_ffn_weight2)
    x = _from_tokens(t, x)
    return x


_drawn_inputs = setup_inputs


def setup_inputs(seed=0):
    import zlib

    import numpy as np

    out = dict(_drawn_inputs(seed))
    spreads = {'L0_conv_Ds': (1.0, 0.6),
     'L0_conv_ln_g': (1.0, 0.537),
     'L0_conv_ln_b': (0.0, 0.375),
     'L1_conv_ln1_g': (1.0, 0.2),
     'L1_conv_ln1_b': (0.0, 0.1),
     'L1_conv_ln2_g': (1.0, 0.2),
     'L1_conv_ln2_b': (0.0, 0.1),
     'L1_conv_ba': (0.0, 0.1),
     'L1_conv_bga': (0.0, 0.1),
     'L1_conv_bb': (0.0, 0.1),
     'L1_conv_bgb': (0.0, 0.1),
     'L1_conv_bg': (0.0, 0.1),
     'L1_conv_bo': (0.0, 0.1),
     'L2_attn_gn_w': (1.0, 0.2),
     'L2_attn_gn_b': (0.0, 0.1),
     'L2_ffn_router_b': (0.0, 0.1),
     'L2_ffn_expert_b': (0.0, 0.1),
     'L3_ffn_gate_b': (0.0, 0.1)}
    factors = {'L0_conv_cv1_g': 3.348,
     'L0_conv_cv1_b': 3.124,
     'L0_conv_x_proj_w': 8.0,
     'L0_conv_dt_w': 8.0,
     'L0_conv_dt_b': 8.0,
     'L0_conv_A_logs': 8.0,
     'L0_conv_cv_g': 4.127,
     'L3_attn_q_proj': 8.0,
     'L3_ffn_gate_w': 8.0,
     'L3_ffn_weight1': 8.0,
     'L3_ffn_weight2': 8.0}
    for name, (base, spread) in spreads.items():
        noise = np.random.default_rng([zlib.crc32(name.encode()), seed]).standard_normal(out[name].shape)
        drawn = base * np.exp(spread * noise) if base else spread * noise
        out[name] = jnp.asarray(drawn.astype(out[name].dtype))
    for name, factor in factors.items():
        out[name] = (out[name] * factor).astype(out[name].dtype)
    return out
```

```python
from contextlib import ExitStack

import concourse.bass as bass
from concourse import mybir

ALU = mybir.AluOpType
ACT = mybir.ActivationFunctionType
AX_X = mybir.AxisListType.X
F32 = mybir.dt.float32
BF16 = mybir.dt.bfloat16

P = 128
NB, IMG = 4, 64
TOK = IMG * IMG
NTOK = NB * TOK
CH = 512
NCH = TOK // CH
ROWS = CH // IMG
PAD = IMG + 2
HALF = P // 2
NDIR, NST = 4, 16
NEXP2, TOP2 = 8, 2
HD = 8
NEXP3, HID = 64, 512
BIG = 3.0e38

PACK0 = [
    ("ident", P), ("ones", P), ("center", P), ("eps", 1),
    ("cv12", P), ("c1", 9 * P), ("c2", 9 * P), ("c3", P), ("in_xh", P), ("in_z", P),
    ("xp_dt", NDIR * P), ("dt_w", NDIR * P), ("bc", NDIR * 96), ("out_proj", P), ("cv", P), ("cv3", P),
    ("dw", 9), ("A_logs", NDIR * NST), ("Ds", NDIR), ("dt_b", NDIR), ("log3", 3),
    ("cv12_g", 1), ("cv12_b", 1), ("bn0_g", 1), ("bn0_b", 1), ("bn1_g", 1), ("bn1_b", 1), ("c1_b", 1),
    ("bn2_g", 1), ("bn2_b", 1), ("c2_b", 1), ("c3_b", 1), ("dw_b", 1), ("ln_g", 1), ("ln_b", 1),
    ("cv_g", 1), ("cv_b", 1), ("cv3_g", 1), ("cv3_b", 1),
]
PACK1 = [
    ("ident", P), ("ones", P), ("center", P), ("eps", 1), ("group4", P),
    ("ab", 4 * P), ("ab_b", 4 * P), ("g", P), ("o", P),
    ("ln1_g", 1), ("ln1_b", 1), ("ln2_g", 1), ("ln2_b", 1), ("bg", 1), ("bo", 1),
]
PACK2 = [
    ("ident", P), ("ones", P), ("center", P), ("eps", 1), ("heads", P),
    ("k", P), ("qv", 2 * P), ("out", P), ("b_out", 1), ("gn_w", 1), ("gn_b", 1),
    ("router", NEXP2), ("router_b", 4 * NEXP2), ("experts", NEXP2 * P), ("expert_b", P),
]
PACK3 = [
    ("ident", P), ("ones", P), ("center", P), ("eps", 1), ("upto", P), ("last", P),
    ("k", HD * P), ("v", HD * P), ("q", HD * (2 * P - 1)),
]
PACK3F = [
    ("ident", P), ("ones", P), ("center", P), ("eps", 1),
    ("gate", 2 * P), ("gate_b", 1), ("b1", NEXP3 * 4), ("b2", NEXP3),
]


def places(pack):
    at, out = 0, {}
    for name, width in pack:
        out[name] = (at, width)
        at += width
    return out, at


def semaphores(nc, ctx, prefix):
    held = []

    def sem(name):
        held.append(nc.alloc_semaphore(name=prefix + name))
        return held[-1]

    def close():
        nc.clear_and_free_semaphores(held)
        nc.all_engine_barrier()

    ctx.callback(close)
    return sem


def layer0(nc, xT, pack, sel, x1):
    with ExitStack() as ctx:
        def sb(name, shape, dt=F32):
            return ctx.enter_context(nc.sbuf_tensor("l0_" + name, shape, dt))

        sem = semaphores(nc, ctx, "l0_")

        where, width = places(PACK0)
        W = sb("W", [P, width])

        def w(name, a=0, n=None):
            at, size = where[name]
            return W[:, at + a:at + (size if n is None else a + n)]

        SEL = sb("SEL", [96, 2 * NST * P], BF16)
        DWD = sb("DWD", [P, 9 * P])
        WDT = sb("WDT", [P, NDIR * P])
        WCV = sb("WCV", [P, P])
        A = sb("A", [P, NDIR * NST])
        NIL, PNIL = sb("NIL", [P, 1]), sb("PNIL", [P, 1])
        VEC = sb("VEC", [P, 4])
        LX = sb("LX", [P, TOK])
        Z = sb("Z", [P, TOK])
        YA = sb("YA", [P, PAD * PAD])
        YB = sb("YB", [P, PAD * PAD])
        XH = sb("XH", [P, TOK + CH])
        XC = sb("XC", [P, TOK + CH])
        H = sb("H", [P, NST * CH])
        HL = sb("HL", [P, NDIR * NST])
        BS = sb("BS", [P, 2, CH])
        DBU = sb("DBU", [P, 2, CH])
        HC = sb("HC", [P, 2, CH])
        DL = sb("DL", [P, 2, CH])
        DU = sb("DU", [P, 2, CH])
        S = sb("S", [96, 2, CH], BF16)
        TE, TL, TP, TR = (sb(n, [P, CH]) for n in ("TE", "TL", "TP", "TR"))
        RS = sb("RS", [HALF, CH])
        PS = ctx.enter_context(nc.psum_tensor("l0_PS", [P, 8, CH], F32))
        B_BANK, C_BANK, DA_BANK, Y_BANK, PREP_BANK = 0, 2, 4, 6, 7

        X = H[:, 0:TOK]
        C2 = XH
        AB = XC
        P1 = YA[:, :].rearrange("p (h w) -> p h w", h=PAD)
        P2 = YB[:, :].rearrange("p (h w) -> p h w", h=PAD)
        PH = H[:, 0:PAD * PAD].rearrange("p (h w) -> p h w", h=PAD)
        XCv = XC[:, 0:TOK].rearrange("p (w h) -> p h w", h=IMG)
        YBv = YB[:, 0:TOK].rearrange("p (w h) -> p h w", h=IMG)

        loaded = sem("loaded")
        x_in = sem("x_in")
        x_out = sem("x_out")
        setup_pe, setup_act, setup_dve = sem("setup_pe"), sem("setup_act"), sem("setup_dve")
        padded = sem("padded")
        bn0_done = sem("bn0_done")
        cols_done = sem("cols_done")
        mm = sem("mm")
        ev = sem("ev")
        b_up, b_sb = sem("b_up"), sem("b_sb")
        dbu_up = sem("dbu_up")
        da_up = sem("da_up")
        scanned = sem("scanned")
        c_up = sem("c_up")
        hc_up = sem("hc_up")
        y_up = sem("y_up")
        pd_up, pb_up = sem("pd_up"), sem("pb_up")
        e_up, ln_up = sem("e_up"), sem("ln_up")
        ab_up = sem("ab_up")
        relu_up = sem("relu_up")
        poly = sem("poly")
        dl_w = sem("dl_w")
        dl_up, du_up = sem("dl_up"), sem("du_up")
        s_hi, s_mid, s_lo, r_up = sem("s_hi"), sem("s_mid"), sem("s_lo"), sem("r_up")
        y_out = sem("y_out")
        y_init = sem("y_init")
        hl_up = sem("hl_up")
        ln_pe, ln_act, ln_dve = sem("ln_pe"), sem("ln_act"), sem("ln_dve")
        ln_w = sem("ln_w")
        res = sem("res")

        NGA = 9 * NCH
        PREPS = NCH * NDIR + 1

        block = ctx.enter_context(nc.Block())

        @block.sync
        def _(sp):
            sp.dma_start(W[:, :], pack).then_inc(loaded, 16)
            sp.dma_start(SEL[:, :], sel).then_inc(loaded, 16)
            sp.sem_inc(x_out, 16)
            with sp.Fori(0, NB) as b:
                sp.dma_start(X, xT[:, bass.ds(b * TOK, TOK)]).then_inc(x_in, 16)
                sp.wait_ge(ln_dve, (b + 1) * 16)
                sp.dma_start(X, xT[:, bass.ds(b * TOK, TOK)]).then_inc(x_in, 16)
                sp.wait_ge(res, (b + 1) * NCH)
                sp.dma_start(x1[:, bass.ds(b * TOK, TOK)], Z[:, :]).then_inc(x_out, 16)
            sp.wait_ge(x_out, (NB + 1) * 16)

        def conv(pe, src, taps, bank, row):
            for t in range(9):
                ins = nc.tensor.matmul(PS[:, bank, :], taps[:, t * P:(t + 1) * P],
                                       src[:, bass.ds(row + t // 3, ROWS), t % 3:t % 3 + IMG],
                                       start=(t == 0), stop=(t == 8))
            return ins

        @block.tensor
        def _(pe):
            pe.wait_ge(loaded, 32)
            for k in range(NDIR):
                nc.tensor.matmul(PS[:, 0, k * P:(k + 1) * P], w("xp_dt", k * P, P)[0:4, :],
                                 w("dt_w", k * P, P)[0:4, :], start=True, stop=True)
            nc.tensor.matmul(PS[:, 1, 0:P], w("out_proj")[0:HALF, :], w("cv")[0:HALF, :],
                             start=True, stop=True).then_inc(setup_pe, 1)
            pe.wait_ge(setup_act, 3)
            pe.wait_ge(setup_dve, 9)

            with pe.Fori(0, NB) as b:
                def ring(stage, j, u):
                    pe.wait_ge(ev, b * NGA + stage * NCH + j * 2 + u + 1)

                def stage_done(stage):
                    pe.wait_ge(ev, b * NGA + stage * NCH + 2)

                with pe.Fori(0, NCH // 2) as j:
                    for u in range(2):
                        pe.wait_ge(x_in, b * 32 + 16)
                        ring(0, j, u)
                        nc.tensor.matmul(PS[:, u, :], w("cv12"), X[:, bass.ds((j * 2 + u) * CH, CH)],
                                         start=True, stop=True).then_inc(mm, 1)
                with pe.Fori(0, NCH // 2) as j:
                    for u in range(2):
                        pe.wait_ge(bn0_done, (b + 1) * NCH)
                        ring(1, j, u)
                        conv(pe, P1, w("c1"), u, (j * 2 + u) * ROWS).then_inc(mm, 1)
                with pe.Fori(0, NCH // 2) as j:
                    for u in range(2):
                        stage_done(2)
                        ring(2, j, u)
                        conv(pe, P2, w("c2"), u, (j * 2 + u) * ROWS).then_inc(mm, 1)
                with pe.Fori(0, NCH // 2) as j:
                    for u in range(2):
                        stage_done(3)
                        ring(3, j, u)
                        nc.tensor.matmul(PS[:, u, :], w("c3"), C2[:, bass.ds((j * 2 + u) * CH, CH)],
                                         start=True, stop=True).then_inc(mm, 1)
                for stage, name in ((4, "in_xh"), (5, "in_z")):
                    with pe.Fori(0, NCH // 2) as j:
                        for u in range(2):
                            ring(stage, j, u)
                            nc.tensor.matmul(PS[:, u, :], w(name), AB[:, bass.ds((j * 2 + u) * CH, CH)],
                                             start=True, stop=True).then_inc(mm, 1)
                with pe.Fori(0, NCH // 2) as j:
                    for u in range(2):
                        ring(6, j, u)
                        conv(pe, PH, DWD, u, (j * 2 + u) * ROWS).then_inc(mm, 1)
                stage_done(7)
                pe.wait_ge(cols_done, (b + 1) * NCH)

                def delta_arg(k, at, n):
                    nc.tensor.matmul(PS[:, PREP_BANK, :], WDT[:, k * P:(k + 1) * P],
                                     (XH if k % 2 == 0 else XC)[:, bass.ds(at, CH)],
                                     start=True, stop=True).then_inc(pd_up, 1)

                def b_and_c(k, at, n):
                    pe.wait_ge(ab_up, n)
                    pe.wait_ge(relu_up, n)
                    nc.tensor.matmul(PS[0:96, PREP_BANK, :], w("bc", k * 96, 96),
                                     (XH if k % 2 == 0 else XC)[:, bass.ds(at, CH)],
                                     start=True, stop=True).then_inc(pb_up, 1)

                def add_y(u0, n):
                    if n == 0:
                        pe.wait_ge(y_out, u0[1])
                    pe.wait_ge(hc_up, u0[0] + n + 1 + 2)
                    nc.tensor.matmul(PS[:, Y_BANK, :], w("ident"), HC[:, n % 2, :],
                                     start=(n == 0), stop=(n == NST - 1)).then_inc(y_up, 1)

                delta_arg(0, 0, b * PREPS + 1)
                b_and_c(0, 0, b * PREPS + 1)
                with pe.Fori(0, NCH) as c:
                    for k in range(NDIR):
                        it = (b * NCH + c) * NDIR + k
                        u0 = (it * NST, it + 1)
                        prep = b * PREPS + c * NDIR + k + 2
                        kn, cn = (k + 1) % NDIR, (c if k < NDIR - 1 else c + 1)
                        nxt = (cn if kn < 2 else (NCH - 1) - cn) * CH
                        pe.wait_ge(s_lo, prep - 1)
                        for n in range(NST):
                            pe.wait_ge(b_sb, u0[0] + n + 1)
                            nc.tensor.matmul(PS[:, B_BANK + n % 2, :], SEL[:, n * P:(n + 1) * P],
                                             S[:, k % 2, :], start=True, stop=True).then_inc(b_up, 1)
                            if n == 3:
                                pe.wait_ge(r_up, prep - 1)
                            pe.wait_ge(hc_up, u0[0] + n + 1)
                            nc.tensor.matmul(PS[:, C_BANK + n % 2, :], SEL[:, (NST + n) * P:(NST + n + 1) * P],
                                             S[:, k % 2, :], start=True, stop=True).then_inc(c_up, 1)
                            if n >= 2:
                                add_y(u0, n - 2)
                            if n == 3:
                                delta_arg(kn, nxt, prep)
                            if n == 7:
                                b_and_c(kn, nxt, prep)
                        add_y(u0, NST - 2)
                        add_y(u0, NST - 1)

                for g in range(2):
                    for i in range(4):
                        pe.wait_ge(ln_dve, b * 16 + g * 8 + i + 1)
                        nc.tensor.matmul(PS[:, i, :], w("center"), YA[:, (4 * g + i) * CH:(4 * g + i + 1) * CH],
                                         start=True, stop=True).then_inc(ln_pe, 1)
                    for i in range(4):
                        pe.wait_ge(ln_act, b * 24 + g * 12 + i + 1)
                        pe.wait_ge(r_up, (b + 1) * PREPS)
                        nc.tensor.matmul(PS[:, 4 + i, :], w("ones"), H[:, i * CH:(i + 1) * CH],
                                         start=True, stop=True).then_inc(ln_pe, 1)
                with pe.Fori(0, NCH // 2) as j:
                    for u in range(2):
                        pe.wait_ge(ln_dve, (b + 1) * 16)
                        ring(7, j, u)
                        nc.tensor.matmul(PS[:, u, :], WCV[:, :], YA[:, bass.ds((j * 2 + u) * CH, CH)],
                                         start=True, stop=True).then_inc(mm, 1)
                with pe.Fori(0, NCH // 2) as j:
                    for u in range(2):
                        stage_done(8)
                        ring(8, j, u)
                        nc.tensor.matmul(PS[:, u, :], w("cv3"), LX[:, bass.ds((j * 2 + u) * CH, CH)],
                                         start=True, stop=True).then_inc(mm, 1)
                stage_done(9)

        @block.scalar
        def _(act):
            act.wait_ge(loaded, 32)
            act.sem_inc(ev, 2)
            act.sem_inc(b_sb, 2)
            act.wait_ge(setup_pe, 1)
            nc.scalar.copy(WDT[:, :], PS[:, 0, :]).then_inc(setup_act, 1)
            nc.scalar.copy(WCV[:, :], PS[:, 1, 0:P]).then_inc(setup_act, 1)
            nc.scalar.activation(A[:, :], w("A_logs"), ACT.Exp).then_inc(setup_act, 1)
            act.wait_ge(setup_dve, 12)
            with act.Fori(0, NB) as b:
                def take(stage, body):
                    with act.Fori(0, NCH // 2) as j:
                        for u in range(2):
                            act.wait_ge(mm, b * NGA + stage * NCH + j * 2 + u + 1)
                            body(j * 2 + u, PS[:, u, :]).then_inc(ev, 1)

                def rows(ap):
                    return ap.rearrange("p (h w) -> p h w", w=IMG)

                def inner(buf, j):
                    return buf[:, bass.ds(j * ROWS + 1, ROWS), 1:1 + IMG]

                take(0, lambda j, ps: nc.scalar.activation(
                    AB[:, bass.ds(j * CH, CH)], ps, ACT.Silu, scale=w("cv12_g"), bias=w("cv12_b")))
                act.wait_ge(padded, (b + 1) * 3)
                take(1, lambda j, ps: nc.scalar.activation(
                    inner(P2, j), rows(ps), ACT.Relu, scale=w("bn1_g"), bias=VEC[:, 0:1]))
                take(2, lambda j, ps: nc.scalar.activation(
                    C2[:, bass.ds(j * CH, CH)], ps, ACT.Relu, scale=w("bn2_g"), bias=VEC[:, 1:2]))
                take(3, lambda j, ps: nc.scalar.activation(
                    LX[0:HALF, bass.ds(j * CH, CH)], ps[0:HALF, :], ACT.Relu, bias=w("c3_b")[0:HALF, :]))
                take(4, lambda j, ps: nc.scalar.copy(inner(PH, j), rows(ps)))
                act.wait_ge(x_out, (b + 1) * 16)
                take(5, lambda j, ps: nc.scalar.activation(Z[:, bass.ds(j * CH, CH)], ps, ACT.Silu))
                take(6, lambda j, ps: nc.scalar.activation(
                    XH[:, bass.ds(j * CH, CH)], ps, ACT.Silu, bias=w("dw_b")))

                def softplus(k, n):
                    act.wait_ge(pd_up, n)
                    act.wait_ge(dl_up, n)
                    nc.scalar.activation(TE[:, :], PS[:, PREP_BANK, :], ACT.Abs,
                                         bias=w("dt_b", k, 1)).then_inc(ab_up, 1)
                    act.wait_ge(ab_up, n)
                    nc.scalar.activation(TE[:, :], TE[:, :], ACT.Exp, scale=-1.0).then_inc(e_up, 1)
                    act.wait_ge(e_up, n)
                    nc.scalar.activation(TL[:, :], TE[:, :], ACT.Ln, bias=1.0).then_inc(ln_up, 1)

                def high(k, n):
                    act.wait_ge(pb_up, n)
                    nc.scalar.copy(S[:, k % 2, :], PS[0:96, PREP_BANK, :]).then_inc(s_hi, 1)

                def middle(k, n):
                    act.wait_ge(r_up, n)
                    nc.scalar.copy(S[0:HALF, k % 2, :], RS[:, :]).then_inc(s_mid, 1)

                softplus(0, b * PREPS + 1)
                high(0, b * PREPS + 1)
                middle(0, b * PREPS + 1)
                with act.Fori(0, NCH) as c:
                    for k in range(NDIR):
                        u0 = ((b * NCH + c) * NDIR + k) * NST
                        prep = b * PREPS + c * NDIR + k + 2
                        act.wait_ge(dl_up, prep)
                        for n in range(NST):
                            act.wait_ge(b_up, u0 + n + 1)
                            act.wait_ge(dbu_up, u0 + n + 1)
                            nc.scalar.copy(BS[:, n % 2, :], PS[:, B_BANK + n % 2, :]).then_inc(b_sb, 1)
                            act.wait_ge(scanned, u0 + n + 1)
                            nc.scalar.activation(PS[:, DA_BANK + n % 2, :], DL[:, k % 2, :], ACT.Exp,
                                                 scale=A[:, k * NST + n:k * NST + n + 1]).then_inc(da_up, 1)
                            if n == 4:
                                softplus((k + 1) % NDIR, prep)
                            if n == 9:
                                high((k + 1) % NDIR, prep)
                            if n == 12:
                                middle((k + 1) % NDIR, prep)

                for g in range(2):
                    for i in range(4):
                        act.wait_ge(ln_pe, b * 16 + g * 8 + i + 1)
                        nc.scalar.activation(H[:, i * CH:(i + 1) * CH], PS[:, i, :],
                                             ACT.Square).then_inc(ln_act, 1)
                    for i in range(4):
                        act.wait_ge(ln_pe, b * 16 + g * 8 + 4 + i + 1)
                        nc.scalar.activation(H[:, (4 + i) * CH:(5 + i) * CH], PS[:, 4 + i, :], ACT.Ln,
                                             bias=w("eps")).then_inc(ln_act, 1)
                    for i in range(4):
                        act.wait_ge(ln_act, b * 24 + g * 12 + 4 + i + 1)
                        nc.scalar.activation(H[:, (4 + i) * CH:(5 + i) * CH], H[:, (4 + i) * CH:(5 + i) * CH],
                                             ACT.Exp, scale=-0.5).then_inc(ln_act, 1)
                take(7, lambda j, ps: nc.scalar.activation(
                    LX[HALF:P, bass.ds(j * CH, CH)], ps[HALF:P, :], ACT.Silu,
                    scale=w("cv_g")[HALF:P, :], bias=w("cv_b")[HALF:P, :]))
                take(8, lambda j, ps: nc.scalar.activation(
                    Z[:, bass.ds(j * CH, CH)], ps, ACT.Silu, scale=w("cv3_g"), bias=w("cv3_b")))

        @block.gpsimd
        def _(pool):
            pool.sem_inc(dbu_up, 2)
            pool.wait_ge(loaded, 32)
            with pool.Fori(0, NB) as b:
                def short_log(n):
                    q = (n - 1) * 7
                    const = lambda i: w("log3", i, 1).to_broadcast([P, CH])
                    pool.wait_ge(e_up, n)
                    pool.wait_ge(dl_up, n)
                    nc.gpsimd.tensor_tensor(TP[:, :], TE[:, :], const(0), ALU.mult).then_inc(poly, 1)
                    pool.wait_ge(poly, q + 1)
                    nc.gpsimd.tensor_tensor(TP[:, :], TP[:, :], const(1), ALU.subtract).then_inc(poly, 1)
                    pool.wait_ge(poly, q + 2)
                    nc.gpsimd.tensor_tensor(TP[:, :], TP[:, :], TE[:, :], ALU.mult).then_inc(poly, 1)
                    pool.wait_ge(poly, q + 3)
                    nc.gpsimd.tensor_tensor(TP[:, :], TP[:, :], const(2), ALU.add).then_inc(poly, 1)
                    pool.wait_ge(poly, q + 4)
                    nc.gpsimd.tensor_tensor(TP[:, :], TP[:, :], TE[:, :], ALU.mult).then_inc(poly, 1)
                    pool.wait_ge(poly, q + 5)
                    pool.wait_ge(ln_up, n)
                    nc.gpsimd.tensor_tensor(TP[:, :], TP[:, :], TL[:, :], ALU.subtract).then_inc(poly, 1)
                    pool.wait_ge(relu_up, n)
                    pool.wait_ge(poly, q + 6)
                    nc.gpsimd.tensor_tensor(TL[:, :], TL[:, :], TR[:, :], ALU.add).then_inc(poly, 1)

                def delta_u(k, at, n):
                    pool.wait_ge(dl_up, n + 1)
                    nc.gpsimd.tensor_tensor(PNIL[:, :], w("eps"), w("eps"), ALU.mult)
                    nc.gpsimd.tensor_tensor(DU[:, k % 2, :], DL[:, k % 2, :],
                                            (XH if k % 2 == 0 else XC)[:, bass.ds(at, CH)],
                                            ALU.mult).then_inc(du_up, 1)

                short_log(b * PREPS + 1)
                delta_u(0, 0, b * PREPS + 1)
                with pool.Fori(0, NCH) as c:
                    for k in range(NDIR):
                        u0 = ((b * NCH + c) * NDIR + k) * NST
                        prep = b * PREPS + c * NDIR + k + 2
                        kn, cn = (k + 1) % NDIR, (c if k < NDIR - 1 else c + 1)
                        nxt = (cn if kn < 2 else (NCH - 1) - cn) * CH
                        pool.wait_ge(du_up, prep - 1)
                        for n in range(NST):
                            pool.wait_ge(b_sb, u0 + n + 1 + 2)
                            pool.wait_ge(scanned, u0 + n + 1)
                            nc.gpsimd.tensor_tensor(DBU[:, n % 2, :], BS[:, n % 2, :], DU[:, k % 2, :],
                                                    ALU.mult).then_inc(dbu_up, 1)
                            if n == 7:
                                short_log(prep)
                        delta_u(kn, nxt, prep)

        @block.vector
        def _(dve):
            dve.wait_ge(loaded, 32)
            dve.sem_inc(scanned, 2)
            dve.sem_inc(hc_up, 2)
            dve.sem_inc(dl_up, 1)
            dve.sem_inc(y_out, 1)
            for t in range(9):
                nc.vector.tensor_scalar(DWD[:, t * P:(t + 1) * P], w("ident"), w("dw", t, 1), None,
                                        ALU.mult).then_inc(setup_dve, 1)
            nc.vector.scalar_tensor_tensor(VEC[:, 0:1], w("c1_b"), w("bn1_g"), w("bn1_b"), ALU.mult,
                                           ALU.add).then_inc(setup_dve, 1)
            nc.vector.scalar_tensor_tensor(VEC[:, 1:2], w("c2_b"), w("bn2_g"), w("bn2_b"), ALU.mult,
                                           ALU.add).then_inc(setup_dve, 1)
            dve.wait_ge(setup_act, 3)
            nc.vector.tensor_scalar(A[:, :], A[:, :], -1.0, None, ALU.mult).then_inc(setup_dve, 1)
            nc.vector.tensor_reduce(VEC[:, 2:3], w("Ds"), AX_X, ALU.add).then_inc(setup_dve, 1)
            nc.vector.memset(XH[:, TOK:TOK + CH], 0.0).then_inc(setup_dve, 1)
            dve.wait_ge(setup_dve, 14)

            with dve.Fori(0, NB) as b:
                nc.vector.memset(YA[:, :], 0.0).then_inc(padded, 1)
                nc.vector.memset(YB[:, :], 0.0).then_inc(padded, 1)
                nc.vector.memset(HL[:, :], 0.0).then_inc(hl_up, 1)
                with dve.Fori(0, NCH) as j:
                    dve.wait_ge(padded, b * 3 + 2)
                    dve.wait_ge(ev, b * NGA + j + 1 + 2)
                    nc.vector.tensor_scalar(P1[:, bass.ds(j * ROWS + 1, ROWS), 1:1 + IMG],
                                            AB[:, bass.ds(j * CH, CH)].rearrange("p (h w) -> p h w", w=IMG),
                                            w("bn0_g"), w("bn0_b"), ALU.mult, ALU.add).then_inc(bn0_done, 1)
                nc.vector.memset(H[:, :], 0.0).then_inc(padded, 1)
                with dve.Fori(0, NCH) as j:
                    dve.wait_ge(mm, b * NGA + 6 * NCH)
                    dve.wait_ge(ev, b * NGA + 6 * NCH + j + 1 + 2)
                    nc.vector.tensor_copy(XCv[:, bass.ds(j * ROWS, ROWS), :],
                                          XH[:, bass.ds(j * CH, CH)].rearrange("p (h w) -> p h w", w=IMG)
                                          ).then_inc(cols_done, 1)
                nc.vector.tensor_scalar(YA[:, 0:TOK], XH[:, 0:TOK], VEC[:, 2:3], None,
                                        ALU.mult).then_inc(y_init, 1)
                nc.vector.memset(YB[:, 0:TOK], 0.0).then_inc(y_init, 1)
                dve.wait_ge(y_init, (b + 1) * 2)
                dve.wait_ge(hl_up, b * (NCH * NDIR + 1) + 1)

                def relu(k, n):
                    dve.wait_ge(ab_up, n)
                    nc.vector.tensor_scalar(TR[:, :], PS[:, PREP_BANK, :], w("dt_b", k, 1), 0.0, ALU.add,
                                            ALU.max).then_inc(relu_up, 1)

                def rest(k, n):
                    dve.wait_ge(pb_up, n)
                    dve.wait_ge(s_hi, n)
                    nc.vector.tensor_tensor(RS[:, :], PS[0:HALF, PREP_BANK, :], S[0:HALF, k % 2, :],
                                            ALU.subtract).then_inc(r_up, 1)

                def low(k, n):
                    dve.wait_ge(s_mid, n)
                    dve.wait_ge(r_up, n)
                    nc.vector.tensor_tensor(S[0:32, k % 2, :], RS[0:32, :], S[0:32, k % 2, :],
                                            ALU.subtract).then_inc(s_lo, 1)

                def delta(k, n):
                    dve.wait_ge(poly, n * 7)
                    nc.vector.scalar_tensor_tensor(TP[:, :], TE[:, :], 0.02, TP[:, :], ALU.is_lt,
                                                   ALU.mult).then_inc(dl_w, 1)
                    dve.wait_ge(dl_w, n)
                    nc.vector.tensor_tensor(DL[:, k % 2, :], TP[:, :], TL[:, :], ALU.add).then_inc(dl_up, 1)

                relu(0, b * PREPS + 1)
                rest(0, b * PREPS + 1)
                low(0, b * PREPS + 1)
                delta(0, b * PREPS + 1)
                with dve.Fori(0, NCH) as c:
                    for k in range(NDIR):
                        it = (b * NCH + c) * NDIR + k
                        u0 = it * NST
                        prep = b * PREPS + c * NDIR + k + 2
                        kn = (k + 1) % NDIR
                        turn = -1 if k >= 2 else 1
                        end = 0 if k >= 2 else CH - 1
                        y_sum = YA if k % 2 == 0 else YB
                        def times_c(n):
                            dve.wait_ge(scanned, u0 + n + 1 + 2)
                            dve.wait_ge(c_up, u0 + n + 1)
                            nc.vector.tensor_tensor(HC[:, n % 2, :], H[:, n * CH:(n + 1) * CH],
                                                    PS[:, C_BANK + n % 2, :], ALU.mult).then_inc(hc_up, 1)

                        for n in range(NST):
                            dve.wait_ge(da_up, u0 + n + 1)
                            dve.wait_ge(dbu_up, u0 + n + 1 + 2)
                            nc.vector.tensor_tensor_scan(
                                H[:, n * CH:(n + 1) * CH][:, ::turn], PS[:, DA_BANK + n % 2, :][:, ::turn],
                                DBU[:, n % 2, :][:, ::turn], HL[:, k * NST + n:k * NST + n + 1],
                                ALU.mult, ALU.add).then_inc(scanned, 1)
                            if n >= 1:
                                if n - 1 >= 2:
                                    dve.wait_ge(y_up, u0 + n - 2)
                                times_c(n - 1)
                            if n == 6:
                                relu(kn, prep)
                            if n == 11:
                                rest(kn, prep)
                            if n == 13:
                                low(kn, prep)
                            if n == 14:
                                delta(kn, prep)
                        dve.wait_ge(y_up, u0 + NST - 2)
                        times_c(NST - 1)
                        nc.vector.tensor_copy(HL[:, k * NST:(k + 1) * NST],
                                              H[:, :].rearrange("p (n t) -> p n t", n=NST)[:, :, end]
                                              ).then_inc(hl_up, 1)
                        dve.wait_ge(y_up, u0 + NST)
                        nc.vector.memset(NIL[:, :], 0.0)
                        at = (c if k < 2 else (NCH - 1) - c) * CH
                        nc.vector.tensor_tensor(y_sum[:, bass.ds(at, CH)], y_sum[:, bass.ds(at, CH)],
                                                PS[:, Y_BANK, :], ALU.add).then_inc(y_out, 1)
                        dve.wait_ge(hl_up, it + b + 2)
                        dve.wait_ge(y_out, it + 2)

                for g in range(2):
                    for i in range(4):
                        j = 4 * g + i
                        yj = YA[:, j * CH:(j + 1) * CH]
                        nc.vector.tensor_tensor(yj.rearrange("p (h w) -> p h w", w=IMG),
                                                yj.rearrange("p (h w) -> p h w", w=IMG),
                                                YBv[:, j * ROWS:(j + 1) * ROWS, :], ALU.add).then_inc(ln_dve, 1)
                    for i in range(4):
                        j = 4 * g + i
                        yj = YA[:, j * CH:(j + 1) * CH]
                        dve.wait_ge(ln_act, b * 24 + g * 12 + 8 + i + 1)
                        dve.wait_ge(ln_pe, b * 16 + g * 8 + 4 + i + 1)
                        nc.vector.scalar_tensor_tensor(H[:, (4 + i) * CH:(5 + i) * CH], PS[:, i, :], w("ln_g"),
                                                       H[:, (4 + i) * CH:(5 + i) * CH], ALU.mult,
                                                       ALU.mult).then_inc(ln_w, 1)
                        dve.wait_ge(ln_w, b * 8 + g * 4 + i + 1)
                        nc.vector.scalar_tensor_tensor(yj, H[:, (4 + i) * CH:(5 + i) * CH], w("ln_b"),
                                                       Z[:, j * CH:(j + 1) * CH], ALU.add,
                                                       ALU.mult).then_inc(ln_dve, 1)
                with dve.Fori(0, NCH) as j:
                    dve.wait_ge(x_in, (b + 1) * 32)
                    dve.wait_ge(ev, b * NGA + 8 * NCH + j + 1 + 2)
                    nc.vector.tensor_tensor(Z[:, bass.ds(j * CH, CH)], X[:, bass.ds(j * CH, CH)],
                                            Z[:, bass.ds(j * CH, CH)], ALU.add).then_inc(res, 1)


class Norm:

    def __init__(self, nc, sem, PS, SQ, RST, center, ones, eps):
        self.nc, self.PS, self.SQ, self.RST = nc, PS, SQ, RST
        self.center, self.ones, self.eps = center, ones, eps
        self.centred, self.squared, self.meaned = sem("n_centred"), sem("n_squared"), sem("n_meaned")
        self.logged, self.scaled, self.out = sem("n_logged"), sem("n_scaled"), sem("n_out")

    def begin(self, dve):
        dve.sem_inc(self.out, 4)

    def pe(self, pe, n0, src, ready):
        for i in range(4):
            ready(i)
            pe.wait_ge(self.out, n0 + i + 1)
            self.nc.tensor.matmul(self.PS[:, i, :], self.center, src(i), start=True,
                                  stop=True).then_inc(self.centred, 1)
        for i in range(4):
            pe.wait_ge(self.squared, n0 + i + 1)
            self.nc.tensor.matmul(self.PS[:, 4 + i, :], self.ones, self.SQ[:, i, :], start=True,
                                  stop=True).then_inc(self.meaned, 1)

    def act(self, act, n0):
        for i in range(4):
            act.wait_ge(self.centred, n0 + i + 1)
            self.nc.scalar.activation(self.SQ[:, i, :], self.PS[:, i, :], ACT.Square).then_inc(self.squared, 1)
        for i in range(4):
            act.wait_ge(self.meaned, n0 + i + 1)
            self.nc.scalar.activation(self.RST[:, i, :], self.PS[:, 4 + i, :], ACT.Ln,
                                      bias=self.eps).then_inc(self.logged, 1)
        for i in range(4):
            act.wait_ge(self.logged, n0 + i + 1)
            self.nc.scalar.activation(self.RST[:, i, :], self.RST[:, i, :], ACT.Exp,
                                      scale=-0.5).then_inc(self.scaled, 1)

    def dve(self, dve, n0, dst, gain=None):
        for i in range(4):
            dve.wait_ge(self.scaled, n0 + i + 1)
            if gain is None:
                self.nc.vector.tensor_tensor(dst(i), self.PS[:, i, :], self.RST[:, i, :],
                                             ALU.mult).then_inc(self.out, 1)
            else:
                self.nc.vector.scalar_tensor_tensor(dst(i), self.PS[:, i, :], gain, self.RST[:, i, :],
                                                    ALU.mult, ALU.mult).then_inc(self.out, 1)


def layer1(nc, x1, pack, XR):
    with ExitStack() as ctx:
        def sb(name, shape, dt=F32):
            return ctx.enter_context(nc.sbuf_tensor("l1_" + name, shape, dt))

        sem = semaphores(nc, ctx, "l1_")

        where, width = places(PACK1)
        W = sb("W", [P, width])

        def w(name, a=0, n=None):
            at, size = where[name]
            return W[:, at + a:at + (size if n is None else a + n)]

        PAIR = 2 * TOK
        G = sb("G", [P, IMG, 2, IMG])
        AB = sb("AB", [P, 2, IMG, P])
        SQ = sb("SQ", [P, 4, CH])
        RST = sb("RST", [P, 4, CH])
        OT = sb("OT", [P, 4, CH])
        T = sb("T", [P, 2, CH])
        SG = sb("SG", [P, 2, 2 * P])
        ST = sb("ST", [P, NCH, 6])
        MV = sb("MV", [P, NB, 2])
        GM = sb("GM", [P, NB, 2])
        PS = ctx.enter_context(nc.psum_tensor("l1_PS", [P, 8, CH], F32))

        x_in = [sem("x_in%d" % b) for b in range(NB)]
        loaded = sem("loaded")
        stats, group, gstat, glog = sem("stats"), sem("group"), sem("gstat"), sem("glog")
        gn_up = sem("gn_up")
        zn_up = sem("zn_up")
        ab_mm, ab_t, ab_s, ab_up = sem("ab_mm"), sem("ab_t"), sem("ab_s"), sem("ab_up")
        g_mm, g_up = sem("g_mm"), sem("g_up")
        o_mm = sem("o_mm")
        o_act, o_dve = sem("o_act"), sem("o_dve")
        t_up, t_out = sem("t_up"), sem("t_out")
        on_up, wo_mm, y_gate, y_up = sem("on_up"), sem("wo_mm"), sem("y_gate"), sem("y_up")
        norm = Norm(nc, sem, PS, SQ, RST, w("center"), w("ones"), w("eps"))

        def chunk(q):
            return G[:, :, :, :].rearrange("p i m k -> p (i m k)")[:, bass.ds(q * CH, CH)]

        NCOL = P // 8
        block = ctx.enter_context(nc.Block())

        @block.sync
        def _(sp):
            sp.dma_start(W[:, :], pack).then_inc(loaded, 16)
            if x1 is not None:
                for b in range(NB):
                    sp.dma_start(XR[:, b * TOK:(b + 1) * TOK], x1[:, b * TOK:(b + 1) * TOK]).then_inc(x_in[b], 16)

        @block.tensor
        def _(pe):
            pe.wait_ge(loaded, 16)
            pe.wait_ge(stats, NB * (NCH + 1) + 2)
            nc.tensor.matmul(PS[:, 0, 0:2 * NB], w("group4"), MV[:, :, :], start=True,
                             stop=True).then_inc(group, 1)
            for pr in range(2):
                pe.wait_ge(gn_up, 2 * (pr + 1))
                with pe.Fori(0, 4) as g:
                    norm.pe(pe, pr * 32 + g * 4, lambda i: chunk(g * 4 + i), lambda i: None)
                pe.wait_ge(zn_up, (pr + 1) * 16)
                for i in range(IMG):
                    pe.wait_ge(ab_t, pr * IMG + i + 1)
                    nc.tensor.matmul(PS[:, i % 2, :], G[:, i, :, :], w("ab"),
                                     start=True, stop=True).then_inc(ab_mm, 1)
                    if i % 4 == 3:
                        q = i // 4
                        pe.wait_ge(g_up, pr * 16 + q + 1)
                        nc.tensor.matmul(PS[:, 2 + q % 2, :], w("g"), chunk(q), start=True,
                                         stop=True).then_inc(g_mm, 1)
                pe.wait_ge(ab_up, (pr + 1) * IMG)
                for c8 in range(NCOL):
                    pe.wait_ge(o_act if c8 % 2 == 0 else o_dve, pr * (NCOL // 2) + c8 // 2 + 1)
                    for c in range(8):
                        for m in range(2):
                            s = slice(m * HALF, (m + 1) * HALF)
                            ins = nc.tensor.matmul(PS[s, 4 + c8 % 2, c * IMG:(c + 1) * IMG],
                                                   AB[s, 0, :, c8 * 8 + c], AB[s, 1, :, c8 * 8 + c],
                                                   start=True, stop=True)
                    ins.then_inc(o_mm, 1)
                pe.wait_ge(o_act, (pr + 1) * (NCOL // 2) + 1)
                pe.wait_ge(o_dve, (pr + 1) * (NCOL // 2) + 1)
                for g in range(4):
                    n0 = pr * 16 + g * 4
                    for i in range(4):
                        pe.wait_ge(y_gate, n0 + i + 1)
                        for j in range(4):
                            ins = nc.tensor.transpose(PS[:, 4 + i, j * P:(j + 1) * P],
                                                      AB[:, 0, (g * 4 + i) * 4 + j, :], w("ident"))
                        ins.then_inc(t_up, 1)
                    norm.pe(pe, pr * 32 + 16 + g * 4, lambda i: OT[:, i, :],
                            lambda i: pe.wait_ge(t_out, n0 + i + 1))
                    for i in range(4):
                        pe.wait_ge(on_up, n0 + i + 1)
                        nc.tensor.matmul(PS[:, 4 + i, :], w("o"), OT[:, i, :], start=True,
                                         stop=True).then_inc(wo_mm, 1)

        @block.scalar
        def _(act):
            act.wait_ge(loaded, 16)
            act.sem_inc(g_up, 2)
            act.sem_inc(o_act, 1)
            act.wait_ge(gstat, 2)
            nc.scalar.activation(GM[:, :, 1], GM[:, :, 1], ACT.Ln, bias=w("eps")).then_inc(glog, 1)
            act.wait_ge(glog, 1)
            nc.scalar.activation(GM[:, :, 1], GM[:, :, 1], ACT.Exp, scale=-0.5).then_inc(glog, 1)
            with act.Fori(0, 2) as pr:
                with act.Fori(0, 4) as g:
                    norm.act(act, pr * 32 + g * 4)
                for i in range(IMG):
                    act.wait_ge(ab_t, pr * IMG + i + 1 + 2)
                    act.wait_ge(ab_up, pr * IMG + i + 1 - 2) if i >= 2 else None
                    nc.scalar.activation(SG[:, i % 2, :], T[:, i % 2, 2 * P:], ACT.Sigmoid).then_inc(ab_s, 1)
                    if i % 4 == 3:
                        q = i // 4
                        act.wait_ge(g_mm, pr * 16 + q + 1)
                        nc.scalar.activation(chunk(q), PS[:, 2 + q % 2, :], ACT.Sigmoid, bias=w("bg")).then_inc(g_up, 1)
                for c8 in range(0, NCOL, 2):
                    act.wait_ge(o_mm, pr * NCOL + c8 + 1)
                    nc.scalar.copy(AB[:, 0, :, c8 * 8:(c8 + 1) * 8].rearrange("p j c -> p c j"),
                                   PS[:, 4 + c8 % 2, :].rearrange("p (c j) -> p c j", c=8)).then_inc(o_act, 1)
                for g in range(4):
                    n0 = pr * 16 + g * 4
                    for i in range(4):
                        act.wait_ge(t_up, n0 + i + 1)
                        act.wait_ge(y_up, n0 + i + 1)
                        nc.scalar.copy(OT[:, i, :], PS[:, 4 + i, :]).then_inc(t_out, 1)
                    norm.act(act, pr * 32 + 16 + g * 4)

        @block.gpsimd
        def _(pool):
            with pool.Fori(0, 2) as pr:
                for i in range(IMG):
                    pool.wait_ge(ab_s, pr * IMG + i + 1)
                    nc.gpsimd.tensor_tensor(AB[:, :, i, :], T[:, i % 2, 0:2 * P].rearrange("p (m c) -> p m c", m=2),
                                            SG[:, i % 2, :].rearrange("p (m c) -> p m c", m=2),
                                            ALU.mult).then_inc(ab_up, 1)

        @block.vector
        def _(dve):
            norm.begin(dve)
            dve.sem_inc(ab_t, 2)
            dve.sem_inc(o_dve, 1)
            dve.sem_inc(y_gate, 4)
            dve.sem_inc(y_up, 4)
            for b in range(NB):
                if x1 is not None:
                    dve.wait_ge(x_in[b], 16)
                for j in range(NCH):
                    at = b * TOK + j * CH
                    if b:
                        dve.wait_ge(stats, b * (NCH + 1))
                    nc.vector.bn_stats(ST[:, j, :], XR[:, at:at + CH]).then_inc(stats, 1)
                dve.wait_ge(stats, b * (NCH + 1) + NCH)
                nc.vector.bn_aggr(MV[:, b, :], ST[:, :, :]).then_inc(stats, 1)
            dve.wait_ge(stats, NB * (NCH + 1))
            nc.vector.tensor_tensor(GM[:, :, 0], MV[:, :, 0], MV[:, :, 0], ALU.mult).then_inc(stats, 1)
            dve.wait_ge(stats, NB * (NCH + 1) + 1)
            nc.vector.tensor_tensor(MV[:, :, 1], MV[:, :, 1], GM[:, :, 0], ALU.add).then_inc(stats, 1)
            dve.wait_ge(group, 1)
            nc.vector.tensor_copy(GM[:, :, :], PS[:, 0, 0:2 * NB].rearrange("p (b s) -> p b s", s=2)
                                  ).then_inc(group, 1)
            dve.wait_ge(group, 2)
            nc.vector.tensor_tensor(MV[:, :, 0], GM[:, :, 0], GM[:, :, 0], ALU.mult).then_inc(gstat, 1)
            dve.wait_ge(gstat, 1)
            nc.vector.tensor_tensor(GM[:, :, 1], GM[:, :, 1], MV[:, :, 0], ALU.subtract).then_inc(gstat, 1)
            dve.wait_ge(glog, 2)
            nc.vector.scalar_tensor_tensor(GM[:, :, 0], GM[:, :, 0], -1.0, GM[:, :, 1], ALU.mult,
                                           ALU.mult).then_inc(gstat, 1)
            dve.wait_ge(gstat, 3)
            with dve.Fori(0, 2) as pr:
                nc.vector.tensor_copy(MV[:, 0:2, :], GM[:, bass.ds(pr * 2, 2), :]).then_inc(gstat, 1)
                dve.wait_ge(gstat, pr + 4)
                for m in range(2):
                    nc.vector.tensor_scalar(G[:, :, m, :], XR[:, bass.ds(pr * PAIR + m * TOK, TOK)]
                                            .rearrange("p (i k) -> p i k", k=IMG),
                                            MV[:, m, 1:2], MV[:, m, 0:1], ALU.mult, ALU.add).then_inc(gn_up, 1)
                with dve.Fori(0, 4) as g:
                    n0 = pr * 32 + g * 4
                    for i in range(4):
                        dve.wait_ge(norm.scaled, n0 + i + 1)
                        nc.vector.scalar_tensor_tensor(
                            chunk(g * 4 + i), PS[:, i, :], w("ln1_g"), RST[:, i, :], ALU.mult,
                            ALU.mult).then_inc(norm.out, 1)
                    for i in range(4):
                        dve.wait_ge(norm.out, n0 + i + 1 + 4)
                        nc.vector.tensor_scalar(chunk(g * 4 + i), chunk(g * 4 + i), w("ln1_b"), None,
                                                ALU.add).then_inc(zn_up, 1)
                for i in range(IMG):
                    dve.wait_ge(ab_mm, pr * IMG + i + 1)
                    dve.wait_ge(ab_up, pr * IMG + i + 1 - 2) if i >= 2 else None
                    nc.vector.tensor_tensor(T[:, i % 2, :], PS[:, i % 2, :], w("ab_b"), ALU.add).then_inc(ab_t, 1)
                for c8 in range(1, NCOL, 2):
                    dve.wait_ge(o_mm, pr * NCOL + c8 + 1)
                    nc.vector.tensor_copy(AB[:, 0, :, c8 * 8:(c8 + 1) * 8].rearrange("p j c -> p c j"),
                                          PS[:, 4 + c8 % 2, :].rearrange("p (c j) -> p c j", c=8)
                                          ).then_inc(o_dve, 1)
                for g in range(4):
                    n0 = pr * 16 + g * 4
                    norm.dve(dve, pr * 32 + 16 + g * 4, lambda i: OT[:, i, :], w("ln2_g"))
                    for i in range(4):
                        dve.wait_ge(norm.out, pr * 32 + 16 + g * 4 + i + 1 + 4)
                        nc.vector.tensor_scalar(OT[:, i, :], OT[:, i, :], w("ln2_b"), None,
                                                ALU.add).then_inc(on_up, 1)
                    for i in range(4):
                        q = g * 4 + i
                        dve.wait_ge(wo_mm, n0 + i + 1)
                        for m in range(2):
                            gate = G[:, :, m, q * 4:q * 4 + 4].rearrange("p i j -> p j i")
                            ins = nc.vector.scalar_tensor_tensor(
                                OT[:, i, :].rearrange("p (j m t) -> p j m t", j=4, m=2)[:, :, m, :],
                                PS[:, 4 + i, :].rearrange("p (j m t) -> p j m t", j=4, m=2)[:, :, m, :],
                                w("bo"), gate, ALU.add, ALU.mult)
                        ins.then_inc(y_gate, 1)
                    for i in range(4):
                        q = g * 4 + i
                        dve.wait_ge(y_gate, n0 + i + 1 + 4)
                        x = XR[:, bass.ds(pr * PAIR, PAIR)].rearrange("p (t j) -> p j t", j=IMG)[:, q * 4:q * 4 + 4, :]
                        nc.vector.tensor_tensor(x, x, OT[:, i, :].rearrange("p (j t) -> p j t", j=4),
                                                ALU.add).then_inc(y_up, 1)


def layer2_attn(nc, pack, XR):
    with ExitStack() as ctx:
        def sb(name, shape, dt=F32):
            return ctx.enter_context(nc.sbuf_tensor("l2a_" + name, shape, dt))

        sem = semaphores(nc, ctx, "l2a_")

        where, width = places(PACK2)
        W = sb("W", [P, width])

        def w(name, a=0, n=None):
            at, size = where[name]
            return W[:, at + a:at + (size if n is None else a + n)]

        XN = sb("XN", [P, TOK])
        K = sb("K", [P, TOK])
        QT = sb("QT", [P, TOK])
        SQ = sb("SQ", [P, 4, CH])
        RST = sb("RST", [P, 4, CH])
        KM = sb("KM", [P, NCH])
        KV = sb("KV", [P, 3])
        QS = sb("QS", [P, 2, 16, 32])
        MX, SM = sb("MX", [P, 2, 16]), sb("SM", [P, 2, 16])
        VS, KT = sb("VS", [P, 2, 4, P]), sb("KT", [P, 2, 4, P])
        CT, MT = sb("CT", [P, P]), sb("MT", [P, P])
        ST = sb("ST", [P, NCH, 6])
        MV, GV = sb("MV", [P, 2]), sb("GV", [P, 4])
        NIL = sb("NIL", [P, 1])
        PS = ctx.enter_context(nc.psum_tensor("l2a_PS", [P, 8, CH], F32))
        KT_BANK, QT_BANK, CTX_BANK, MISC_BANK = 4, 5, 6, 7

        loaded = sem("loaded")
        k_mm, k_out, k_max, k_top = sem("k_mm"), sem("k_out"), sem("k_max"), sem("k_top")
        k_exp, k_rec = sem("k_exp"), sem("k_rec")
        qv_mm, q_max, q_sub, q_exp = sem("qv_mm"), sem("q_max"), sem("q_sub"), sem("q_exp")
        q_sum, q_rec, q_up = sem("q_sum"), sem("q_rec"), sem("q_up")
        v_out, kt_mm, kt_out, qt_mm, qt_out = sem("v_out"), sem("kt_mm"), sem("kt_out"), sem("qt_mm"), sem("qt_out")
        c_mm, c_up, m_mm, m_up = sem("c_mm"), sem("c_up"), sem("m_mm"), sem("m_up")
        o_mm, o_out, o_stat = sem("o_mm"), sem("o_out"), sem("o_stat")
        gs_mm, gs, gs_log, o_norm, done = sem("gs_mm"), sem("gs"), sem("gs_log"), sem("o_norm"), sem("done")
        norm = Norm(nc, sem, PS, SQ, RST, w("center"), w("ones"), w("eps"))

        def c(j, buf=None):
            return (XN if buf is None else buf)[:, j * CH:(j + 1) * CH]

        def qv(g):
            return PS[:, (g % 2) * 2:(g % 2) * 2 + 2, :].rearrange("p a n -> p (a n)").rearrange(
                "p (t n) -> p t n", t=4)

        def heads(ap):
            return ap.rearrange("p t (h d) -> p t h d", d=32)

        def bc(small, g):
            return small[:, g % 2, :].rearrange("p (t h) -> p t h", t=4).unsqueeze(3).to_broadcast([P, 4, 4, 32])

        block = ctx.enter_context(nc.Block())

        @block.sync
        def _(sp):
            sp.dma_start(W[:, :], pack).then_inc(loaded, 16)

        @block.tensor
        def _(pe):
            pe.wait_ge(loaded, 16)
            with pe.Fori(0, NB) as b:
                for g in range(2):
                    norm.pe(pe, b * NCH + g * 4, lambda i: XR[:, bass.ds(b * TOK + (4 * g + i) * CH, CH)],
                            lambda i: pe.wait_ge(done, b + 1))
                for j in range(NCH):
                    pe.wait_ge(norm.out, b * NCH + NCH + 4)
                    pe.wait_ge(k_out, b * NCH + j + 1)
                    nc.tensor.matmul(PS[:, j % 4, :], w("k"), c(j), start=True, stop=True).then_inc(k_mm, 1)
                pe.wait_ge(k_out, b * NCH + NCH + 4)

                def context(g):
                    pe.wait_ge(q_up, b * NCH + g + 1)
                    pe.wait_ge(qt_out, b * NCH + g + 1)
                    for t in range(4):
                        ins = nc.tensor.transpose(PS[:, QT_BANK, t * P:(t + 1) * P],
                                                  QS[:, g % 2, 4 * t:4 * t + 4, :].rearrange("p h d -> p (h d)"),
                                                  w("ident"))
                    ins.then_inc(qt_mm, 1)
                    pe.wait_ge(v_out, b * NCH + g + 1 + 2)
                    pe.wait_ge(kt_out, b * NCH + g + 1 + 1)
                    for t in range(4):
                        ins = nc.tensor.matmul(PS[:, CTX_BANK, 0:P], KT[:, g % 2, t, :], VS[:, g % 2, t, :],
                                               start=(g == 0 and t == 0), stop=(g == NCH - 1 and t == 3))
                    ins.then_inc(c_mm, 1)

                for g in range(NCH):
                    pe.wait_ge(v_out, b * NCH + g + 1)
                    for t in range(4):
                        ins = nc.tensor.matmul(qv(g)[:, t, :], XN[:, (4 * g + t) * P:(4 * g + t + 1) * P],
                                               w("qv"), start=True, stop=True)
                    ins.then_inc(qv_mm, 1)
                    pe.wait_ge(k_exp, b + 1)
                    pe.wait_ge(kt_out, b * NCH + g + 1)
                    for t in range(4):
                        ins = nc.tensor.transpose(PS[:, KT_BANK, t * P:(t + 1) * P],
                                                  K[:, (4 * g + t) * P:(4 * g + t + 1) * P], w("ident"))
                    ins.then_inc(kt_mm, 1)
                    if g >= 1:
                        context(g - 1)
                context(NCH - 1)
                pe.wait_ge(c_up, b + 1)
                nc.tensor.matmul(PS[:, MISC_BANK, 0:P], CT[:, :], w("out"), start=True, stop=True).then_inc(m_mm, 1)
                pe.wait_ge(m_up, b + 1)
                pe.wait_ge(qt_out, (b + 1) * NCH + 1)
                for j in range(NCH):
                    pe.wait_ge(o_out, b * NCH + j + 1)
                    nc.tensor.matmul(PS[:, j % 4, :], MT[:, :], c(j, QT), start=True, stop=True).then_inc(o_mm, 1)
                pe.wait_ge(gs, b * 7 + 3)
                nc.tensor.matmul(PS[:, MISC_BANK, 0:2], w("ones"), MV[:, :], start=True,
                                 stop=True).then_inc(gs_mm, 1)

        @block.scalar
        def _(act):
            act.wait_ge(loaded, 16)
            act.sem_inc(k_out, 4)
            act.sem_inc(v_out, 2)
            act.sem_inc(kt_out, 1)
            act.sem_inc(o_out, 4)
            with act.Fori(0, NB) as b:
                for g in range(2):
                    norm.act(act, b * NCH + g * 4)
                for j in range(NCH):
                    act.wait_ge(k_mm, b * NCH + j + 1)
                    nc.scalar.copy(c(j, K), PS[:, j % 4, :]).then_inc(k_out, 1)
                act.wait_ge(k_top, b + 1)
                nc.scalar.activation(K[:, :], K[:, :], ACT.Exp, bias=KV[:, 0:1],
                                     accum_out=KV[:, 1:2]).then_inc(k_exp, 1)
                for g in range(NCH):
                    act.wait_ge(q_sub, b * NCH + g + 1)
                    nc.scalar.activation(QS[:, g % 2, :, :], QS[:, g % 2, :, :], ACT.Exp).then_inc(q_exp, 1)
                    if g >= 2:
                        act.wait_ge(c_mm, b * NCH + g - 1)
                    nc.scalar.copy(VS[:, g % 2, :, :], qv(g)[:, :, P:2 * P]).then_inc(v_out, 1)
                    act.wait_ge(kt_mm, b * NCH + g + 1)
                    nc.scalar.copy(KT[:, g % 2, :, :], PS[:, KT_BANK, :].rearrange("p (t n) -> p t n", t=4)
                                   ).then_inc(kt_out, 1)
                for j in range(NCH):
                    act.wait_ge(o_mm, b * NCH + j + 1)
                    nc.scalar.activation(c(j, K), PS[:, j % 4, :], ACT.Identity, bias=w("b_out")).then_inc(o_out, 1)
                act.wait_ge(gs, b * 7 + 6)
                nc.scalar.activation(GV[:, 1:2], GV[:, 1:2], ACT.Ln, bias=w("eps")).then_inc(gs_log, 1)
                act.wait_ge(gs_log, b * 2 + 1)
                nc.scalar.activation(GV[:, 1:2], GV[:, 1:2], ACT.Exp, scale=-0.5).then_inc(gs_log, 1)

        @block.vector
        def _(dve):
            norm.begin(dve)
            dve.sem_inc(qt_out, 1)
            dve.sem_inc(done, 1)
            with dve.Fori(0, NB) as b:
                for g in range(2):
                    norm.dve(dve, b * NCH + g * 4, lambda i: c(4 * g + i))
                for j in range(NCH):
                    dve.wait_ge(k_out, b * NCH + j + 1 + 4)
                    nc.vector.tensor_reduce(KM[:, j:j + 1], c(j, K), AX_X, ALU.max).then_inc(k_max, 1)
                dve.wait_ge(k_max, (b + 1) * NCH)
                nc.vector.tensor_reduce(KV[:, 0:1], KM[:, :], AX_X, ALU.max, negate=True).then_inc(k_top, 1)
                dve.wait_ge(k_exp, b + 1)
                nc.vector.reciprocal(KV[:, 2:3], KV[:, 1:2]).then_inc(k_rec, 1)

                def scale_q(g):
                    n = b * NCH + g + 1
                    dve.wait_ge(q_exp, n)
                    nc.vector.tensor_reduce(SM[:, g % 2, :], QS[:, g % 2, :, :], AX_X, ALU.add).then_inc(q_sum, 1)
                    dve.wait_ge(q_sum, n)
                    nc.vector.reciprocal(SM[:, g % 2, :], SM[:, g % 2, :]).then_inc(q_rec, 1)
                    dve.wait_ge(q_rec, n)
                    q4 = QS[:, g % 2, :, :].rearrange("p (t h) d -> p t h d", t=4)
                    nc.vector.tensor_tensor(q4, q4, bc(SM, g), ALU.mult).then_inc(q_up, 1)

                def take_q(g):
                    dve.wait_ge(qt_mm, b * NCH + g + 1)
                    nc.vector.tensor_copy(c(g, QT), PS[:, QT_BANK, :]).then_inc(qt_out, 1)

                for g in range(NCH):
                    n = b * NCH + g + 1
                    q = heads(qv(g)[:, :, 0:P])
                    dve.wait_ge(qv_mm, n)
                    nc.vector.tensor_reduce(MX[:, g % 2, :].rearrange("p (t h) -> p t h", t=4), q, AX_X,
                                            ALU.max).then_inc(q_max, 1)
                    dve.wait_ge(q_max, n)
                    if g >= 2:
                        dve.wait_ge(qt_mm, n - 2)
                    nc.vector.tensor_tensor(QS[:, g % 2, :, :].rearrange("p (t h) d -> p t h d", t=4), q,
                                            bc(MX, g), ALU.subtract).then_inc(q_sub, 1)
                    if g >= 1:
                        scale_q(g - 1)
                    if g >= 2:
                        take_q(g - 2)
                scale_q(NCH - 1)
                take_q(NCH - 2)
                take_q(NCH - 1)
                dve.wait_ge(c_mm, (b + 1) * NCH)
                dve.wait_ge(k_rec, b + 1)
                nc.vector.scalar_tensor_tensor(CT[:, :], PS[:, CTX_BANK, 0:P], KV[:, 2:3], w("heads"), ALU.mult,
                                               ALU.mult).then_inc(c_up, 1)
                dve.wait_ge(m_mm, b + 1)
                nc.vector.tensor_copy(MT[:, :], PS[:, MISC_BANK, 0:P]).then_inc(m_up, 1)
                for j in range(NCH):
                    dve.wait_ge(o_out, b * NCH + j + 1 + 4)
                    nc.vector.bn_stats(ST[:, j, :], c(j, K)).then_inc(o_stat, 1)
                dve.wait_ge(o_stat, (b + 1) * NCH)
                nc.vector.memset(NIL[:, :], 0.0)
                nc.vector.bn_aggr(MV[:, :], ST[:, :, :]).then_inc(gs, 1)
                dve.wait_ge(gs, b * 7 + 1)
                nc.vector.tensor_tensor(GV[:, 0:1], MV[:, 0:1], MV[:, 0:1], ALU.mult).then_inc(gs, 1)
                dve.wait_ge(gs, b * 7 + 2)
                nc.vector.tensor_tensor(MV[:, 1:2], MV[:, 1:2], GV[:, 0:1], ALU.add).then_inc(gs, 1)
                dve.wait_ge(gs_mm, b + 1)
                nc.vector.tensor_copy(GV[:, 0:2], PS[:, MISC_BANK, 0:2]).then_inc(gs, 1)
                dve.wait_ge(gs, b * 7 + 4)
                nc.vector.tensor_tensor(GV[:, 2:3], GV[:, 0:1], GV[:, 0:1], ALU.mult).then_inc(gs, 1)
                dve.wait_ge(gs, b * 7 + 5)
                nc.vector.tensor_tensor(GV[:, 1:2], GV[:, 1:2], GV[:, 2:3], ALU.subtract).then_inc(gs, 1)
                dve.wait_ge(gs_log, b * 2 + 2)
                nc.vector.tensor_tensor(GV[:, 2:3], GV[:, 1:2], w("gn_w"), ALU.mult).then_inc(gs, 1)
                dve.wait_ge(gs, b * 7 + 7)
                nc.vector.tensor_tensor(GV[:, 3:4], GV[:, 0:1], GV[:, 2:3], ALU.mult).then_inc(o_norm, 1)
                dve.wait_ge(o_norm, b * 3 + 1)
                nc.vector.tensor_tensor(GV[:, 3:4], w("gn_b"), GV[:, 3:4], ALU.subtract).then_inc(o_norm, 1)
                dve.wait_ge(o_norm, b * 3 + 2)
                nc.vector.tensor_scalar(K[:, :], K[:, :], GV[:, 2:3], GV[:, 3:4], ALU.mult,
                                        ALU.add).then_inc(o_norm, 1)
                dve.wait_ge(o_norm, b * 3 + 3)
                x = XR[:, bass.ds(b * TOK, TOK)]
                nc.vector.tensor_tensor(x, x, K[:, :], ALU.add).then_inc(done, 1)


def layer2_ffn(nc, pack, XR):
    with ExitStack() as ctx:
        def sb(name, shape, dt=F32):
            return ctx.enter_context(nc.sbuf_tensor("l2f_" + name, shape, dt))

        sem = semaphores(nc, ctx, "l2f_")

        where, width = places(PACK2)
        W = sb("W", [P, width])

        def w(name, a=0, n=None):
            at, size = where[name]
            return W[:, at + a:at + (size if n is None else a + n)]

        E8, SENT = NEXP2, NEXP2 - TOP2
        XN = sb("XN", [P, TOK])
        SQ = sb("SQ", [P, 4, CH])
        RST = sb("RST", [P, 4, CH])
        LG = sb("LG", [P, 4, E8 + SENT])
        FOUND = sb("FOUND", [P, 4, E8 + SENT])
        M8, TOP = sb("M8", [P, 4, 8]), sb("TOP", [P, 4, 8])
        EX = sb("EX", [P, 4, E8])
        SM = sb("SM", [P, 4])
        NIL = sb("NIL", [P, 1])
        GATE = sb("GATE", [P, 2, 4, E8])
        GT = sb("GT", [E8, CH])
        PR = sb("PR", [P, 2, E8, P])
        H1 = sb("H1", [P, 2, E8 // 2, P])
        H2 = sb("H2", [P, 2, E8 // 4, P])
        PS = ctx.enter_context(nc.psum_tensor("l2f_PS", [P, 8, CH], F32))
        R_BANK, GT_BANK, Y_BANK = 4, 5, 6

        loaded, ready = sem("loaded"), sem("ready")
        r_mm, r_step, r_exp, gate_up = sem("r_mm"), sem("r_step"), sem("r_exp"), sem("gate_up")
        gt_mm, gt_up = sem("gt_mm"), sem("gt_up")
        e_mm, pr_up, h1_up, h2_up, y_mm, done = (sem(n) for n in ("e_mm", "pr_up", "h1_up", "h2_up", "y_mm", "done"))
        norm = Norm(nc, sem, PS, SQ, RST, w("center"), w("ones"), w("eps"))
        NT = NCH * 4
        STEPS = 15

        block = ctx.enter_context(nc.Block())

        @block.sync
        def _(sp):
            sp.dma_start(W[:, :], pack).then_inc(loaded, 16)

        @block.tensor
        def _(pe):
            pe.wait_ge(loaded, 16)
            with pe.Fori(0, NB) as b:
                for g in range(2):
                    norm.pe(pe, b * NCH + g * 4, lambda i: XR[:, bass.ds(b * TOK + (4 * g + i) * CH, CH)],
                            lambda i: pe.wait_ge(done, b * NCH + 1))

                def tile(t):
                    return XN[:, t * P:(t + 1) * P]

                def router(g):
                    pe.wait_ge(r_step, (b * NCH + g) * STEPS + 1)
                    for t in range(4):
                        ins = nc.tensor.matmul(PS[:, R_BANK, t * E8:(t + 1) * E8], tile(4 * g + t), w("router"),
                                               start=True, stop=True)
                    ins.then_inc(r_mm, 1)

                def biases(g):
                    pe.wait_ge(gate_up, b * NCH + g + 1)
                    for t in range(4):
                        ins = nc.tensor.transpose(PS[0:E8, GT_BANK, t * P:(t + 1) * P], GATE[:, g % 2, t, :],
                                                  w("ident"))
                    ins.then_inc(gt_mm, 1)
                    pe.wait_ge(gt_up, b * NCH + g + 1)
                    pe.wait_ge(done, b * NCH + g + 1)
                    nc.tensor.matmul(PS[:, Y_BANK, :], w("expert_b")[0:E8, :], GT[:, :], start=True, stop=False)

                def experts(t):
                    pe.wait_ge(pr_up, b * NT + t + 1)
                    for half in range(2):
                        ins = nc.tensor.matmul(PS[:, (t % 2) * 2 + half, :], tile(t),
                                               w("experts", half * CH, CH), start=True, stop=True)
                    ins.then_inc(e_mm, 1)

                def sums(t):
                    pe.wait_ge(h2_up, b * NT + t + 1)
                    for half in range(2):
                        ins = nc.tensor.matmul(PS[:, Y_BANK, (t % 4) * P:(t % 4 + 1) * P], H2[:, t % 2, half, :],
                                               w("ident"), start=False, stop=(half == 1 and t % 4 == 3))
                    ins.then_inc(y_mm, 1)

                pe.wait_ge(norm.out, b * NCH + NCH + 4)
                router(0)
                for g in range(NCH):
                    for t in range(4 * g, 4 * g + 4):
                        experts(t)
                        if t % 4 == 1 and g + 1 < NCH:
                            router(g + 1)
                        if t >= 1 and t % 4 != 0:
                            if t % 4 == 1:
                                biases(g)
                            sums(t - 1)
                    sums(4 * g + 3)

        @block.scalar
        def _(act):
            with act.Fori(0, NB) as b:
                for g in range(2):
                    norm.act(act, b * NCH + g * 4)
                for g in range(NCH):
                    act.wait_ge(r_step, (b * NCH + g + 1) * STEPS + 11)
                    nc.scalar.activation(EX[:, :, :], EX[:, :, :], ACT.Exp).then_inc(r_exp, 1)
                    act.wait_ge(gt_mm, b * NCH + g + 1)
                    if g >= 1:
                        act.wait_ge(y_mm, b * NT + 4 * g - 3)
                    nc.scalar.copy(GT[:, :], PS[0:E8, GT_BANK, :]).then_inc(gt_up, 1)

        @block.gpsimd
        def _(pool):
            pool.wait_ge(loaded, 16)
            with pool.Fori(0, NB) as b:
                for t in range(NT):
                    pool.wait_ge(pr_up, b * NT + t + 1 + 2)
                    nc.gpsimd.tensor_tensor(H1[:, t % 2, :, :], PR[:, t % 2, 0:4, :], PR[:, t % 2, 4:8, :],
                                            ALU.add).then_inc(h1_up, 1)
                    pool.wait_ge(h1_up, b * NT + t + 1)
                    if t >= 2:
                        pool.wait_ge(y_mm, b * NT + t - 1)
                    nc.gpsimd.tensor_tensor(H2[:, t % 2, :, :], H1[:, t % 2, 0:2, :], H1[:, t % 2, 2:4, :],
                                            ALU.add).then_inc(h2_up, 1)

        @block.vector
        def _(dve):
            norm.begin(dve)
            dve.sem_inc(done, 1)
            dve.sem_inc(pr_up, 2)
            nc.vector.memset(LG[:, :, E8:], -BIG).then_inc(ready, 1)
            nc.vector.memset(TOP[:, :, :], -BIG).then_inc(ready, 1)
            dve.wait_ge(ready, 2)
            dve.wait_ge(loaded, 16)
            dve.sem_inc(r_step, STEPS)
            with dve.Fori(0, NB) as b:
                for g in range(2):
                    norm.dve(dve, b * NCH + g * 4, lambda i: XN[:, (4 * g + i) * CH:(4 * g + i + 1) * CH])

                def gates(g):
                    n0 = (b * NCH + g + 1) * STEPS
                    steps = [0]

                    def step(ins):
                        steps[0] += 1
                        ins.then_inc(r_step, 1)

                    def after():
                        dve.wait_ge(r_step, n0 + steps[0])

                    dve.wait_ge(r_mm, b * NCH + g + 1)
                    step(nc.vector.tensor_tensor(LG[:, :, 0:E8],
                                                 PS[:, R_BANK, 0:4 * E8].rearrange("p (t e) -> p t e", t=4),
                                                 w("router_b").rearrange("p (t e) -> p t e", t=4), ALU.add))
                    after()
                    nc.vector.memset(NIL[:, :], 0.0)
                    for t in range(4):
                        step(nc.vector.max(M8[:, t, :], LG[:, t, 0:E8]))
                    after()
                    step(nc.vector.tensor_copy(TOP[:, :, 0:TOP2], M8[:, :, 0:TOP2]))
                    after()
                    nc.vector.memset(NIL[:, :], 0.0)
                    for t in range(4):
                        step(nc.vector.match_replace(FOUND[:, t, :], TOP[:, t, :], LG[:, t, :], BIG))
                    step(nc.vector.tensor_tensor(EX[:, :, :], LG[:, :, 0:E8],
                                                 M8[:, :, 0:1].to_broadcast([P, 4, E8]), ALU.subtract))
                    after()
                    dve.wait_ge(r_exp, b * NCH + g + 1)
                    step(nc.vector.scalar_tensor_tensor(EX[:, :, :], FOUND[:, :, 0:E8], BIG / 2, EX[:, :, :],
                                                        ALU.is_ge, ALU.mult))
                    after()
                    step(nc.vector.tensor_reduce(SM[:, :], EX[:, :, :], AX_X, ALU.add))
                    after()
                    step(nc.vector.reciprocal(SM[:, :], SM[:, :]))
                    after()
                    nc.vector.tensor_tensor(GATE[:, g % 2, :, :], EX[:, :, :],
                                            SM[:, :].unsqueeze(2).to_broadcast([P, 4, E8]),
                                            ALU.mult).then_inc(gate_up, 1)
                    dve.wait_ge(gate_up, b * NCH + g + 1)
                    dve.sem_inc(r_step, STEPS - steps[0])

                gates(0)
                for g in range(NCH):
                    for t in range(4 * g, 4 * g + 4):
                        dve.wait_ge(e_mm, b * NT + t + 1)
                        if t >= 2:
                            dve.wait_ge(h1_up, b * NT + t - 1)
                        nc.vector.tensor_tensor(
                            PR[:, t % 2, :, :],
                            PS[:, (t % 2) * 2:(t % 2) * 2 + 2, :].rearrange("p a n -> p (a n)").rearrange(
                                "p (e c) -> p e c", e=E8),
                            GATE[:, g % 2, t % 4, :].unsqueeze(2).to_broadcast([P, E8, P]),
                            ALU.mult).then_inc(pr_up, 1)
                        if t % 4 == 2 and g + 1 < NCH:
                            gates(g + 1)
                    dve.wait_ge(y_mm, b * NT + 4 * g + 4)
                    x = XR[:, bass.ds(b * TOK + g * CH, CH)]
                    nc.vector.tensor_tensor(x, x, PS[:, Y_BANK, :], ALU.add).then_inc(done, 1)


def layer3_attn(nc, pack, XR):
    with ExitStack() as ctx:
        def sb(name, shape, dt=F32):
            return ctx.enter_context(nc.sbuf_tensor("l3a_" + name, shape, dt))

        sem = semaphores(nc, ctx, "l3a_")

        where, width = places(PACK3)
        W = sb("W", [P, width])

        def w(name, a=0, n=None):
            at, size = where[name]
            return W[:, at + a:at + (size if n is None else a + n)]

        VW = HD * P
        XN = sb("XN", [P, NTOK])
        SQ = sb("SQ", [P, 4, CH])
        RST = sb("RST", [P, 4, CH])
        KS = SQ
        SC = sb("SC", [P, 5, CH])
        S, E, M, RU, U1 = (SC[:, n, :] for n in range(5))
        ONE = sb("ONE", [P, CH])
        END = sb("END", [P, 2])
        ET = sb("ET", [P, (NCH + 1) * 4, NB, HD])
        RT = sb("RT", [P, (NCH + 1) * 4, NB, HD])
        XS = sb("XS", [P, 2, CH])
        V = SC[:, 0:4, :].rearrange("p (a c) n -> p a (c n)", a=2).rearrange("p a (h d) -> p a h d", h=HD)
        WP = sb("WP", [P, 2, HD, P])
        Vs = RST[:, :, :].rearrange("p (a c) n -> p a (c n)", a=2)
        H1 = sb("H1", [P, 4, P])
        H2 = sb("H2", [P, 2, 2, P])
        Y = SQ[:, 0:2, :].rearrange("p a n -> p (a n)").rearrange("p (h d) -> p h d", h=HD)
        PS = ctx.enter_context(nc.psum_tensor("l3a_PS", [P, 8, CH], F32))

        loaded, zeroed = sem("loaded"), sem("zeroed")
        k_mm, k_up, s_mm = sem("k_mm"), sem("k_up"), sem("s_mm")
        s_out, s_max, s_sub, e_up, u_up, r_up = (sem(n) for n in ("s_out", "s_max", "s_sub", "e_up", "u_up", "r_up"))
        tr_up, tr_out = sem("tr_up"), sem("tr_out")
        xs_up, v_mm, v_up, ve_up, w_mm, w_up = (sem(n) for n in ("xs_up", "v_mm", "v_up", "ve_up", "w_mm", "w_up"))
        y_up, h1_up, h2_up, y_mm, done, fresh = (sem(n) for n in ("y_up", "h1_up", "h2_up", "y_mm", "done", "fresh"))
        norm = Norm(nc, sem, PS, SQ, RST, w("center"), w("ones"), w("eps"))
        S_BANK, E_BANK, R_BANK = 2, 4, 5
        NU = NB * HD
        TB = 8
        NT = TOK // P

        def q_col(p, h):
            return w("q", h * (2 * P - 1) + P - 1 - p, P)

        block = ctx.enter_context(nc.Block())

        @block.sync
        def _(sp):
            sp.dma_start(W[:, :], pack).then_inc(loaded, 16)

        @block.tensor
        def _(pe):
            pe.wait_ge(loaded, 16)
            with pe.Fori(0, NTOK // CH // 4) as g:
                norm.pe(pe, g * 4, lambda i: XR[:, bass.ds((g * 4 + i) * CH, CH)], lambda i: None)
            pe.wait_ge(norm.out, NTOK // CH + 4)

            def turn(j):
                pe.wait_ge(r_up, j + 1)
                pe.wait_ge(e_up, j + 1)
                pe.wait_ge(tr_out, j * 2 + 1)
                for src, bank in ((E, E_BANK), (RU, R_BANK)):
                    for t in range(4):
                        ins = nc.tensor.transpose(PS[:, bank, t * P:(t + 1) * P], src[:, t * P:(t + 1) * P],
                                                  w("ident"))
                ins.then_inc(tr_up, 1)

            with pe.Fori(0, NCH) as j:
                def score(u):
                    b, h = divmod(u, HD)
                    if u == 0:
                        pe.wait_ge(s_out, j + 1)
                    pe.wait_ge(k_up, j * NU + u + 1 + 2)
                    nc.tensor.matmul(PS[:, S_BANK, :], q_col(32 * b + h, h), KS[:, u % 2, :], start=(u == 0),
                                     stop=(u == NU - 1)).then_inc(s_mm, 1)

                for u in range(NU):
                    b, h = divmod(u, HD)
                    pe.wait_ge(k_up, j * NU + u + 1)
                    nc.tensor.matmul(PS[:, u % 2, :], w("k", h * P, P), XN[:, bass.ds(b * TOK + j * CH, CH)],
                                     start=True, stop=True).then_inc(k_mm, 1)
                    if u >= 1:
                        score(u - 1)
                    if u == 16:
                        turn(j)
                score(NU - 1)
            turn(NCH)
            pe.wait_ge(tr_out, NCH * 2 + 3)
            pe.wait_ge(k_up, NCH * NU + 2)

            with pe.Fori(0, NB) as b:
                with pe.Fori(0, NT // TB) as jj:
                    n0 = (b * (NT // TB) + jj) * TB
                    c0 = (b * (NT // TB) + jj) * 2

                    def values(t):
                        if t % 4 == 0:
                            pe.wait_ge(xs_up, c0 + t // 4 + 1)
                        pe.wait_ge(v_up, n0 + t + 1)
                        for half in range(2):
                            ins = nc.tensor.matmul(PS[:, (t % 2) * 6 + half, :],
                                                   XS[:, t // 4, (t % 4) * P:(t % 4 + 1) * P],
                                                   w("v", half * CH, CH), start=True, stop=True)
                        ins.then_inc(v_mm, 1)

                    def running(t):
                        pe.wait_ge(ve_up, n0 + t + 1 + 2)
                        pe.wait_ge(w_up, n0 + t + 2)
                        for half in range(2):
                            nc.tensor.matmul(PS[:, 2 + half, :], w("upto"),
                                             V[:, t % 2, 4 * half:4 * half + 4, :].rearrange("p h d -> p (h d)"),
                                             start=True, stop=False)
                            ins = nc.tensor.matmul(
                                PS[:, 2 + half, :], w("last"),
                                WP[:, (t + 1) % 2, 4 * half:4 * half + 4, :].rearrange("p h d -> p (h d)"),
                                start=False, stop=True)
                        ins.then_inc(w_mm, 1)

                    def result(t):
                        if t % 4 == 0:
                            pe.wait_ge(done, c0 + t // 4 + 1)
                        pe.wait_ge(h2_up, n0 + t + 1)
                        for half in range(2):
                            ins = nc.tensor.matmul(PS[:, 4 + t // 4, (t % 4) * P:(t % 4 + 1) * P],
                                                   H2[:, t % 2, half, :], w("ident"),
                                                   start=(half == 0), stop=(half == 1))
                        ins.then_inc(y_mm, 1)

                    values(0)
                    for t in range(TB):
                        if t + 1 < TB:
                            values(t + 1)
                        running(t)
                        if t >= 1:
                            result(t - 1)
                    result(TB - 1)

        @block.scalar
        def _(act):
            act.wait_ge(loaded, 16)
            with act.Fori(0, NTOK // CH // 4) as g:
                norm.act(act, g * 4)
            act.wait_ge(norm.meaned, NTOK // CH)
            act.sem_inc(k_up, 2)
            act.sem_inc(v_up, 2)
            act.sem_inc(w_up, 2)
            act.sem_inc(e_up, 1)
            with act.Fori(0, NCH) as j:
                for u in range(NU):
                    act.wait_ge(k_mm, j * NU + u + 1)
                    if u >= 2:
                        act.wait_ge(s_mm, j * NU + u - 1)
                    nc.scalar.activation(KS[:, u % 2, :], PS[:, u % 2, :], ACT.Silu).then_inc(k_up, 1)
                act.wait_ge(s_mm, (j + 1) * NU)
                act.wait_ge(s_sub, j + 1)
                act.wait_ge(tr_up, j + 1)
                nc.scalar.activation(E, E, ACT.Exp).then_inc(e_up, 1)
            with act.Fori(0, NB) as b:
                with act.Fori(0, NT // TB) as jj:
                    n0 = (b * (NT // TB) + jj) * TB

                    def keep(t):
                        act.wait_ge(w_mm, n0 + t + 1)
                        act.wait_ge(y_up, n0 + t + 1)
                        nc.scalar.copy(WP[:, t % 2, :, :].rearrange("p h d -> p (h d)"),
                                       PS[:, 2:4, :].rearrange("p a n -> p (a n)")).then_inc(w_up, 1)

                    act.wait_ge(fresh, b + 1)
                    for t in range(TB):
                        act.wait_ge(v_mm, n0 + t + 1)
                        act.wait_ge(ve_up, n0 + t + 1)
                        nc.scalar.activation(Vs[:, t % 2, :], PS[:, (t % 2) * 6:(t % 2) * 6 + 2, :]
                                             .rearrange("p a n -> p (a n)"), ACT.Silu).then_inc(v_up, 1)
                        if t >= 1:
                            keep(t - 1)
                    keep(TB - 1)

        @block.gpsimd
        def _(pool):
            nc.gpsimd.memset(ONE[:, :], 1.0).then_inc(zeroed, 1)
            pool.wait_ge(norm.out, NTOK // CH + 4)
            with pool.Fori(0, NB) as b:
                with pool.Fori(0, NT // TB) as jj:
                    n0 = (b * (NT // TB) + jj) * TB
                    pool.wait_ge(v_up, n0 + 2)
                    for u in range(2):
                        nc.gpsimd.tensor_copy(XS[:, u, :], XN[:, bass.ds(b * TOK + (jj * 2 + u) * CH, CH)]
                                              ).then_inc(xs_up, 1)
                    for t in range(TB):
                        pool.wait_ge(y_up, n0 + t + 1 + 2)
                        nc.gpsimd.tensor_tensor(H1[:, :, :], Y[:, 0:4, :], Y[:, 4:8, :], ALU.add).then_inc(h1_up, 1)
                        pool.wait_ge(h1_up, n0 + t + 1)
                        if t >= 2:
                            pool.wait_ge(y_mm, n0 + t - 1)
                        nc.gpsimd.tensor_tensor(H2[:, t % 2, :, :], H1[:, 0:2, :], H1[:, 2:4, :],
                                                ALU.add).then_inc(h2_up, 1)
                        pool.wait_ge(h2_up, n0 + t + 1)

        @block.vector
        def _(dve):
            norm.begin(dve)
            dve.sem_inc(s_out, 1)
            dve.sem_inc(tr_out, 2)
            dve.sem_inc(ve_up, 2)
            dve.sem_inc(y_up, 2)
            dve.sem_inc(done, 2)
            nc.vector.memset(E, 0.0).then_inc(zeroed, 1)
            nc.vector.memset(RU, 0.0).then_inc(r_up, 1)
            nc.vector.memset(END[:, 0:1], -BIG).then_inc(zeroed, 1)
            nc.vector.memset(END[:, 1:2], 0.0).then_inc(zeroed, 1)
            with dve.Fori(0, NTOK // CH // 4) as g:
                norm.dve(dve, g * 4, lambda i: XN[:, bass.ds((g * 4 + i) * CH, CH)])
            dve.wait_ge(zeroed, 4)

            def take(j):
                dve.wait_ge(tr_up, j + 1)
                for dst, bank in ((ET, E_BANK), (RT, R_BANK)):
                    nc.vector.tensor_copy(dst[:, bass.ds(j * 4, 4), :, :],
                                          PS[:, bank, :].rearrange("p (t b h) -> p t b h", t=4, b=NB)[:, :, :, 0:HD]
                                          ).then_inc(tr_out, 1)

            with dve.Fori(0, NCH) as j:
                take(j)
                dve.wait_ge(s_mm, (j + 1) * NU)
                nc.vector.tensor_copy(S, PS[:, S_BANK, :]).then_inc(s_out, 1)
                dve.wait_ge(s_out, j + 2)
                nc.vector.tensor_tensor_scan(M, S, S, END[:, 0:1], ALU.max,
                                             ALU.max).then_inc(s_max, 1)
                dve.wait_ge(s_max, j * 2 + 1)
                nc.vector.tensor_copy(END[:, 0:1], M[:, CH - 1:CH]).then_inc(s_max, 1)
                nc.vector.tensor_tensor(E, S, M, ALU.subtract).then_inc(s_sub, 1)
                dve.wait_ge(e_up, j + 2)
                nc.vector.tensor_tensor_scan(U1, ONE[:, :], E, END[:, 1:2], ALU.mult,
                                             ALU.add).then_inc(u_up, 1)
                dve.wait_ge(u_up, j * 3 + 1)
                nc.vector.tensor_copy(END[:, 1:2], U1[:, CH - 1:CH]).then_inc(u_up, 1)
                nc.vector.reciprocal(RU, U1).then_inc(u_up, 1)
                dve.wait_ge(u_up, j * 3 + 3)
                nc.vector.tensor_scalar(RU, RU, 1.0 / HD, None, ALU.mult).then_inc(r_up, 1)
                dve.wait_ge(r_up, j + 2)
            take(NCH)
            dve.wait_ge(tr_out, NCH * 2 + 4)

            with dve.Fori(0, NB) as b:
                nc.vector.memset(WP[:, 1, :, :], 0.0).then_inc(fresh, 1)
                with dve.Fori(0, NT // TB) as jj:
                    n0 = (b * (NT // TB) + jj) * TB
                    c0 = (b * (NT // TB) + jj) * 2

                    def by_head(table, t):
                        return table[:, bass.ds((jj * TB + t + 4), 1), bass.ds(b, 1), :].rearrange(
                            "p t b h -> p (t b h)").unsqueeze(2).to_broadcast([P, HD, P])

                    def weigh(t):
                        dve.wait_ge(w_up, n0 + t + 1 + 2)
                        dve.wait_ge(h1_up, n0 + t) if t else None
                        nc.vector.tensor_tensor(Y[:, :, :], WP[:, t % 2, :, :], by_head(RT, t),
                                                ALU.mult).then_inc(y_up, 1)
                        if t % 4 == 3:
                            dve.wait_ge(y_mm, n0 + t + 1)
                            x = XR[:, bass.ds(b * TOK + (jj * 2 + t // 4) * CH, CH)]
                            nc.vector.tensor_tensor(x, x, PS[:, 4 + t // 4, :], ALU.add).then_inc(done, 1)

                    for t in range(TB):
                        dve.wait_ge(v_up, n0 + t + 1 + 2)
                        dve.wait_ge(w_up, n0 + t + 1)
                        nc.vector.tensor_tensor(V[:, t % 2, :, :], Vs[:, t % 2, :].rearrange("p (h d) -> p h d", h=HD),
                                                by_head(ET, t), ALU.mult).then_inc(ve_up, 1)
                        if t >= 1:
                            weigh(t - 1)
                    weigh(TB - 1)


def layer3_ffn(nc, pack, w1, w2, XR, out):
    with ExitStack() as ctx:
        def sb(name, shape, dt=F32):
            return ctx.enter_context(nc.sbuf_tensor("l3f_" + name, shape, dt))

        sem = semaphores(nc, ctx, "l3f_")

        where, width = places(PACK3F)
        W = sb("W", [P, width])

        def w(name, a=0, n=None):
            at, size = where[name]
            return W[:, at + a:at + (size if n is None else a + n)]

        QH = HID // P
        EG = 2
        XN = sb("XN", [P, 2 * TOK])
        SQ = sb("SQ", [P, 4, CH])
        RST = sb("RST", [P, 4, CH])
        PM = sb("PM", [P, 2, TOK])
        LG = sb("LG", [P, TOK])
        V4 = sb("V4", [P, 4])
        M8 = sb("M8", [P, 8])
        NIL = sb("NIL", [P, 1])
        XT = sb("XT", [P, 2, 3 * P])
        PO = sb("PO", [P, NB, NEXP3])
        W1 = sb("W1", [P, 2, EG, HID])
        W2 = sb("W2", [P, 2, EG, QH, P])
        HS = sb("HS", [P, 2, EG, QH, NB])
        OT = sb("OT", [P, NB, NEXP3])
        OE = sb("OE", [P, NB, P])
        PS = ctx.enter_context(nc.psum_tensor("l3f_PS", [P, 8, CH], F32))

        loaded = sem("loaded")
        l_mm, l_out, l_max, p_exp, p_rec, p_up = (sem(n) for n in ("l_mm", "l_out", "l_max", "p_exp", "p_rec", "p_up"))
        top, marked, chosen = sem("top"), sem("marked"), sem("chosen")
        t_mm, t_out, po_mm, po_up = sem("t_mm"), sem("t_out"), sem("po_mm"), sem("po_up")
        w1_in, w2_in = [sem("w1_in0"), sem("w1_in1")], [sem("w2_in0"), sem("w2_in1")]
        h_mm, h_b, h_up, o_mm, o_up = (sem(n) for n in ("h_mm", "h_b", "h_up", "o_mm", "o_up"))
        oe_zero, oe_mm, oe_up, y_mm, y_up, stored = (
            sem(n) for n in ("oe_zero", "oe_mm", "oe_up", "y_mm", "y_up", "stored"))
        norm = Norm(nc, sem, PS, SQ, RST, w("center"), w("ones"), w("eps"))
        NT = TOK // P
        NG = NEXP3 // EG

        block = ctx.enter_context(nc.Block())

        @block.sync
        def _(sp):
            sp.dma_start(W[:, :], pack).then_inc(loaded, 16)
            for u in range(2):
                sp.dma_start(W1[:, u, :, :], w1[:, u * EG:(u + 1) * EG, :]).then_inc(w1_in[u], 16)
                sp.dma_start(W2[:, u, :, :, :], w2[:, u * EG:(u + 1) * EG, :, :]).then_inc(w2_in[u], 16)
            with sp.Fori(1, NG // 2) as gg:
                for u in range(2):
                    at = (gg * 2 + u) * EG
                    sp.wait_ge(h_mm, (gg - 1) * 2 + u + 1)
                    sp.dma_start(W1[:, u, :, :], w1[:, bass.ds(at, EG), :]).then_inc(w1_in[u], 16)
                    sp.wait_ge(o_mm, (gg - 1) * 2 + u + 1)
                    sp.dma_start(W2[:, u, :, :, :], w2[:, bass.ds(at, EG), :, :]).then_inc(w2_in[u], 16)
            for n in range(2 * NB):
                sp.wait_ge(y_up, (n + 1) * NCH // 2 + 4)
                at = n * TOK // 2
                sp.dma_start(out[:, at:at + TOK // 2], XR[:, at:at + TOK // 2]).then_inc(stored, 16)
            sp.wait_ge(stored, 2 * NB * 16)

        @block.tensor
        def _(pe):
            pe.wait_ge(loaded, 16)
            for pr in range(2):
                for g in range(4):
                    if pr and g == 0:
                        pe.wait_ge(t_out, NT + 2)
                        pe.wait_ge(po_up, 2)
                    norm.pe(pe, pr * 16 + g * 4,
                            lambda i: XR[:, pr * 2 * TOK + (4 * g + i) * CH:pr * 2 * TOK + (4 * g + i + 1) * CH],
                            lambda i: None)
                pe.wait_ge(norm.out, pr * 16 + 16 + 4)
                for j in range(NCH):
                    pe.wait_ge(l_out, pr * NCH + j + 1)
                    for m in range(2):
                        at = m * TOK + j * CH
                        ins = nc.tensor.matmul(PS[:, j % 4, :], w("gate", m * P, P), XN[:, at:at + CH],
                                               start=(m == 0), stop=(m == 1))
                    ins.then_inc(l_mm, 1)

                def pooled(t):
                    pe.wait_ge(t_out, pr * NT + t + 1 + 2)
                    for m in range(2):
                        ins = nc.tensor.matmul(PS[:, 6 + m, 0:NEXP3], XT[:, t % 2, m * P:(m + 1) * P],
                                               XT[:, t % 2, 2 * P + m * NEXP3:2 * P + (m + 1) * NEXP3],
                                               start=(t == 0), stop=(t == NT - 1))
                    ins.then_inc(po_mm, 1)

                pe.wait_ge(chosen, pr + 1)
                for t in range(NT):
                    pe.wait_ge(t_out, pr * NT + t + 1)
                    for n, src in enumerate((XN[:, t * P:(t + 1) * P], XN[:, TOK + t * P:TOK + (t + 1) * P],
                                             PM[:, pr, t * P:(t + 1) * P])):
                        ins = nc.tensor.transpose(PS[:, 4 + t % 2, n * P:(n + 1) * P], src, w("ident"))
                    ins.then_inc(t_mm, 1)
                    if t >= 1:
                        pooled(t - 1)
                pooled(NT - 1)

            pe.wait_ge(po_up, 4)
            with pe.Fori(0, NG // 2) as gg:
                def hidden(u):
                    n = gg * 2 + u
                    pe.wait_ge(w1_in[u], (gg + 1) * 16)
                    pe.wait_ge(h_b, n + 1)
                    for e in range(EG):
                        for q in range(QH):
                            at = (e * QH + q) * NB
                            ins = nc.tensor.matmul(PS[:, u, at:at + NB], W1[:, u, e, q * P:(q + 1) * P],
                                                   PO[:, :, bass.ds(n * EG + e, 1)].rearrange("p b e -> p (b e)"),
                                                   start=True, stop=True)
                    ins.then_inc(h_mm, 1)

                def second(u):
                    n = gg * 2 + u
                    pe.wait_ge(w2_in[u], (gg + 1) * 16)
                    pe.wait_ge(h_up, n + 1)
                    pe.wait_ge(o_up, n + 1)
                    for e in range(EG):
                        for q in range(QH):
                            ins = nc.tensor.matmul(PS[:, 2 + u, e * NB:(e + 1) * NB], W2[:, u, e, q, :],
                                                   HS[:, u, e, q, :], start=(q == 0), stop=(q == QH - 1))
                    ins.then_inc(o_mm, 1)

                hidden(0)
                hidden(1)
                second(0)
                second(1)

            pe.wait_ge(o_up, NG + 2)
            for pr in range(2):
                nc.tensor.transpose(PS[:, 4 + pr, 0:P], OT[:, 2 * pr:2 * pr + 2, :].rearrange("p b e -> p (b e)"),
                                    w("ident")).then_inc(oe_mm, 1)
            pe.wait_ge(oe_up, NB)
            for n in range(NB * NCH):
                b, j = divmod(n, NCH)
                pe.wait_ge(y_up, n + 1)
                nc.tensor.matmul(PS[:, n % 4, :], OE[:, b, :], PM[:, b // 2, j * CH:(j + 1) * CH],
                                 start=True, stop=True).then_inc(y_mm, 1)

        @block.scalar
        def _(act):
            act.wait_ge(loaded, 16)
            act.sem_inc(l_out, 4)
            act.sem_inc(t_out, 2)
            for pr in range(2):
                for g in range(4):
                    norm.act(act, pr * 16 + g * 4)
                for j in range(NCH):
                    act.wait_ge(l_mm, pr * NCH + j + 1)
                    if pr and j == 0:
                        act.wait_ge(chosen, pr)
                    nc.scalar.activation(LG[:, j * CH:(j + 1) * CH], PS[:, j % 4, :], ACT.Identity,
                                         bias=w("gate_b")).then_inc(l_out, 1)
                act.wait_ge(l_max, pr + 1)
                nc.scalar.activation(PM[:, pr, :], LG[:, :], ACT.Exp, bias=V4[:, 0:1],
                                     accum_out=V4[:, 1:2]).then_inc(p_exp, 1)
                for t in range(NT):
                    act.wait_ge(t_mm, pr * NT + t + 1)
                    if t >= 2:
                        act.wait_ge(po_mm, pr * NT + t - 1)
                    nc.scalar.copy(XT[:, t % 2, :], PS[:, 4 + t % 2, 0:3 * P]).then_inc(t_out, 1)
            with act.Fori(0, NG // 2) as gg:
                for u in range(2):
                    act.wait_ge(h_b, gg * 2 + u + 1 + 2)
                    nc.scalar.activation(HS[:, u, :, :, :], HS[:, u, :, :, :], ACT.Gelu).then_inc(h_up, 1)

        @block.gpsimd
        def _(pool):
            nc.gpsimd.memset(OE[:, :, :], 0.0).then_inc(oe_zero, 1)

        @block.vector
        def _(dve):
            norm.begin(dve)
            dve.sem_inc(h_b, 2)
            dve.sem_inc(o_up, 2)
            dve.sem_inc(y_up, 4)
            for pr in range(2):
                for g in range(4):
                    norm.dve(dve, pr * 16 + g * 4, lambda i: XN[:, (4 * g + i) * CH:(4 * g + i + 1) * CH])
                dve.wait_ge(l_out, (pr + 1) * NCH + 4)
                nc.vector.tensor_reduce(V4[:, 0:1], LG[:, :], AX_X, ALU.max, negate=True).then_inc(l_max, 1)
                dve.wait_ge(p_exp, pr + 1)
                nc.vector.reciprocal(V4[:, 2:3], V4[:, 1:2]).then_inc(p_rec, 1)
                dve.wait_ge(p_rec, pr + 1)
                nc.vector.tensor_scalar(PM[:, pr, :], PM[:, pr, :], V4[:, 2:3], None, ALU.mult).then_inc(p_up, 1)
                dve.wait_ge(p_up, pr + 1)
                nc.vector.max(M8[:, :], PM[:, pr, :]).then_inc(top, 1)
                dve.wait_ge(top, pr + 1)
                nc.vector.match_replace(LG[:, :], M8[:, :], PM[:, pr, :], -1.0).then_inc(marked, 1)
                dve.wait_ge(marked, pr + 1)
                nc.vector.scalar_tensor_tensor(PM[:, pr, :], LG[:, :], 0.0, PM[:, pr, :], ALU.is_lt,
                                               ALU.mult).then_inc(chosen, 1)
                dve.wait_ge(po_mm, (pr + 1) * NT)
                nc.vector.tensor_copy(PO[:, 2 * pr:2 * pr + 2, :], PS[:, 6:8, 0:NEXP3]).then_inc(po_up, 2)
            with dve.Fori(0, NG // 2) as gg:
                for u in range(2):
                    n = gg * 2 + u
                    dve.wait_ge(h_mm, n + 1)
                    b1 = w("b1").rearrange("p (e q) -> p e q", q=QH)[:, bass.ds(n * EG, EG), :]
                    hid = HS[:, u, :, :, :].rearrange("p e q b -> p (e q) b")
                    nc.vector.tensor_tensor(hid, PS[:, u, 0:EG * QH * NB].rearrange("p (e b) -> p e b", b=NB),
                                            b1.rearrange("p e q -> p (e q)").unsqueeze(2)
                                            .to_broadcast([P, EG * QH, NB]), ALU.add).then_inc(h_b, 1)
                for u in range(2):
                    n = gg * 2 + u
                    dve.wait_ge(o_mm, n + 1)
                    nc.vector.tensor_tensor(OT[:, :, bass.ds(n * EG, EG)].rearrange("p b e -> p e b"),
                                            PS[:, 2 + u, 0:EG * NB].rearrange("p (e b) -> p e b", b=NB),
                                            w("b2")[:, bass.ds(n * EG, EG)].unsqueeze(2)
                                            .to_broadcast([P, EG, NB]), ALU.add).then_inc(o_up, 1)
            dve.wait_ge(oe_zero, 1)
            for b in range(NB):
                s = slice((b % 2) * HALF, (b % 2 + 1) * HALF)
                dve.wait_ge(oe_mm, b // 2 + 1)
                nc.vector.tensor_copy(OE[s, b, :], PS[s, 4 + b // 2, 0:P]).then_inc(oe_up, 1)
            for n in range(NB * NCH):
                dve.wait_ge(y_mm, n + 1)
                x = XR[:, n * CH:(n + 1) * CH]
                nc.vector.tensor_tensor(x, x, PS[:, n % 4, :], ALU.add).then_inc(y_up, 1)


def program(nc, xT, p0, sel, p1, p2, p3, p3f, w1, w2, out):
    x1 = nc.dram_tensor("layer0_out", [P, NTOK], F32).ap()
    layer0(nc, xT, p0, sel, x1)
    with nc.sbuf_tensor("XR", [P, NTOK], F32) as XR:
        layer1(nc, x1, p1, XR)
        layer2_attn(nc, p2, XR)
        layer2_ffn(nc, p2, XR)
        layer3_attn(nc, p3, XR)
        layer3_ffn(nc, p3f, w1, w2, XR, out)


def _pack(np, names, parts):
    at, width = places(names)
    out = np.zeros((P, width), np.float32)
    for name, part in parts.items():
        for row, col, a in part if isinstance(part, list) else [(0, 0, part)]:
            a = np.asarray(a)
            a = a.reshape(-1, 1) if a.ndim == 1 else a
            out[row:row + a.shape[0], at[name][0] + col:at[name][0] + col + a.shape[1]] = a
    return out


def _common(np):
    return {"ident": np.eye(P), "ones": np.full((P, P), 1.0 / P), "center": np.eye(P) - 1.0 / P,
            "eps": np.full(P, 1e-5)}


def _pack0(np, i):
    i = {k[len("L0_conv_"):]: np.asarray(v) for k, v in i.items() if k.startswith("L0_")}
    h = HALF
    shuffled = lambda a: a.reshape(2, h, -1).swapaxes(0, 1).reshape(P, -1)
    parts = dict(_common(np))
    parts["cv12"] = [(0, 0, i["cv2_w"].T), (h, h, i["cv1_w"].T)]
    for c in ("c1", "c2"):
        parts[c] = [(0, t * P, i[c + "_w"][t // 3, t % 3]) for t in range(9)]
    parts["c3"] = [(0, 0, i["c3_w"].T)]
    parts["in_xh"] = [(h, 0, i["in_proj_w"][:P].T)]
    parts["in_z"] = [(h, 0, i["in_proj_w"][P:].T)]
    xp = i["x_proj_w"]
    parts["xp_dt"] = [(0, k * P, xp[k, 0:4]) for k in range(NDIR)]
    parts["dt_w"] = [(0, k * P, i["dt_w"][k].T) for k in range(NDIR)]
    parts["bc"] = [(0, k * 96 + c * 32, xp[k, 4:].T) for k in range(NDIR) for c in range(3)]
    parts["out_proj"] = i["out_proj_w"]
    parts["cv"] = [(0, h, i["cv_w"].T)]
    parts["cv3"] = shuffled(i["cv3_w"]).T
    parts["dw"] = i["dw_w"].reshape(9, P).T
    parts["A_logs"] = i["A_logs"].reshape(NDIR, P, NST).transpose(1, 0, 2).reshape(P, -1)
    parts["Ds"] = i["Ds"].reshape(NDIR, P).T
    parts["dt_b"] = i["dt_b"].T
    parts["log3"] = np.broadcast_to([[1 / 3, 0.5, 1]], (P, 3))
    for c in "gb":
        parts["cv12_" + c] = [(0, 0, i["cv2_" + c]), (h, 0, i["cv1_" + c])]
        parts["cv3_" + c] = shuffled(i["cv3_" + c])
        parts["cv_" + c] = [(h, 0, i["cv_" + c])]
        for n in ("bn0_", "bn1_", "bn2_", "ln_"):
            parts[n + c] = i[n + c]
    for n in ("c1_b", "c2_b", "c3_b", "dw_b"):
        parts[n] = i[n]
    return _pack(np, PACK0, parts)


def _selectors(np):
    out = np.zeros((96, 2 * NST, P), mybir.dt.np(BF16))
    for r in range(2 * NST):
        out[[r, 32 + r, 64 + r], r] = 1
    return out.reshape(96, -1)


def _pack1(np, i):
    i = {k[len("L1_conv_"):]: np.asarray(v) for k, v in i.items() if k.startswith("L1_")}
    parts = dict(_common(np))
    parts["group4"] = np.kron(np.eye(P // 4), np.full((4, 4), 0.25))
    names = ("a", "b", "ga", "gb")
    parts["ab"] = [(0, n * P, i["W" + s]) for n, s in enumerate(names)]
    parts["ab_b"] = [(0, n * P, np.broadcast_to(i["b" + s], (P, P))) for n, s in enumerate(names)]
    parts["g"], parts["o"] = i["Wg"], i["Wo"]
    for n in ("ln1_g", "ln1_b", "ln2_g", "ln2_b", "bg", "bo"):
        parts[n] = i[n]
    return _pack(np, PACK1, parts)


def _pack2(np, i):
    a = {k[len("L2_attn_"):]: np.asarray(v) for k, v in i.items() if k.startswith("L2_attn_")}
    f = {k[len("L2_ffn_"):]: np.asarray(v) for k, v in i.items() if k.startswith("L2_ffn_")}
    parts = dict(_common(np))
    parts["heads"] = np.kron(np.eye(4), np.full((32, 32), 32 ** -0.5))
    q, k, v = a["W_qkv"].reshape(3, P, P)
    parts["k"], parts["qv"], parts["out"] = k.T, [(0, 0, q.T), (0, P, v.T)], a["W_out"].T
    parts["b_out"], parts["gn_w"], parts["gn_b"] = a["b_out"], a["gn_w"], a["gn_b"]
    parts["router"] = f["router_w"]
    parts["router_b"] = np.broadcast_to(np.concatenate([f["router_b"]] * 4), (P, 4 * NEXP2))
    parts["experts"] = f["expert_w"].transpose(1, 0, 2).reshape(P, -1)
    parts["expert_b"] = [(0, 0, f["expert_b"])]
    return _pack(np, PACK2, parts)


def _pack3(np, i):
    a = {k[len("L3_attn_"):]: np.asarray(v) for k, v in i.items() if k.startswith("L3_attn_")}
    parts = dict(_common(np))
    parts["upto"] = np.triu(np.ones((P, P)))
    parts["last"] = [(P - 1, 0, np.ones((1, P)))]
    kv = a["W_kv"].reshape(HD, P, 2, P)
    parts["k"], parts["v"] = (kv[:, :, n].transpose(2, 0, 1).reshape(P, -1) for n in range(2))
    parts["q"] = [(0, h * (2 * P - 1) + P - 1, a["q_proj"][h]) for h in range(HD)]
    return _pack(np, PACK3, parts)


def _pack3f(np, i):
    f = {k[len("L3_ffn_"):]: np.asarray(v) for k, v in i.items() if k.startswith("L3_ffn_")}
    parts = dict(_common(np))
    parts["gate"] = [(0, 0, f["gate_w"].T), (0, P + HALF, f["gate_w"].T)]
    parts["gate_b"] = np.concatenate([f["gate_b"]] * 2)
    parts["b1"] = f["weight1"][:, P].reshape(NEXP3, HID // P, P).transpose(2, 0, 1).reshape(P, -1)
    parts["b2"] = f["weight2"][:, HID].T
    return _pack(np, PACK3F, parts)


def _experts(np, i):
    w1, w2 = np.asarray(i["L3_ffn_weight1"])[:, :P], np.asarray(i["L3_ffn_weight2"])[:, :HID]
    return {"w1": np.ascontiguousarray(w1.transpose(1, 0, 2)),
            "w2": np.ascontiguousarray(w2.reshape(NEXP3, HID // P, P, P).transpose(2, 0, 1, 3))}


def kernel(**inputs):
    import numpy as np
    import concourse.bacc as bacc
    from concourse.bass_utils import run_bass_kernel_spmd

    x = np.asarray(inputs["x"])
    arrays = {
        "xT": np.ascontiguousarray(x.reshape(NTOK, P).T),
        "p0": _pack0(np, inputs), "sel": _selectors(np), "p1": _pack1(np, inputs), "p2": _pack2(np, inputs),
        "p3": _pack3(np, inputs), "p3f": _pack3f(np, inputs), **_experts(np, inputs),
    }
    nc = bacc.Bacc("TRN2", target_bir_lowering=False, num_devices=1)
    args = {n: nc.dram_tensor(n, a.shape, mybir.dt.from_np(a.dtype), kind="ExternalInput").ap()
            for n, a in arrays.items()}
    args["out"] = nc.dram_tensor("out", (P, NTOK), F32, kind="ExternalOutput").ap()
    program(nc, **args)
    r = run_bass_kernel_spmd(nc, [arrays], core_ids=[0])
    return np.ascontiguousarray(r.results[0]["out"].T).reshape(x.shape)
```

```python
from contextlib import ExitStack

import concourse.bass as bass
from concourse import mybir

ALU = mybir.AluOpType
ACT = mybir.ActivationFunctionType
AX_X = mybir.AxisListType.X
F32 = mybir.dt.float32
BF16 = mybir.dt.bfloat16

P = 128
NB, IMG = 4, 64
TOK = IMG * IMG
NTOK = NB * TOK
CH = 512
NCH = TOK // CH
ROWS = CH // IMG
PAD = IMG + 2
HALF = P // 2
NDIR, NST = 4, 16
NEXP2, TOP2 = 8, 2
HD = 8
NEXP3, HID = 64, 512
BIG = 3.0e38
EXP_LN, SILU = "natural_log_exp_and_others", "silu_and_others"

RING, ERING = 4, 8
HRING = 8
LEAD_B, LEAD_E, LEAD_C = 4, 4, 1

PACK0 = [
    ("ident", P), ("ones", P), ("center", P), ("eps", 1), ("one", 1), ("minus_one", 1),
    ("cv12", P), ("c1", 9 * P), ("c2", 9 * P), ("c3", P), ("in_xh", P), ("in_z", P),
    ("xp_dt", NDIR * P), ("dt_w", NDIR * P), ("bc", NDIR * 96), ("out_proj", P), ("cv", P), ("cv3", P),
    ("dw", 9), ("A_logs", NDIR * NST), ("Ds", NDIR), ("dt_b", NDIR),
    ("cv12_g", 1), ("cv12_b", 1), ("bn0_g", 1), ("bn0_b", 1), ("bn1_g", 1), ("bn1_b", 1), ("c1_b", 1),
    ("bn2_g", 1), ("bn2_b", 1), ("c2_b", 1), ("c3_b", 1), ("dw_b", 1), ("ln_g", 1), ("ln_b", 1),
    ("cv_g", 1), ("cv_b", 1), ("cv3_g", 1), ("cv3_b", 1),
]
PACK1 = [
    ("ident", P), ("ones", P), ("center", P), ("eps", 1), ("group4", P),
    ("ab", 4 * P), ("ab_b", 4 * P), ("g", P), ("o", P),
    ("ln1_g", 1), ("ln1_b", 1), ("ln2_g", 1), ("ln2_b", 1), ("bg", 1), ("bo", 1),
]
PACK2 = [
    ("ident", P), ("ones", P), ("center", P), ("eps", 1), ("heads", P),
    ("k", P), ("qv", 2 * P), ("out", P), ("b_out", 1), ("gn_w", 1), ("gn_b", 1),
    ("router", NEXP2), ("router_b", 4 * NEXP2), ("experts", NEXP2 * P), ("expert_b", P),
]
PACK3 = [
    ("ident", P), ("ones", P), ("center", P), ("eps", 1), ("upto", P), ("last", P),
    ("k", HD * P), ("v", HD * P), ("q", HD * (2 * P - 1)),
]
PACK3F = [
    ("ident", P), ("ones", P), ("center", P), ("eps", 1),
    ("gate", 2 * P), ("gate_b", 1), ("b1", NEXP3 * 4), ("b2", NEXP3),
]


def places(pack):
    at, out = 0, {}
    for name, width in pack:
        out[name] = (at, width)
        at += width
    return out, at


def semaphores(nc, ctx, prefix):
    held = []

    def sem(name):
        held.append(nc.alloc_semaphore(name=prefix + name))
        return held[-1]

    def close():
        nc.clear_and_free_semaphores(held)
        nc.all_engine_barrier()

    ctx.callback(close)
    return sem


def layer0(nc, xT, pack, sel, x1):
    with ExitStack() as ctx:
        def sb(name, shape, dt=F32):
            return ctx.enter_context(nc.sbuf_tensor("l0_" + name, shape, dt))

        sem = semaphores(nc, ctx, "l0_")

        where, width = places(PACK0)
        W = sb("W", [P, width])

        def w(name, a=0, n=None):
            at, size = where[name]
            return W[:, at + a:at + (size if n is None else a + n)]

        SEL = sb("SEL", [96, 2 * NST * P], BF16)
        WDT = sb("WDT", [P, NDIR * P])
        WCV = sb("WCV", [P, P])
        A = sb("A", [P, NDIR * NST])
        NIL, PNIL = sb("NIL", [P, 1]), sb("PNIL", [P, 1])
        VEC = sb("VEC", [P, 4])
        LX = sb("LX", [P, TOK])
        Z = sb("Z", [P, TOK])
        YA = sb("YA", [P, PAD * PAD])
        YB = sb("YB", [P, PAD * PAD])
        XH = sb("XH", [P, TOK + CH])
        XC = sb("XC", [P, TOK])
        H = sb("H", [P, (HRING + 1) * CH])
        HL = sb("HL", [P, NDIR * NST])
        BS, DBU, HC = (sb(n, [P, RING, CH]) for n in ("BS", "DBU", "HC"))
        DA = sb("DA", [P, ERING * CH])
        DL = sb("DL", [P, 2, CH])
        DU = sb("DU", [P, CH])
        S = sb("S", [96, 2, CH], BF16)
        TE, TU, TL, TP, TR = (sb(n, [P, CH]) for n in ("TE", "TU", "TL", "TP", "TR"))
        RS = H[0:HALF, HRING * CH:(HRING + 1) * CH]
        PS = ctx.enter_context(nc.psum_tensor("l0_PS", [P, 8, CH], F32))
        B_BANK, C_BANK, Y_BANK, DT_BANK, BC_BANK = 0, 2, 4, 6, 7

        DWD = DA[:, 0:9 * P]
        X = H[:, 0:TOK]
        C2 = XH
        AB = XC
        P1 = YA[:, :].rearrange("p (h w) -> p h w", h=PAD)
        P2 = YB[:, :].rearrange("p (h w) -> p h w", h=PAD)
        PH = H[:, 0:PAD * PAD].rearrange("p (h w) -> p h w", h=PAD)
        XCv = XC[:, 0:TOK].rearrange("p (w h) -> p h w", h=IMG)
        YBv = YB[:, 0:TOK].rearrange("p (w h) -> p h w", h=IMG)

        loaded = sem("loaded")
        x_in = sem("x_in")
        x_out = sem("x_out")
        setup_pe, setup_act, setup_dve = sem("setup_pe"), sem("setup_act"), sem("setup_dve")
        padded = sem("padded")
        bn0_done = sem("bn0_done")
        dwd_up = sem("dwd_up")
        cols_done = sem("cols_done")
        mm = sem("mm")
        ev = sem("ev")
        b_up, b_sb = sem("b_up"), sem("b_sb")
        dbu_up = sem("dbu_up")
        da_up = sem("da_up")
        scanned = sem("scanned")
        c_up = sem("c_up")
        hc_up = sem("hc_up")
        y_up = sem("y_up")
        pd_up, pb_up = sem("pd_up"), sem("pb_up")
        e_up, ln_up = sem("e_up"), sem("ln_up")
        ab_up = sem("ab_up")
        relu_up = sem("relu_up")
        u_up, t_up = sem("u_up"), sem("t_up")
        lp = sem("lp")
        dl_up, du_up = sem("dl_up"), sem("du_up")
        s_hi, s_mid, s_lo, r_up = sem("s_hi"), sem("s_mid"), sem("s_lo"), sem("r_up")
        y_out = sem("y_out")
        y_init = sem("y_init")
        hl_up = sem("hl_up")
        ln_pe, ln_act, ln_dve = sem("ln_pe"), sem("ln_act"), sem("ln_dve")
        ln_w = sem("ln_w")
        res = sem("res")

        NGA = 9 * NCH
        PREPS = NCH * NDIR + 1
        UNITS = NCH * NDIR * NST

        block = ctx.enter_context(nc.Block())

        @block.sync
        def _(sp):
            sp.dma_start(W[:, :], pack).then_inc(loaded, 16)
            sp.dma_start(SEL[:, :], sel).then_inc(loaded, 16)
            sp.sem_inc(x_out, 16)
            with sp.Fori(0, NB) as b:
                sp.dma_start(X, xT[:, bass.ds(b * TOK, TOK)]).then_inc(x_in, 16)
                sp.wait_ge(ln_dve, (b + 1) * 16)
                sp.dma_start(X, xT[:, bass.ds(b * TOK, TOK)]).then_inc(x_in, 16)
                sp.wait_ge(res, (b + 1) * NCH)
                sp.dma_start(x1[:, bass.ds(b * TOK, TOK)], Z[:, :]).then_inc(x_out, 16)
            sp.wait_ge(x_out, (NB + 1) * 16)

        def conv(pe, src, taps, bank, row):
            for t in range(9):
                ins = nc.tensor.matmul(PS[:, bank, :], taps[:, t * P:(t + 1) * P],
                                       src[:, bass.ds(row + t // 3, ROWS), t % 3:t % 3 + IMG],
                                       start=(t == 0), stop=(t == 8))
            return ins

        @block.tensor
        def _(pe):
            pe.wait_ge(loaded, 32)
            for k in range(NDIR):
                nc.tensor.matmul(PS[:, 0, k * P:(k + 1) * P], w("xp_dt", k * P, P)[0:4, :],
                                 w("dt_w", k * P, P)[0:4, :], start=True, stop=True)
            nc.tensor.matmul(PS[:, 1, 0:P], w("out_proj")[0:HALF, :], w("cv")[0:HALF, :],
                             start=True, stop=True).then_inc(setup_pe, 1)
            pe.wait_ge(setup_act, 3)

            with pe.Fori(0, NB) as b:
                def ring(stage, j, u):
                    pe.wait_ge(ev, b * NGA + stage * NCH + j * 2 + u + 1)

                def stage_done(stage):
                    pe.wait_ge(ev, b * NGA + stage * NCH + 2)

                with pe.Fori(0, NCH // 2) as j:
                    for u in range(2):
                        pe.wait_ge(x_in, b * 32 + 16)
                        ring(0, j, u)
                        nc.tensor.matmul(PS[:, u, :], w("cv12"), X[:, bass.ds((j * 2 + u) * CH, CH)],
                                         start=True, stop=True).then_inc(mm, 1)
                with pe.Fori(0, NCH // 2) as j:
                    for u in range(2):
                        pe.wait_ge(bn0_done, (b + 1) * NCH)
                        ring(1, j, u)
                        conv(pe, P1, w("c1"), u, (j * 2 + u) * ROWS).then_inc(mm, 1)
                with pe.Fori(0, NCH // 2) as j:
                    for u in range(2):
                        stage_done(2)
                        ring(2, j, u)
                        conv(pe, P2, w("c2"), u, (j * 2 + u) * ROWS).then_inc(mm, 1)
                with pe.Fori(0, NCH // 2) as j:
                    for u in range(2):
                        stage_done(3)
                        ring(3, j, u)
                        nc.tensor.matmul(PS[:, u, :], w("c3"), C2[:, bass.ds((j * 2 + u) * CH, CH)],
                                         start=True, stop=True).then_inc(mm, 1)
                for stage, name in ((4, "in_xh"), (5, "in_z")):
                    with pe.Fori(0, NCH // 2) as j:
                        for u in range(2):
                            ring(stage, j, u)
                            nc.tensor.matmul(PS[:, u, :], w(name), AB[:, bass.ds((j * 2 + u) * CH, CH)],
                                             start=True, stop=True).then_inc(mm, 1)
                with pe.Fori(0, NCH // 2) as j:
                    for u in range(2):
                        pe.wait_ge(dwd_up, (b + 1) * 9)
                        ring(6, j, u)
                        conv(pe, PH, DWD, u, (j * 2 + u) * ROWS).then_inc(mm, 1)
                stage_done(7)
                pe.wait_ge(cols_done, (b + 1) * NCH)

                def delta_arg(k, at, n):
                    nc.tensor.matmul(PS[:, DT_BANK, :], WDT[:, k * P:(k + 1) * P],
                                     (XH if k % 2 == 0 else XC)[:, bass.ds(at, CH)],
                                     start=True, stop=True).then_inc(pd_up, 1)

                def b_and_c(k, at, n):
                    nc.tensor.matmul(PS[0:96, BC_BANK, :], w("bc", k * 96, 96),
                                     (XH if k % 2 == 0 else XC)[:, bass.ds(at, CH)],
                                     start=True, stop=True).then_inc(pb_up, 1)

                def bcast_b(k, n, i):
                    pe.wait_ge(b_sb, b * (UNITS + LEAD_B) + i + 1)
                    nc.tensor.matmul(PS[:, B_BANK + n % 2, :], SEL[:, n * P:(n + 1) * P],
                                     S[:, k % 2, :], start=True, stop=True).then_inc(b_up, 1)

                def bcast_c(k, n, i):
                    pe.wait_ge(hc_up, b * UNITS + i + 1)
                    nc.tensor.matmul(PS[:, C_BANK + n % 2, :], SEL[:, (NST + n) * P:(NST + n + 1) * P],
                                     S[:, k % 2, :], start=True, stop=True).then_inc(c_up, 1)

                def add_y(k, n, it, i):
                    if n == 0:
                        pe.wait_ge(y_out, it + 1)
                    pe.wait_ge(hc_up, b * UNITS + i + 1 + 2)
                    nc.tensor.matmul(PS[:, Y_BANK + k % 2, :], w("ident"), HC[:, n % RING, :],
                                     start=(n == 0), stop=(n == NST - 1)).then_inc(y_up, 1)

                delta_arg(0, 0, b * PREPS + 1)
                b_and_c(0, 0, b * PREPS + 1)
                for n in range(LEAD_B):
                    pe.wait_ge(s_lo, b * PREPS + 1)
                    bcast_b(0, n, n)
                bcast_c(0, 0, 0)
                with pe.Fori(0, NCH) as c:
                    for k in range(NDIR):
                        it = (b * NCH + c) * NDIR + k
                        i0 = (c * NDIR + k) * NST
                        prep = b * PREPS + c * NDIR + k + 2
                        kn, cn = (k + 1) % NDIR, (c if k < NDIR - 1 else c + 1)
                        nxt = (cn if kn < 2 else (NCH - 1) - cn) * CH
                        for n in range(NST):
                            nb, nc_ = n + LEAD_B, n + LEAD_C
                            if nb == NST:
                                pe.wait_ge(s_lo, prep)
                            bcast_b(k if nb < NST else kn, nb % NST, i0 + nb)
                            if n == 0:
                                pe.wait_ge(ab_up, prep - 1)
                                pe.wait_ge(relu_up, prep - 1)
                                pe.wait_ge(r_up, prep - 1)
                            if n >= 2:
                                add_y(k, n - 2, it, i0 + n - 2)
                            elif k > 0:
                                add_y(k - 1, NST + n - 2, it - 1, i0 + n - 2)
                            bcast_c(k if nc_ < NST else kn, nc_ % NST, i0 + nc_)
                            if n == 1:
                                delta_arg(kn, nxt, prep)
                            if n == 4:
                                b_and_c(kn, nxt, prep)
                    for n in (NST - 2, NST - 1):
                        add_y(k, n, it, i0 + n)

                for g in range(2):
                    for i in range(4):
                        pe.wait_ge(b_sb, (b + 1) * (UNITS + LEAD_B) + 2)
                        pe.wait_ge(ln_dve, b * 16 + g * 8 + i + 1)
                        nc.tensor.matmul(PS[:, i, :], w("center"), YA[:, (4 * g + i) * CH:(4 * g + i + 1) * CH],
                                         start=True, stop=True).then_inc(ln_pe, 1)
                    for i in range(4):
                        pe.wait_ge(ln_act, b * 24 + g * 12 + i + 1)
                        pe.wait_ge(r_up, (b + 1) * PREPS)
                        nc.tensor.matmul(PS[:, 4 + i, :], w("ones"), H[:, i * CH:(i + 1) * CH],
                                         start=True, stop=True).then_inc(ln_pe, 1)
                with pe.Fori(0, NCH // 2) as j:
                    for u in range(2):
                        pe.wait_ge(ln_dve, (b + 1) * 16)
                        ring(7, j, u)
                        nc.tensor.matmul(PS[:, u, :], WCV[:, :], YA[:, bass.ds((j * 2 + u) * CH, CH)],
                                         start=True, stop=True).then_inc(mm, 1)
                with pe.Fori(0, NCH // 2) as j:
                    for u in range(2):
                        stage_done(8)
                        ring(8, j, u)
                        nc.tensor.matmul(PS[:, u, :], w("cv3"), LX[:, bass.ds((j * 2 + u) * CH, CH)],
                                         start=True, stop=True).then_inc(mm, 1)
                stage_done(9)

        @block.scalar
        def _(act):
            act.wait_ge(loaded, 32)
            act.sem_inc(ev, 2)
            act.sem_inc(b_sb, 2)
            act.wait_ge(setup_pe, 1)
            nc.scalar.copy(WDT[:, :], PS[:, 0, :]).then_inc(setup_act, 1)
            nc.scalar.copy(WCV[:, :], PS[:, 1, 0:P]).then_inc(setup_act, 1)
            nc.scalar.activation(A[:, :], w("A_logs"), ACT.Exp).then_inc(setup_act, 1)
            act.wait_ge(setup_dve, 3)
            with act.Fori(0, NB) as b:
                def take(stage, body):
                    with act.Fori(0, NCH // 2) as j:
                        for u in range(2):
                            act.wait_ge(mm, b * NGA + stage * NCH + j * 2 + u + 1)
                            body(j * 2 + u, PS[:, u, :]).then_inc(ev, 1)

                def rows(ap):
                    return ap.rearrange("p (h w) -> p h w", w=IMG)

                def inner(buf, j):
                    return buf[:, bass.ds(j * ROWS + 1, ROWS), 1:1 + IMG]

                nc.scalar.preload_act_table_set(SILU)
                take(0, lambda j, ps: nc.scalar.activation(
                    AB[:, bass.ds(j * CH, CH)], ps, ACT.Silu, scale=w("cv12_g"), bias=w("cv12_b")))
                act.wait_ge(padded, (b + 1) * 3)
                take(1, lambda j, ps: nc.scalar.activation(
                    inner(P2, j), rows(ps), ACT.Relu, scale=w("bn1_g"), bias=VEC[:, 0:1]))
                take(2, lambda j, ps: nc.scalar.activation(
                    C2[:, bass.ds(j * CH, CH)], ps, ACT.Relu, scale=w("bn2_g"), bias=VEC[:, 1:2]))
                take(3, lambda j, ps: nc.scalar.activation(
                    LX[0:HALF, bass.ds(j * CH, CH)], ps[0:HALF, :], ACT.Relu, bias=w("c3_b")[0:HALF, :]))
                take(4, lambda j, ps: nc.scalar.copy(inner(PH, j), rows(ps)))
                act.wait_ge(x_out, (b + 1) * 16)
                take(5, lambda j, ps: nc.scalar.activation(Z[:, bass.ds(j * CH, CH)], ps, ACT.Silu))
                take(6, lambda j, ps: nc.scalar.activation(
                    XH[:, bass.ds(j * CH, CH)], ps, ACT.Silu, bias=w("dw_b")))

                def absolute(k, n):
                    act.wait_ge(pd_up, n)
                    act.wait_ge(dl_up, n)
                    nc.scalar.activation(TE[:, :], PS[:, DT_BANK, :], ACT.Abs,
                                         bias=w("dt_b", k, 1)).then_inc(ab_up, 1)

                def exponential(k, n):
                    act.wait_ge(ab_up, n)
                    nc.scalar.activation(TE[:, :], TE[:, :], ACT.Exp, scale=-1.0).then_inc(e_up, 1)

                def one_plus(k, n):
                    act.wait_ge(e_up, n)
                    nc.scalar.activation(TU[:, :], TE[:, :], ACT.Identity, bias=w("one")).then_inc(u_up, 1)

                def minus_one(k, n):
                    act.wait_ge(u_up, n)
                    nc.scalar.activation(TP[:, :], TU[:, :], ACT.Identity, bias=w("minus_one")).then_inc(t_up, 1)

                def logarithm(k, n):
                    act.wait_ge(u_up, n)
                    nc.scalar.activation(TL[:, :], TU[:, :], ACT.Ln).then_inc(ln_up, 1)

                def high(k, n):
                    act.wait_ge(pb_up, n)
                    nc.scalar.copy(S[:, k % 2, :], PS[0:96, BC_BANK, :]).then_inc(s_hi, 1)

                def middle(k, n):
                    act.wait_ge(r_up, n)
                    nc.scalar.copy(S[0:HALF, k % 2, :], RS).then_inc(s_mid, 1)

                def take_b(k, n, i):
                    act.wait_ge(b_up, b * (UNITS + LEAD_B) + i + 1)
                    act.wait_ge(dbu_up, b * UNITS + i + 1)
                    nc.scalar.copy(BS[:, n % RING, :], PS[:, B_BANK + n % 2, :]).then_inc(b_sb, 1)

                def exp_a(k, n, i):
                    act.wait_ge(scanned, b * UNITS + i + 1)
                    nc.scalar.activation(DA[:, n % ERING * CH:(n % ERING + 1) * CH], DL[:, k % 2, :], ACT.Exp,
                                         scale=A[:, k * NST + n:k * NST + n + 1]).then_inc(da_up, 1)

                nc.scalar.preload_act_table_set(EXP_LN)
                first = b * PREPS + 1
                absolute(0, first)
                exponential(0, first)
                one_plus(0, first)
                minus_one(0, first)
                high(0, first)
                logarithm(0, first)
                middle(0, first)
                for n in range(LEAD_B):
                    take_b(0, n, n)
                for n in range(LEAD_E):
                    act.wait_ge(dl_up, first + 1)
                    exp_a(0, n, n)
                with act.Fori(0, NCH) as c:
                    for k in range(NDIR):
                        i0 = (c * NDIR + k) * NST
                        prep = b * PREPS + c * NDIR + k + 2
                        kn = (k + 1) % NDIR
                        for n in range(NST):
                            nb = n + LEAD_B
                            take_b(k if nb < NST else kn, nb % NST, i0 + nb)
                            ne = n + LEAD_E
                            if ne == NST:
                                act.wait_ge(dl_up, prep + 1)
                            exp_a(k if ne < NST else kn, ne % NST, i0 + ne)
                            for at, work in ((2, absolute), (3, exponential), (4, one_plus), (5, minus_one),
                                             (5, high), (6, logarithm), (7, middle)):
                                if n == at:
                                    work(kn, prep)

                for g in range(2):
                    for i in range(4):
                        act.wait_ge(ln_pe, b * 16 + g * 8 + i + 1)
                        nc.scalar.activation(H[:, i * CH:(i + 1) * CH], PS[:, i, :],
                                             ACT.Square).then_inc(ln_act, 1)
                    for i in range(4):
                        act.wait_ge(ln_pe, b * 16 + g * 8 + 4 + i + 1)
                        nc.scalar.activation(H[:, (4 + i) * CH:(5 + i) * CH], PS[:, 4 + i, :], ACT.Ln,
                                             bias=w("eps")).then_inc(ln_act, 1)
                    for i in range(4):
                        act.wait_ge(ln_act, b * 24 + g * 12 + 4 + i + 1)
                        nc.scalar.activation(H[:, (4 + i) * CH:(5 + i) * CH], H[:, (4 + i) * CH:(5 + i) * CH],
                                             ACT.Exp, scale=-0.5).then_inc(ln_act, 1)
                nc.scalar.preload_act_table_set(SILU)
                take(7, lambda j, ps: nc.scalar.activation(
                    LX[HALF:P, bass.ds(j * CH, CH)], ps[HALF:P, :], ACT.Silu,
                    scale=w("cv_g")[HALF:P, :], bias=w("cv_b")[HALF:P, :]))
                take(8, lambda j, ps: nc.scalar.activation(
                    Z[:, bass.ds(j * CH, CH)], ps, ACT.Silu, scale=w("cv3_g"), bias=w("cv3_b")))

        @block.gpsimd
        def _(pool):
            pool.sem_inc(dbu_up, RING)
            pool.sem_inc(dl_up, 1)
            pool.wait_ge(loaded, 32)
            with pool.Fori(0, NB) as b:
                def lost(n):
                    pool.wait_ge(t_up, n)
                    nc.gpsimd.tensor_tensor(TP[:, :], TE[:, :], TP[:, :], ALU.subtract).then_inc(lp, 1)

                def plus_relu(n):
                    pool.wait_ge(lp, (n - 1) * 2 + 1)
                    pool.wait_ge(relu_up, n)
                    nc.gpsimd.tensor_tensor(TP[:, :], TP[:, :], TR[:, :], ALU.add).then_inc(lp, 1)

                def delta(k, n):
                    pool.wait_ge(ln_up, n)
                    pool.wait_ge(lp, n * 2)
                    nc.gpsimd.tensor_tensor(DL[:, k % 2, :], TP[:, :], TL[:, :], ALU.add).then_inc(dl_up, 1)

                def delta_u(k, at, n):
                    pool.wait_ge(dl_up, n + 1)
                    nc.gpsimd.tensor_tensor(PNIL[:, :], w("eps"), w("eps"), ALU.mult)
                    nc.gpsimd.tensor_tensor(DU[:, :], DL[:, k % 2, :],
                                            (XH if k % 2 == 0 else XC)[:, bass.ds(at, CH)],
                                            ALU.mult).then_inc(du_up, 1)

                first = b * PREPS + 1
                lost(first)
                plus_relu(first)
                delta(0, first)
                delta_u(0, 0, first)
                with pool.Fori(0, NCH) as c:
                    for k in range(NDIR):
                        i0 = (c * NDIR + k) * NST
                        prep = b * PREPS + c * NDIR + k + 2
                        kn, cn = (k + 1) % NDIR, (c if k < NDIR - 1 else c + 1)
                        nxt = (cn if kn < 2 else (NCH - 1) - cn) * CH
                        pool.wait_ge(du_up, prep - 1)
                        for n in range(NST):
                            pool.wait_ge(b_sb, b * (UNITS + LEAD_B) + i0 + n + 1 + 2)
                            pool.wait_ge(scanned, b * UNITS + i0 + n + 1 - RING + ERING)
                            nc.gpsimd.tensor_tensor(DBU[:, n % RING, :], BS[:, n % RING, :], DU[:, :],
                                                    ALU.mult).then_inc(dbu_up, 1)
                            if n == 9:
                                lost(prep)
                            if n == 10:
                                plus_relu(prep)
                            if n == 11:
                                delta(kn, prep)
                        pool.wait_ge(dbu_up, b * UNITS + i0 + NST + RING)
                        delta_u(kn, nxt, prep)

        @block.vector
        def _(dve):
            dve.wait_ge(loaded, 32)
            dve.sem_inc(scanned, ERING)
            dve.sem_inc(hc_up, 2)
            dve.sem_inc(y_up, RING)
            dve.sem_inc(y_out, 2)
            nc.vector.scalar_tensor_tensor(VEC[:, 0:1], w("c1_b"), w("bn1_g"), w("bn1_b"), ALU.mult,
                                           ALU.add).then_inc(setup_dve, 1)
            nc.vector.scalar_tensor_tensor(VEC[:, 1:2], w("c2_b"), w("bn2_g"), w("bn2_b"), ALU.mult,
                                           ALU.add).then_inc(setup_dve, 1)
            dve.wait_ge(setup_act, 3)
            nc.vector.tensor_scalar(A[:, :], A[:, :], -1.0, None, ALU.mult).then_inc(setup_dve, 1)
            nc.vector.tensor_reduce(VEC[:, 2:3], w("Ds"), AX_X, ALU.add).then_inc(setup_dve, 1)
            nc.vector.memset(XH[:, TOK:TOK + CH], 0.0).then_inc(setup_dve, 1)
            dve.wait_ge(setup_dve, 5)

            with dve.Fori(0, NB) as b:
                nc.vector.memset(YA[:, :], 0.0).then_inc(padded, 1)
                nc.vector.memset(YB[:, :], 0.0).then_inc(padded, 1)
                nc.vector.memset(HL[:, :], 0.0).then_inc(hl_up, 1)
                with dve.Fori(0, NCH) as j:
                    dve.wait_ge(padded, b * 3 + 2)
                    dve.wait_ge(ev, b * NGA + j + 1 + 2)
                    nc.vector.tensor_scalar(P1[:, bass.ds(j * ROWS + 1, ROWS), 1:1 + IMG],
                                            AB[:, bass.ds(j * CH, CH)].rearrange("p (h w) -> p h w", w=IMG),
                                            w("bn0_g"), w("bn0_b"), ALU.mult, ALU.add).then_inc(bn0_done, 1)
                for t in range(9):
                    nc.vector.tensor_scalar(DWD[:, t * P:(t + 1) * P], w("ident"), w("dw", t, 1), None,
                                            ALU.mult).then_inc(dwd_up, 1)
                nc.vector.memset(H[:, :], 0.0).then_inc(padded, 1)
                with dve.Fori(0, NCH) as j:
                    dve.wait_ge(mm, b * NGA + 6 * NCH)
                    dve.wait_ge(ev, b * NGA + 6 * NCH + j + 1 + 2)
                    nc.vector.tensor_copy(XCv[:, bass.ds(j * ROWS, ROWS), :],
                                          XH[:, bass.ds(j * CH, CH)].rearrange("p (h w) -> p h w", w=IMG)
                                          ).then_inc(cols_done, 1)
                nc.vector.tensor_scalar(YA[:, 0:TOK], XH[:, 0:TOK], VEC[:, 2:3], None,
                                        ALU.mult).then_inc(y_init, 1)
                nc.vector.memset(YB[:, 0:TOK], 0.0).then_inc(y_init, 1)
                dve.wait_ge(y_init, (b + 1) * 2)
                dve.wait_ge(hl_up, b * (NCH * NDIR * 2 + 1) + 1)

                def relu(k, n):
                    dve.wait_ge(ab_up, n)
                    nc.vector.tensor_scalar(TR[:, :], PS[:, DT_BANK, :], w("dt_b", k, 1), 0.0, ALU.add,
                                            ALU.max).then_inc(relu_up, 1)

                def rest(k, n):
                    dve.wait_ge(pb_up, n)
                    dve.wait_ge(s_hi, n)
                    nc.vector.tensor_tensor(RS, PS[0:HALF, BC_BANK, :], S[0:HALF, k % 2, :],
                                            ALU.subtract).then_inc(r_up, 1)

                def low(k, n):
                    dve.wait_ge(s_mid, n)
                    dve.wait_ge(r_up, n)
                    nc.vector.tensor_tensor(S[0:32, k % 2, :], RS[0:32], S[0:32, k % 2, :],
                                            ALU.subtract).then_inc(s_lo, 1)

                relu(0, b * PREPS + 1)
                rest(0, b * PREPS + 1)
                low(0, b * PREPS + 1)
                with dve.Fori(0, NCH) as c:
                    for k in range(NDIR):
                        it = (b * NCH + c) * NDIR + k
                        i0 = (c * NDIR + k) * NST
                        u0 = it * NST
                        prep = b * PREPS + c * NDIR + k + 2
                        kn = (k + 1) % NDIR
                        turn = -1 if k >= 2 else 1
                        end = 0 if k >= 2 else CH - 1

                        def times_c(n):
                            dve.wait_ge(scanned, u0 + n + 1 + ERING)
                            dve.wait_ge(c_up, b * (UNITS + LEAD_C) + i0 + n + 1)
                            dve.wait_ge(y_up, u0 + n + 1)
                            nc.vector.tensor_tensor(HC[:, n % RING, :], H[:, n % HRING * CH:(n % HRING + 1) * CH],
                                                    PS[:, C_BANK + n % 2, :], ALU.mult).then_inc(hc_up, 1)

                        def take_y(k, it):
                            y_sum = YA if k % 2 == 0 else YB
                            at = (c if k < 2 else (NCH - 1) - c) * CH
                            dve.wait_ge(y_out, it + 2)
                            dve.wait_ge(y_up, (it + 1) * NST + RING)
                            nc.vector.memset(NIL[:, :], 0.0)
                            nc.vector.tensor_tensor(y_sum[:, bass.ds(at, CH)], y_sum[:, bass.ds(at, CH)],
                                                    PS[:, Y_BANK + k % 2, :], ALU.add).then_inc(y_out, 1)

                        for n in range(NST):
                            if n == 8:
                                dve.wait_ge(hl_up, it * 2 + b + 2)
                            dve.wait_ge(da_up, b * (UNITS + LEAD_E) + i0 + n + 1)
                            dve.wait_ge(dbu_up, u0 + n + 1 + RING)
                            nc.vector.tensor_tensor_scan(
                                H[:, n % HRING * CH:(n % HRING + 1) * CH][:, ::turn], DA[:, n % ERING * CH:(n % ERING + 1) * CH][:, ::turn],
                                DBU[:, n % RING, :][:, ::turn], HL[:, k * NST + n:k * NST + n + 1],
                                ALU.mult, ALU.add).then_inc(scanned, 1)
                            if n >= 1:
                                times_c(n - 1)
                            if n % HRING == HRING - 1:
                                dve.wait_ge(scanned, u0 + n + 1 + ERING)
                                nc.vector.tensor_copy(
                                    HL[:, k * NST + n + 1 - HRING:k * NST + n + 1],
                                    H[:, 0:HRING * CH].rearrange("p (n t) -> p n t", n=HRING)[:, :, end]
                                ).then_inc(hl_up, 1)
                            if n == 4:
                                relu(kn, prep)
                            if n == 3 and k > 0:
                                take_y(k - 1, it - 1)
                            if n == 7:
                                rest(kn, prep)
                            if n == 11:
                                low(kn, prep)
                        times_c(NST - 1)
                        dve.wait_ge(hl_up, it * 2 + b + 3)
                        if k == NDIR - 1:
                            take_y(k, it)
                            dve.wait_ge(y_out, it + 3)

                for g in range(2):
                    for i in range(4):
                        j = 4 * g + i
                        yj = YA[:, j * CH:(j + 1) * CH]
                        nc.vector.tensor_tensor(yj.rearrange("p (h w) -> p h w", w=IMG),
                                                yj.rearrange("p (h w) -> p h w", w=IMG),
                                                YBv[:, j * ROWS:(j + 1) * ROWS, :], ALU.add).then_inc(ln_dve, 1)
                    for i in range(4):
                        j = 4 * g + i
                        yj = YA[:, j * CH:(j + 1) * CH]
                        dve.wait_ge(ln_act, b * 24 + g * 12 + 8 + i + 1)
                        dve.wait_ge(ln_pe, b * 16 + g * 8 + 4 + i + 1)
                        nc.vector.scalar_tensor_tensor(H[:, (4 + i) * CH:(5 + i) * CH], PS[:, i, :], w("ln_g"),
                                                       H[:, (4 + i) * CH:(5 + i) * CH], ALU.mult,
                                                       ALU.mult).then_inc(ln_w, 1)
                        dve.wait_ge(ln_w, b * 8 + g * 4 + i + 1)
                        nc.vector.scalar_tensor_tensor(yj, H[:, (4 + i) * CH:(5 + i) * CH], w("ln_b"),
                                                       Z[:, j * CH:(j + 1) * CH], ALU.add,
                                                       ALU.mult).then_inc(ln_dve, 1)
                with dve.Fori(0, NCH) as j:
                    dve.wait_ge(x_in, (b + 1) * 32)
                    dve.wait_ge(ev, b * NGA + 8 * NCH + j + 1 + 2)
                    nc.vector.tensor_tensor(Z[:, bass.ds(j * CH, CH)], X[:, bass.ds(j * CH, CH)],
                                            Z[:, bass.ds(j * CH, CH)], ALU.add).then_inc(res, 1)


class Norm:

    def __init__(self, nc, sem, PS, SQ, RST, center, ones, eps):
        self.nc, self.PS, self.SQ, self.RST = nc, PS, SQ, RST
        self.center, self.ones, self.eps = center, ones, eps
        self.centred, self.squared, self.meaned = sem("n_centred"), sem("n_squared"), sem("n_meaned")
        self.logged, self.scaled, self.out = sem("n_logged"), sem("n_scaled"), sem("n_out")

    def begin(self, dve):
        dve.sem_inc(self.out, 4)

    def pe(self, pe, n0, src, ready):
        for i in range(4):
            ready(i)
            pe.wait_ge(self.out, n0 + i + 1)
            self.nc.tensor.matmul(self.PS[:, i, :], self.center, src(i), start=True,
                                  stop=True).then_inc(self.centred, 1)
        for i in range(4):
            pe.wait_ge(self.squared, n0 + i + 1)
            self.nc.tensor.matmul(self.PS[:, 4 + i, :], self.ones, self.SQ[:, i, :], start=True,
                                  stop=True).then_inc(self.meaned, 1)

    def act(self, act, n0):
        for i in range(4):
            act.wait_ge(self.centred, n0 + i + 1)
            self.nc.scalar.activation(self.SQ[:, i, :], self.PS[:, i, :], ACT.Square).then_inc(self.squared, 1)
        for i in range(4):
            act.wait_ge(self.meaned, n0 + i + 1)
            self.nc.scalar.activation(self.RST[:, i, :], self.PS[:, 4 + i, :], ACT.Ln,
                                      bias=self.eps).then_inc(self.logged, 1)
            act.wait_ge(self.logged, n0 + i + 1)
            self.nc.scalar.activation(self.RST[:, i, :], self.RST[:, i, :], ACT.Exp,
                                      scale=-0.5).then_inc(self.scaled, 1)

    def dve(self, dve, n0, dst, gain=None):
        for i in range(4):
            dve.wait_ge(self.scaled, n0 + i + 1)
            if gain is None:
                self.nc.vector.tensor_tensor(dst(i), self.PS[:, i, :], self.RST[:, i, :],
                                             ALU.mult).then_inc(self.out, 1)
            else:
                self.nc.vector.scalar_tensor_tensor(dst(i), self.PS[:, i, :], gain, self.RST[:, i, :],
                                                    ALU.mult, ALU.mult).then_inc(self.out, 1)


def layer1(nc, x1, pack, XR):
    with ExitStack() as ctx:
        def sb(name, shape, dt=F32):
            return ctx.enter_context(nc.sbuf_tensor("l1_" + name, shape, dt))

        sem = semaphores(nc, ctx, "l1_")

        where, width = places(PACK1)
        W = sb("W", [P, width])

        def w(name, a=0, n=None):
            at, size = where[name]
            return W[:, at + a:at + (size if n is None else a + n)]

        PAIR = 2 * TOK
        G = sb("G", [P, IMG, 2, IMG])
        AB = sb("AB", [P, 2, IMG, P])
        SQ = sb("SQ", [P, 4, CH])
        RST = sb("RST", [P, 4, CH])
        OT = sb("OT", [P, 4, CH])
        T = sb("T", [P, 2, CH])
        SG = sb("SG", [P, 2, 2 * P])
        ST = sb("ST", [P, NCH, 6])
        MV = sb("MV", [P, NB, 2])
        GM = sb("GM", [P, NB, 2])
        PS = ctx.enter_context(nc.psum_tensor("l1_PS", [P, 8, CH], F32))

        x_in = [sem("x_in%d" % b) for b in range(NB)]
        loaded = sem("loaded")
        stats, group, gstat, glog = sem("stats"), sem("group"), sem("gstat"), sem("glog")
        gn_up = sem("gn_up")
        zn_up = sem("zn_up")
        ab_mm, ab_t, ab_s, ab_up = sem("ab_mm"), sem("ab_t"), sem("ab_s"), sem("ab_up")
        g_mm, g_up = sem("g_mm"), sem("g_up")
        o_mm = sem("o_mm")
        o_act, o_dve = sem("o_act"), sem("o_dve")
        t_up, t_out = sem("t_up"), sem("t_out")
        on_up, wo_mm, y_gate, y_up = sem("on_up"), sem("wo_mm"), sem("y_gate"), sem("y_up")
        norm = Norm(nc, sem, PS, SQ, RST, w("center"), w("ones"), w("eps"))

        def chunk(q):
            return G[:, :, :, :].rearrange("p i m k -> p (i m k)")[:, bass.ds(q * CH, CH)]

        NCOL = P // 8
        block = ctx.enter_context(nc.Block())

        @block.sync
        def _(sp):
            sp.dma_start(W[:, :], pack).then_inc(loaded, 16)
            if x1 is not None:
                for b in range(NB):
                    sp.dma_start(XR[:, b * TOK:(b + 1) * TOK], x1[:, b * TOK:(b + 1) * TOK]).then_inc(x_in[b], 16)

        @block.tensor
        def _(pe):
            pe.wait_ge(loaded, 16)
            pe.wait_ge(stats, NB * (NCH + 1) + 2)
            nc.tensor.matmul(PS[:, 0, 0:2 * NB], w("group4"), MV[:, :, :], start=True,
                             stop=True).then_inc(group, 1)
            for pr in range(2):
                pe.wait_ge(gn_up, 2 * (pr + 1))
                with pe.Fori(0, 4) as g:
                    norm.pe(pe, pr * 32 + g * 4, lambda i: chunk(g * 4 + i), lambda i: None)
                pe.wait_ge(zn_up, (pr + 1) * 16)
                for i in range(IMG):
                    pe.wait_ge(ab_t, pr * IMG + i + 1)
                    nc.tensor.matmul(PS[:, i % 2, :], G[:, i, :, :], w("ab"),
                                     start=True, stop=True).then_inc(ab_mm, 1)
                    if i % 4 == 3:
                        q = i // 4
                        pe.wait_ge(g_up, pr * 16 + q + 1)
                        nc.tensor.matmul(PS[:, 2 + q % 2, :], w("g"), chunk(q), start=True,
                                         stop=True).then_inc(g_mm, 1)
                pe.wait_ge(ab_up, (pr + 1) * IMG)
                for c8 in range(NCOL):
                    pe.wait_ge(o_act if c8 % 2 == 0 else o_dve, pr * (NCOL // 2) + c8 // 2 + 1)
                    for c in range(8):
                        for m in range(2):
                            s = slice(m * HALF, (m + 1) * HALF)
                            ins = nc.tensor.matmul(PS[s, 4 + c8 % 2, c * IMG:(c + 1) * IMG],
                                                   AB[s, 0, :, c8 * 8 + c], AB[s, 1, :, c8 * 8 + c],
                                                   start=True, stop=True)
                    ins.then_inc(o_mm, 1)
                pe.wait_ge(o_act, (pr + 1) * (NCOL // 2) + 1)
                pe.wait_ge(o_dve, (pr + 1) * (NCOL // 2) + 1)
                for g in range(4):
                    n0 = pr * 16 + g * 4
                    for i in range(4):
                        pe.wait_ge(y_gate, n0 + i + 1)
                        for j in range(4):
                            ins = nc.tensor.transpose(PS[:, 4 + i, j * P:(j + 1) * P],
                                                      AB[:, 0, (g * 4 + i) * 4 + j, :], w("ident"))
                        ins.then_inc(t_up, 1)
                    norm.pe(pe, pr * 32 + 16 + g * 4, lambda i: OT[:, i, :],
                            lambda i: pe.wait_ge(t_out, n0 + i + 1))
                    for i in range(4):
                        pe.wait_ge(on_up, n0 + i + 1)
                        nc.tensor.matmul(PS[:, 4 + i, :], w("o"), OT[:, i, :], start=True,
                                         stop=True).then_inc(wo_mm, 1)

        @block.scalar
        def _(act):
            act.wait_ge(loaded, 16)
            act.sem_inc(g_up, 2)
            act.sem_inc(o_act, 1)
            act.wait_ge(gstat, 2)
            nc.scalar.preload_act_table_set(EXP_LN)
            nc.scalar.activation(GM[:, :, 1], GM[:, :, 1], ACT.Ln, bias=w("eps")).then_inc(glog, 1)
            act.wait_ge(glog, 1)
            nc.scalar.activation(GM[:, :, 1], GM[:, :, 1], ACT.Exp, scale=-0.5).then_inc(glog, 1)
            with act.Fori(0, 2) as pr:
                nc.scalar.preload_act_table_set(EXP_LN)
                with act.Fori(0, 4) as g:
                    norm.act(act, pr * 32 + g * 4)
                for i in range(IMG):
                    act.wait_ge(ab_t, pr * IMG + i + 1 + 2)
                    act.wait_ge(ab_up, pr * IMG + i + 1 - 2) if i >= 2 else None
                    nc.scalar.activation(SG[:, i % 2, :], T[:, i % 2, 2 * P:], ACT.Sigmoid).then_inc(ab_s, 1)
                    if i % 4 == 3:
                        q = i // 4
                        act.wait_ge(g_mm, pr * 16 + q + 1)
                        nc.scalar.activation(chunk(q), PS[:, 2 + q % 2, :], ACT.Sigmoid, bias=w("bg")).then_inc(g_up, 1)
                for c8 in range(0, NCOL, 2):
                    act.wait_ge(o_mm, pr * NCOL + c8 + 1)
                    nc.scalar.copy(AB[:, 0, :, c8 * 8:(c8 + 1) * 8].rearrange("p j c -> p c j"),
                                   PS[:, 4 + c8 % 2, :].rearrange("p (c j) -> p c j", c=8)).then_inc(o_act, 1)
                nc.scalar.preload_act_table_set(EXP_LN)
                for g in range(4):
                    n0 = pr * 16 + g * 4
                    for i in range(4):
                        act.wait_ge(t_up, n0 + i + 1)
                        act.wait_ge(y_up, n0 + i + 1)
                        nc.scalar.copy(OT[:, i, :], PS[:, 4 + i, :]).then_inc(t_out, 1)
                    norm.act(act, pr * 32 + 16 + g * 4)

        @block.gpsimd
        def _(pool):
            with pool.Fori(0, 2) as pr:
                for i in range(IMG):
                    pool.wait_ge(ab_s, pr * IMG + i + 1)
                    nc.gpsimd.tensor_tensor(AB[:, :, i, :], T[:, i % 2, 0:2 * P].rearrange("p (m c) -> p m c", m=2),
                                            SG[:, i % 2, :].rearrange("p (m c) -> p m c", m=2),
                                            ALU.mult).then_inc(ab_up, 1)

        @block.vector
        def _(dve):
            norm.begin(dve)
            dve.sem_inc(ab_t, 2)
            dve.sem_inc(o_dve, 1)
            dve.sem_inc(y_gate, 4)
            dve.sem_inc(y_up, 4)
            for b in range(NB):
                if x1 is not None:
                    dve.wait_ge(x_in[b], 16)
                for j in range(NCH):
                    at = b * TOK + j * CH
                    if b:
                        dve.wait_ge(stats, b * (NCH + 1))
                    nc.vector.bn_stats(ST[:, j, :], XR[:, at:at + CH]).then_inc(stats, 1)
                dve.wait_ge(stats, b * (NCH + 1) + NCH)
                nc.vector.bn_aggr(MV[:, b, :], ST[:, :, :]).then_inc(stats, 1)
            dve.wait_ge(stats, NB * (NCH + 1))
            nc.vector.tensor_tensor(GM[:, :, 0], MV[:, :, 0], MV[:, :, 0], ALU.mult).then_inc(stats, 1)
            dve.wait_ge(stats, NB * (NCH + 1) + 1)
            nc.vector.tensor_tensor(MV[:, :, 1], MV[:, :, 1], GM[:, :, 0], ALU.add).then_inc(stats, 1)
            dve.wait_ge(group, 1)
            nc.vector.tensor_copy(GM[:, :, :], PS[:, 0, 0:2 * NB].rearrange("p (b s) -> p b s", s=2)
                                  ).then_inc(group, 1)
            dve.wait_ge(group, 2)
            nc.vector.tensor_tensor(MV[:, :, 0], GM[:, :, 0], GM[:, :, 0], ALU.mult).then_inc(gstat, 1)
            dve.wait_ge(gstat, 1)
            nc.vector.tensor_tensor(GM[:, :, 1], GM[:, :, 1], MV[:, :, 0], ALU.subtract).then_inc(gstat, 1)
            dve.wait_ge(glog, 2)
            nc.vector.scalar_tensor_tensor(GM[:, :, 0], GM[:, :, 0], -1.0, GM[:, :, 1], ALU.mult,
                                           ALU.mult).then_inc(gstat, 1)
            dve.wait_ge(gstat, 3)
            with dve.Fori(0, 2) as pr:
                nc.vector.tensor_copy(MV[:, 0:2, :], GM[:, bass.ds(pr * 2, 2), :]).then_inc(gstat, 1)
                dve.wait_ge(gstat, pr + 4)
                for m in range(2):
                    nc.vector.tensor_scalar(G[:, :, m, :], XR[:, bass.ds(pr * PAIR + m * TOK, TOK)]
                                            .rearrange("p (i k) -> p i k", k=IMG),
                                            MV[:, m, 1:2], MV[:, m, 0:1], ALU.mult, ALU.add).then_inc(gn_up, 1)
                with dve.Fori(0, 4) as g:
                    n0 = pr * 32 + g * 4
                    for i in range(4):
                        dve.wait_ge(norm.scaled, n0 + i + 1)
                        nc.vector.scalar_tensor_tensor(
                            chunk(g * 4 + i), PS[:, i, :], w("ln1_g"), RST[:, i, :], ALU.mult,
                            ALU.mult).then_inc(norm.out, 1)
                    for i in range(4):
                        dve.wait_ge(norm.out, n0 + i + 1 + 4)
                        nc.vector.tensor_scalar(chunk(g * 4 + i), chunk(g * 4 + i), w("ln1_b"), None,
                                                ALU.add).then_inc(zn_up, 1)
                for i in range(IMG):
                    dve.wait_ge(ab_mm, pr * IMG + i + 1)
                    dve.wait_ge(ab_up, pr * IMG + i + 1 - 2) if i >= 2 else None
                    nc.vector.tensor_tensor(T[:, i % 2, :], PS[:, i % 2, :], w("ab_b"), ALU.add).then_inc(ab_t, 1)
                for c8 in range(1, NCOL, 2):
                    dve.wait_ge(o_mm, pr * NCOL + c8 + 1)
                    nc.vector.tensor_copy(AB[:, 0, :, c8 * 8:(c8 + 1) * 8].rearrange("p j c -> p c j"),
                                          PS[:, 4 + c8 % 2, :].rearrange("p (c j) -> p c j", c=8)
                                          ).then_inc(o_dve, 1)
                for g in range(4):
                    n0 = pr * 16 + g * 4
                    norm.dve(dve, pr * 32 + 16 + g * 4, lambda i: OT[:, i, :], w("ln2_g"))
                    for i in range(4):
                        dve.wait_ge(norm.out, pr * 32 + 16 + g * 4 + i + 1 + 4)
                        nc.vector.tensor_scalar(OT[:, i, :], OT[:, i, :], w("ln2_b"), None,
                                                ALU.add).then_inc(on_up, 1)
                    for i in range(4):
                        q = g * 4 + i
                        dve.wait_ge(wo_mm, n0 + i + 1)
                        for m in range(2):
                            gate = G[:, :, m, q * 4:q * 4 + 4].rearrange("p i j -> p j i")
                            ins = nc.vector.scalar_tensor_tensor(
                                OT[:, i, :].rearrange("p (j m t) -> p j m t", j=4, m=2)[:, :, m, :],
                                PS[:, 4 + i, :].rearrange("p (j m t) -> p j m t", j=4, m=2)[:, :, m, :],
                                w("bo"), gate, ALU.add, ALU.mult)
                        ins.then_inc(y_gate, 1)
                    for i in range(4):
                        q = g * 4 + i
                        dve.wait_ge(y_gate, n0 + i + 1 + 4)
                        x = XR[:, bass.ds(pr * PAIR, PAIR)].rearrange("p (t j) -> p j t", j=IMG)[:, q * 4:q * 4 + 4, :]
                        nc.vector.tensor_tensor(x, x, OT[:, i, :].rearrange("p (j t) -> p j t", j=4),
                                                ALU.add).then_inc(y_up, 1)


def layer2_attn(nc, pack, XR):
    with ExitStack() as ctx:
        def sb(name, shape, dt=F32):
            return ctx.enter_context(nc.sbuf_tensor("l2a_" + name, shape, dt))

        sem = semaphores(nc, ctx, "l2a_")

        where, width = places(PACK2)
        W = sb("W", [P, width])

        def w(name, a=0, n=None):
            at, size = where[name]
            return W[:, at + a:at + (size if n is None else a + n)]

        XN = sb("XN", [P, TOK])
        K = sb("K", [P, TOK])
        QT = sb("QT", [P, TOK])
        SQ = sb("SQ", [P, 4, CH])
        RST = sb("RST", [P, 4, CH])
        KM = sb("KM", [P, NCH])
        KV = sb("KV", [P, 3])
        QS = sb("QS", [P, 2, 16, 32])
        MX, SM = sb("MX", [P, 2, 16]), sb("SM", [P, 2, 16])
        VS, KT = sb("VS", [P, 2, 4, P]), sb("KT", [P, 2, 4, P])
        CT, MT = sb("CT", [P, P]), sb("MT", [P, P])
        ST = sb("ST", [P, NCH, 6])
        MV, GV = sb("MV", [P, 2]), sb("GV", [P, 4])
        NIL = sb("NIL", [P, 1])
        PS = ctx.enter_context(nc.psum_tensor("l2a_PS", [P, 8, CH], F32))
        KT_BANK, QT_BANK, CTX_BANK, MISC_BANK = 4, 5, 6, 7

        loaded = sem("loaded")
        k_mm, k_out, k_max, k_top = sem("k_mm"), sem("k_out"), sem("k_max"), sem("k_top")
        k_exp, k_rec = sem("k_exp"), sem("k_rec")
        qv_mm, q_max, q_sub, q_exp = sem("qv_mm"), sem("q_max"), sem("q_sub"), sem("q_exp")
        q_sum, q_rec, q_up = sem("q_sum"), sem("q_rec"), sem("q_up")
        v_out, kt_mm, kt_out, qt_mm, qt_out = sem("v_out"), sem("kt_mm"), sem("kt_out"), sem("qt_mm"), sem("qt_out")
        c_mm, c_up, m_mm, m_up = sem("c_mm"), sem("c_up"), sem("m_mm"), sem("m_up")
        o_mm, o_out, o_stat = sem("o_mm"), sem("o_out"), sem("o_stat")
        gs_mm, gs, gs_log, o_norm, done = sem("gs_mm"), sem("gs"), sem("gs_log"), sem("o_norm"), sem("done")
        norm = Norm(nc, sem, PS, SQ, RST, w("center"), w("ones"), w("eps"))

        def c(j, buf=None):
            return (XN if buf is None else buf)[:, j * CH:(j + 1) * CH]

        def qv(g):
            return PS[:, (g % 2) * 2:(g % 2) * 2 + 2, :].rearrange("p a n -> p (a n)").rearrange(
                "p (t n) -> p t n", t=4)

        def heads(ap):
            return ap.rearrange("p t (h d) -> p t h d", d=32)

        def bc(small, g):
            return small[:, g % 2, :].rearrange("p (t h) -> p t h", t=4).unsqueeze(3).to_broadcast([P, 4, 4, 32])

        block = ctx.enter_context(nc.Block())

        @block.sync
        def _(sp):
            sp.dma_start(W[:, :], pack).then_inc(loaded, 16)

        @block.tensor
        def _(pe):
            pe.wait_ge(loaded, 16)
            with pe.Fori(0, NB) as b:
                for g in range(2):
                    norm.pe(pe, b * NCH + g * 4, lambda i: XR[:, bass.ds(b * TOK + (4 * g + i) * CH, CH)],
                            lambda i: pe.wait_ge(done, b + 1))
                for j in range(NCH):
                    pe.wait_ge(norm.out, b * NCH + NCH + 4)
                    pe.wait_ge(k_out, b * NCH + j + 1)
                    nc.tensor.matmul(PS[:, j % 4, :], w("k"), c(j), start=True, stop=True).then_inc(k_mm, 1)
                pe.wait_ge(k_out, b * NCH + NCH + 4)

                def context(g):
                    pe.wait_ge(q_up, b * NCH + g + 1)
                    pe.wait_ge(qt_out, b * NCH + g + 1)
                    for t in range(4):
                        ins = nc.tensor.transpose(PS[:, QT_BANK, t * P:(t + 1) * P],
                                                  QS[:, g % 2, 4 * t:4 * t + 4, :].rearrange("p h d -> p (h d)"),
                                                  w("ident"))
                    ins.then_inc(qt_mm, 1)
                    pe.wait_ge(v_out, b * NCH + g + 1 + 2)
                    pe.wait_ge(kt_out, b * NCH + g + 1 + 1)
                    for t in range(4):
                        ins = nc.tensor.matmul(PS[:, CTX_BANK, 0:P], KT[:, g % 2, t, :], VS[:, g % 2, t, :],
                                               start=(g == 0 and t == 0), stop=(g == NCH - 1 and t == 3))
                    ins.then_inc(c_mm, 1)

                for g in range(NCH):
                    pe.wait_ge(v_out, b * NCH + g + 1)
                    for t in range(4):
                        ins = nc.tensor.matmul(qv(g)[:, t, :], XN[:, (4 * g + t) * P:(4 * g + t + 1) * P],
                                               w("qv"), start=True, stop=True)
                    ins.then_inc(qv_mm, 1)
                    pe.wait_ge(k_exp, b + 1)
                    pe.wait_ge(kt_out, b * NCH + g + 1)
                    for t in range(4):
                        ins = nc.tensor.transpose(PS[:, KT_BANK, t * P:(t + 1) * P],
                                                  K[:, (4 * g + t) * P:(4 * g + t + 1) * P], w("ident"))
                    ins.then_inc(kt_mm, 1)
                    if g >= 1:
                        context(g - 1)
                context(NCH - 1)
                pe.wait_ge(c_up, b + 1)
                nc.tensor.matmul(PS[:, MISC_BANK, 0:P], CT[:, :], w("out"), start=True, stop=True).then_inc(m_mm, 1)
                pe.wait_ge(m_up, b + 1)
                pe.wait_ge(qt_out, (b + 1) * NCH + 1)
                for j in range(NCH):
                    pe.wait_ge(o_out, b * NCH + j + 1)
                    nc.tensor.matmul(PS[:, j % 4, :], MT[:, :], c(j, QT), start=True, stop=True).then_inc(o_mm, 1)
                pe.wait_ge(gs, b * 7 + 3)
                nc.tensor.matmul(PS[:, MISC_BANK, 0:2], w("ones"), MV[:, :], start=True,
                                 stop=True).then_inc(gs_mm, 1)

        @block.scalar
        def _(act):
            act.wait_ge(loaded, 16)
            act.sem_inc(k_out, 4)
            act.sem_inc(v_out, 2)
            act.sem_inc(kt_out, 1)
            act.sem_inc(o_out, 4)
            nc.scalar.preload_act_table_set(EXP_LN)
            with act.Fori(0, NB) as b:
                for g in range(2):
                    norm.act(act, b * NCH + g * 4)
                for j in range(NCH):
                    act.wait_ge(k_mm, b * NCH + j + 1)
                    nc.scalar.copy(c(j, K), PS[:, j % 4, :]).then_inc(k_out, 1)
                act.wait_ge(k_top, b + 1)
                nc.scalar.activation(K[:, :], K[:, :], ACT.Exp, bias=KV[:, 0:1],
                                     accum_out=KV[:, 1:2]).then_inc(k_exp, 1)
                for g in range(NCH):
                    act.wait_ge(q_sub, b * NCH + g + 1)
                    nc.scalar.activation(QS[:, g % 2, :, :], QS[:, g % 2, :, :], ACT.Exp).then_inc(q_exp, 1)
                    if g >= 2:
                        act.wait_ge(c_mm, b * NCH + g - 1)
                    nc.scalar.copy(VS[:, g % 2, :, :], qv(g)[:, :, P:2 * P]).then_inc(v_out, 1)
                    act.wait_ge(kt_mm, b * NCH + g + 1)
                    nc.scalar.copy(KT[:, g % 2, :, :], PS[:, KT_BANK, :].rearrange("p (t n) -> p t n", t=4)
                                   ).then_inc(kt_out, 1)
                for j in range(NCH):
                    act.wait_ge(o_mm, b * NCH + j + 1)
                    nc.scalar.activation(c(j, K), PS[:, j % 4, :], ACT.Identity, bias=w("b_out")).then_inc(o_out, 1)
                act.wait_ge(gs, b * 7 + 6)
                nc.scalar.activation(GV[:, 1:2], GV[:, 1:2], ACT.Ln, bias=w("eps")).then_inc(gs_log, 1)
                act.wait_ge(gs_log, b * 2 + 1)
                nc.scalar.activation(GV[:, 1:2], GV[:, 1:2], ACT.Exp, scale=-0.5).then_inc(gs_log, 1)

        @block.vector
        def _(dve):
            norm.begin(dve)
            dve.sem_inc(qt_out, 1)
            dve.sem_inc(done, 1)
            with dve.Fori(0, NB) as b:
                for g in range(2):
                    norm.dve(dve, b * NCH + g * 4, lambda i: c(4 * g + i))
                for j in range(NCH):
                    dve.wait_ge(k_out, b * NCH + j + 1 + 4)
                    nc.vector.tensor_reduce(KM[:, j:j + 1], c(j, K), AX_X, ALU.max).then_inc(k_max, 1)
                dve.wait_ge(k_max, (b + 1) * NCH)
                nc.vector.tensor_reduce(KV[:, 0:1], KM[:, :], AX_X, ALU.max, negate=True).then_inc(k_top, 1)
                dve.wait_ge(k_exp, b + 1)
                nc.vector.reciprocal(KV[:, 2:3], KV[:, 1:2]).then_inc(k_rec, 1)

                def scale_q(g):
                    n = b * NCH + g + 1
                    dve.wait_ge(q_exp, n)
                    nc.vector.tensor_reduce(SM[:, g % 2, :], QS[:, g % 2, :, :], AX_X, ALU.add).then_inc(q_sum, 1)
                    dve.wait_ge(q_sum, n)
                    nc.vector.reciprocal(SM[:, g % 2, :], SM[:, g % 2, :]).then_inc(q_rec, 1)
                    dve.wait_ge(q_rec, n)
                    q4 = QS[:, g % 2, :, :].rearrange("p (t h) d -> p t h d", t=4)
                    nc.vector.tensor_tensor(q4, q4, bc(SM, g), ALU.mult).then_inc(q_up, 1)

                def take_q(g):
                    dve.wait_ge(qt_mm, b * NCH + g + 1)
                    nc.vector.tensor_copy(c(g, QT), PS[:, QT_BANK, :]).then_inc(qt_out, 1)

                for g in range(NCH):
                    n = b * NCH + g + 1
                    q = heads(qv(g)[:, :, 0:P])
                    dve.wait_ge(qv_mm, n)
                    nc.vector.tensor_reduce(MX[:, g % 2, :].rearrange("p (t h) -> p t h", t=4), q, AX_X,
                                            ALU.max).then_inc(q_max, 1)
                    dve.wait_ge(q_max, n)
                    if g >= 2:
                        dve.wait_ge(qt_mm, n - 2)
                    nc.vector.tensor_tensor(QS[:, g % 2, :, :].rearrange("p (t h) d -> p t h d", t=4), q,
                                            bc(MX, g), ALU.subtract).then_inc(q_sub, 1)
                    if g >= 1:
                        scale_q(g - 1)
                    if g >= 2:
                        take_q(g - 2)
                scale_q(NCH - 1)
                take_q(NCH - 2)
                take_q(NCH - 1)
                dve.wait_ge(c_mm, (b + 1) * NCH)
                dve.wait_ge(k_rec, b + 1)
                nc.vector.scalar_tensor_tensor(CT[:, :], PS[:, CTX_BANK, 0:P], KV[:, 2:3], w("heads"), ALU.mult,
                                               ALU.mult).then_inc(c_up, 1)
                dve.wait_ge(m_mm, b + 1)
                nc.vector.tensor_copy(MT[:, :], PS[:, MISC_BANK, 0:P]).then_inc(m_up, 1)
                for j in range(NCH):
                    dve.wait_ge(o_out, b * NCH + j + 1 + 4)
                    nc.vector.bn_stats(ST[:, j, :], c(j, K)).then_inc(o_stat, 1)
                dve.wait_ge(o_stat, (b + 1) * NCH)
                nc.vector.memset(NIL[:, :], 0.0)
                nc.vector.bn_aggr(MV[:, :], ST[:, :, :]).then_inc(gs, 1)
                dve.wait_ge(gs, b * 7 + 1)
                nc.vector.tensor_tensor(GV[:, 0:1], MV[:, 0:1], MV[:, 0:1], ALU.mult).then_inc(gs, 1)
                dve.wait_ge(gs, b * 7 + 2)
                nc.vector.tensor_tensor(MV[:, 1:2], MV[:, 1:2], GV[:, 0:1], ALU.add).then_inc(gs, 1)
                dve.wait_ge(gs_mm, b + 1)
                nc.vector.tensor_copy(GV[:, 0:2], PS[:, MISC_BANK, 0:2]).then_inc(gs, 1)
                dve.wait_ge(gs, b * 7 + 4)
                nc.vector.tensor_tensor(GV[:, 2:3], GV[:, 0:1], GV[:, 0:1], ALU.mult).then_inc(gs, 1)
                dve.wait_ge(gs, b * 7 + 5)
                nc.vector.tensor_tensor(GV[:, 1:2], GV[:, 1:2], GV[:, 2:3], ALU.subtract).then_inc(gs, 1)
                dve.wait_ge(gs_log, b * 2 + 2)
                nc.vector.tensor_tensor(GV[:, 2:3], GV[:, 1:2], w("gn_w"), ALU.mult).then_inc(gs, 1)
                dve.wait_ge(gs, b * 7 + 7)
                nc.vector.tensor_tensor(GV[:, 3:4], GV[:, 0:1], GV[:, 2:3], ALU.mult).then_inc(o_norm, 1)
                dve.wait_ge(o_norm, b * 3 + 1)
                nc.vector.tensor_tensor(GV[:, 3:4], w("gn_b"), GV[:, 3:4], ALU.subtract).then_inc(o_norm, 1)
                dve.wait_ge(o_norm, b * 3 + 2)
                nc.vector.tensor_scalar(K[:, :], K[:, :], GV[:, 2:3], GV[:, 3:4], ALU.mult,
                                        ALU.add).then_inc(o_norm, 1)
                dve.wait_ge(o_norm, b * 3 + 3)
                x = XR[:, bass.ds(b * TOK, TOK)]
                nc.vector.tensor_tensor(x, x, K[:, :], ALU.add).then_inc(done, 1)


def layer2_ffn(nc, pack, XR):
    with ExitStack() as ctx:
        def sb(name, shape, dt=F32):
            return ctx.enter_context(nc.sbuf_tensor("l2f_" + name, shape, dt))

        sem = semaphores(nc, ctx, "l2f_")

        where, width = places(PACK2)
        W = sb("W", [P, width])

        def w(name, a=0, n=None):
            at, size = where[name]
            return W[:, at + a:at + (size if n is None else a + n)]

        E8, SENT = NEXP2, NEXP2 - TOP2
        XN = sb("XN", [P, TOK])
        SQ = sb("SQ", [P, 4, CH])
        RST = sb("RST", [P, 4, CH])
        LG = sb("LG", [P, 4, E8 + SENT])
        FOUND = sb("FOUND", [P, 4, E8 + SENT])
        M8, TOP = sb("M8", [P, 4, 8]), sb("TOP", [P, 4, 8])
        EX = sb("EX", [P, 4, E8])
        SM = sb("SM", [P, 4])
        NIL = sb("NIL", [P, 1])
        GATE = sb("GATE", [P, 2, 4, E8])
        GT = sb("GT", [E8, CH])
        PR = sb("PR", [P, 2, E8, P])
        H1 = sb("H1", [P, 2, E8 // 2, P])
        H2 = sb("H2", [P, 2, E8 // 4, P])
        PS = ctx.enter_context(nc.psum_tensor("l2f_PS", [P, 8, CH], F32))
        R_BANK, GT_BANK, Y_BANK = 4, 5, 6

        loaded, ready = sem("loaded"), sem("ready")
        r_mm, r_step, r_exp, gate_up = sem("r_mm"), sem("r_step"), sem("r_exp"), sem("gate_up")
        gt_mm, gt_up = sem("gt_mm"), sem("gt_up")
        e_mm, pr_up, h1_up, h2_up, y_mm, done = (sem(n) for n in ("e_mm", "pr_up", "h1_up", "h2_up", "y_mm", "done"))
        norm = Norm(nc, sem, PS, SQ, RST, w("center"), w("ones"), w("eps"))
        NT = NCH * 4
        STEPS = 15

        block = ctx.enter_context(nc.Block())

        @block.sync
        def _(sp):
            sp.dma_start(W[:, :], pack).then_inc(loaded, 16)

        @block.tensor
        def _(pe):
            pe.wait_ge(loaded, 16)
            with pe.Fori(0, NB) as b:
                for g in range(2):
                    norm.pe(pe, b * NCH + g * 4, lambda i: XR[:, bass.ds(b * TOK + (4 * g + i) * CH, CH)],
                            lambda i: pe.wait_ge(done, b * NCH + 2))

                def tile(t):
                    return XN[:, t * P:(t + 1) * P]

                def router(g):
                    pe.wait_ge(r_step, (b * NCH + g) * STEPS + 1)
                    for t in range(4):
                        ins = nc.tensor.matmul(PS[:, R_BANK, t * E8:(t + 1) * E8], tile(4 * g + t), w("router"),
                                               start=True, stop=True)
                    ins.then_inc(r_mm, 1)

                def biases(g):
                    pe.wait_ge(gate_up, b * NCH + g + 1)
                    for t in range(4):
                        ins = nc.tensor.transpose(PS[0:E8, GT_BANK, t * P:(t + 1) * P], GATE[:, g % 2, t, :],
                                                  w("ident"))
                    ins.then_inc(gt_mm, 1)
                    pe.wait_ge(gt_up, b * NCH + g + 1)
                    pe.wait_ge(done, b * NCH + g + 1)
                    nc.tensor.matmul(PS[:, Y_BANK + g % 2, :], w("expert_b")[0:E8, :], GT[:, :], start=True, stop=False)

                def experts(t):
                    pe.wait_ge(pr_up, b * NT + t + 1)
                    for half in range(2):
                        ins = nc.tensor.matmul(PS[:, (t % 2) * 2 + half, :], tile(t),
                                               w("experts", half * CH, CH), start=True, stop=True)
                    ins.then_inc(e_mm, 1)

                def sums(t):
                    pe.wait_ge(h2_up, b * NT + t + 1)
                    for half in range(2):
                        ins = nc.tensor.matmul(PS[:, Y_BANK + t // 4 % 2, (t % 4) * P:(t % 4 + 1) * P], H2[:, t % 2, half, :],
                                               w("ident"), start=False, stop=(half == 1 and t % 4 == 3))
                    ins.then_inc(y_mm, 1)

                pe.wait_ge(norm.out, b * NCH + NCH + 4)
                router(0)
                for t in range(NT + 2):
                    if t < NT:
                        experts(t)
                    if t % 4 == 0 and t + 4 < NT:
                        router(t // 4 + 1)
                    if t >= 2:
                        if t % 4 == 2:
                            biases(t // 4)
                        sums(t - 2)

        @block.scalar
        def _(act):
            nc.scalar.preload_act_table_set(EXP_LN)
            with act.Fori(0, NB) as b:
                for g in range(2):
                    norm.act(act, b * NCH + g * 4)
                for g in range(NCH):
                    act.wait_ge(r_step, (b * NCH + g + 1) * STEPS + 7)
                    nc.scalar.activation(EX[:, :, :], EX[:, :, :], ACT.Exp).then_inc(r_exp, 1)
                    act.wait_ge(gt_mm, b * NCH + g + 1)
                    if g >= 1:
                        act.wait_ge(y_mm, b * NT + 4 * g - 3)
                    nc.scalar.copy(GT[:, :], PS[0:E8, GT_BANK, :]).then_inc(gt_up, 1)

        @block.gpsimd
        def _(pool):
            pool.wait_ge(loaded, 16)
            with pool.Fori(0, NB) as b:
                for t in range(NT):
                    pool.wait_ge(pr_up, b * NT + t + 1 + 2)
                    nc.gpsimd.tensor_tensor(H1[:, t % 2, :, :], PR[:, t % 2, 0:4, :], PR[:, t % 2, 4:8, :],
                                            ALU.add).then_inc(h1_up, 1)
                    pool.wait_ge(h1_up, b * NT + t + 1)
                    if t >= 2:
                        pool.wait_ge(y_mm, b * NT + t - 1)
                    nc.gpsimd.tensor_tensor(H2[:, t % 2, :, :], H1[:, t % 2, 0:2, :], H1[:, t % 2, 2:4, :],
                                            ALU.add).then_inc(h2_up, 1)

        @block.vector
        def _(dve):
            norm.begin(dve)
            dve.sem_inc(done, 2)
            dve.sem_inc(pr_up, 2)
            nc.vector.memset(LG[:, :, E8:], -BIG).then_inc(ready, 1)
            nc.vector.memset(TOP[:, :, :], -BIG).then_inc(ready, 1)
            dve.wait_ge(ready, 2)
            dve.wait_ge(loaded, 16)
            dve.sem_inc(r_step, STEPS)
            with dve.Fori(0, NB) as b:
                for g in range(2):
                    norm.dve(dve, b * NCH + g * 4, lambda i: XN[:, (4 * g + i) * CH:(4 * g + i + 1) * CH])

                def after(g, steps):
                    dve.wait_ge(r_step, (b * NCH + g + 1) * STEPS + steps)

                def largest(g):
                    dve.wait_ge(r_mm, b * NCH + g + 1)
                    nc.vector.tensor_tensor(LG[:, :, 0:E8],
                                            PS[:, R_BANK, 0:4 * E8].rearrange("p (t e) -> p t e", t=4),
                                            w("router_b").rearrange("p (t e) -> p t e", t=4),
                                            ALU.add).then_inc(r_step, 1)
                    after(g, 1)
                    nc.vector.memset(NIL[:, :], 0.0)
                    for t in range(4):
                        nc.vector.max(M8[:, t, :], LG[:, t, 0:E8]).then_inc(r_step, 1)

                def chosen(g):
                    after(g, 5)
                    nc.vector.tensor_copy(TOP[:, :, 0:TOP2], M8[:, :, 0:TOP2]).then_inc(r_step, 1)
                    nc.vector.tensor_tensor(EX[:, :, :], LG[:, :, 0:E8],
                                            M8[:, :, 0:1].to_broadcast([P, 4, E8]),
                                            ALU.subtract).then_inc(r_step, 1)
                    after(g, 7)
                    nc.vector.memset(NIL[:, :], 0.0)
                    for t in range(4):
                        nc.vector.match_replace(FOUND[:, t, :], TOP[:, t, :], LG[:, t, :],
                                                BIG).then_inc(r_step, 1)

                def weights(g):
                    after(g, 11)
                    dve.wait_ge(r_exp, b * NCH + g + 1)
                    nc.vector.scalar_tensor_tensor(EX[:, :, :], FOUND[:, :, 0:E8], BIG / 2, EX[:, :, :],
                                                   ALU.is_ge, ALU.mult).then_inc(r_step, 1)
                    after(g, 12)
                    nc.vector.tensor_reduce(SM[:, :], EX[:, :, :], AX_X, ALU.add).then_inc(r_step, 1)
                    after(g, 13)
                    nc.vector.reciprocal(SM[:, :], SM[:, :]).then_inc(r_step, 1)

                def shares(g):
                    after(g, 14)
                    if g >= 2:
                        dve.wait_ge(gt_mm, b * NCH + g - 1)
                    nc.vector.tensor_tensor(GATE[:, g % 2, :, :], EX[:, :, :],
                                            SM[:, :].unsqueeze(2).to_broadcast([P, 4, E8]),
                                            ALU.mult).then_inc(gate_up, 1)
                    dve.wait_ge(gate_up, b * NCH + g + 1)
                    dve.sem_inc(r_step, STEPS - 14)

                def add_group(g):
                    dve.wait_ge(y_mm, b * NT + 4 * g + 4)
                    x = XR[:, bass.ds(b * TOK + g * CH, CH)]
                    nc.vector.tensor_tensor(x, x, PS[:, Y_BANK + g % 2, :], ALU.add).then_inc(done, 1)

                parts = (largest, chosen, weights, shares)
                for part in parts:
                    part(0)
                for g in range(NCH):
                    for t in range(4 * g, 4 * g + 4):
                        dve.wait_ge(e_mm, b * NT + t + 1)
                        if t >= 2:
                            dve.wait_ge(h1_up, b * NT + t - 1)
                        nc.vector.tensor_tensor(
                            PR[:, t % 2, :, :],
                            PS[:, (t % 2) * 2:(t % 2) * 2 + 2, :].rearrange("p a n -> p (a n)").rearrange(
                                "p (e c) -> p e c", e=E8),
                            GATE[:, g % 2, t % 4, :].unsqueeze(2).to_broadcast([P, E8, P]),
                            ALU.mult).then_inc(pr_up, 1)
                        if g + 1 < NCH:
                            parts[t % 4](g + 1)
                        if t % 4 == 2 and g:
                            add_group(g - 1)
                add_group(NCH - 1)


def layer3_attn(nc, pack, XR):
    with ExitStack() as ctx:
        def sb(name, shape, dt=F32):
            return ctx.enter_context(nc.sbuf_tensor("l3a_" + name, shape, dt))

        sem = semaphores(nc, ctx, "l3a_")

        where, width = places(PACK3)
        W = sb("W", [P, width])

        def w(name, a=0, n=None):
            at, size = where[name]
            return W[:, at + a:at + (size if n is None else a + n)]

        VW = HD * P
        XN = sb("XN", [P, NTOK])
        SQ = sb("SQ", [P, 4, CH])
        RST = sb("RST", [P, 4, CH])
        KS = SQ
        SC = sb("SC", [P, 5, CH])
        S, E, M, RU, U1 = (SC[:, n, :] for n in range(5))
        ONE = sb("ONE", [P, CH])
        END = sb("END", [P, 2])
        ET = sb("ET", [P, (NCH + 1) * 4, NB, HD])
        RT = sb("RT", [P, (NCH + 1) * 4, NB, HD])
        XS = sb("XS", [P, 2, CH])
        V = SC[:, 0:4, :].rearrange("p (a c) n -> p a (c n)", a=2).rearrange("p a (h d) -> p a h d", h=HD)
        WP = sb("WP", [P, 2, HD, P])
        Vs = RST[:, :, :].rearrange("p (a c) n -> p a (c n)", a=2)
        H1 = sb("H1", [P, 4, P])
        H2 = sb("H2", [P, 2, 2, P])
        Y = SQ[:, 0:2, :].rearrange("p a n -> p (a n)").rearrange("p (h d) -> p h d", h=HD)
        PS = ctx.enter_context(nc.psum_tensor("l3a_PS", [P, 8, CH], F32))

        loaded, zeroed = sem("loaded"), sem("zeroed")
        k_mm, k_up, s_mm = sem("k_mm"), sem("k_up"), sem("s_mm")
        s_out, s_max, s_sub, e_up, u_up, r_up = (sem(n) for n in ("s_out", "s_max", "s_sub", "e_up", "u_up", "r_up"))
        tr_up, tr_out = sem("tr_up"), sem("tr_out")
        xs_up, v_mm, v_up, ve_up, w_mm, w_up = (sem(n) for n in ("xs_up", "v_mm", "v_up", "ve_up", "w_mm", "w_up"))
        y_up, h1_up, h2_up, y_mm, done, fresh = (sem(n) for n in ("y_up", "h1_up", "h2_up", "y_mm", "done", "fresh"))
        norm = Norm(nc, sem, PS, SQ, RST, w("center"), w("ones"), w("eps"))
        S_BANK, E_BANK, R_BANK = 2, 4, 5
        NU = NB * HD
        TB = 8
        NT = TOK // P

        def q_col(p, h):
            return w("q", h * (2 * P - 1) + P - 1 - p, P)

        block = ctx.enter_context(nc.Block())

        @block.sync
        def _(sp):
            sp.dma_start(W[:, :], pack).then_inc(loaded, 16)

        @block.tensor
        def _(pe):
            pe.wait_ge(loaded, 16)
            with pe.Fori(0, NTOK // CH // 4) as g:
                norm.pe(pe, g * 4, lambda i: XR[:, bass.ds((g * 4 + i) * CH, CH)], lambda i: None)
            pe.wait_ge(norm.out, NTOK // CH + 4)

            def turn(j):
                pe.wait_ge(r_up, j + 1)
                pe.wait_ge(e_up, j + 1)
                pe.wait_ge(tr_out, j * 2 + 1)
                for src, bank in ((E, E_BANK), (RU, R_BANK)):
                    for t in range(4):
                        ins = nc.tensor.transpose(PS[:, bank, t * P:(t + 1) * P], src[:, t * P:(t + 1) * P],
                                                  w("ident"))
                ins.then_inc(tr_up, 1)

            with pe.Fori(0, NCH) as j:
                def score(u):
                    b, h = divmod(u, HD)
                    if u == 0:
                        pe.wait_ge(s_out, j + 1)
                    pe.wait_ge(k_up, j * NU + u + 1 + 2)
                    nc.tensor.matmul(PS[:, S_BANK, :], q_col(32 * b + h, h), KS[:, u % 2, :], start=(u == 0),
                                     stop=(u == NU - 1)).then_inc(s_mm, 1)

                for u in range(NU):
                    b, h = divmod(u, HD)
                    pe.wait_ge(k_up, j * NU + u + 1)
                    nc.tensor.matmul(PS[:, u % 2, :], w("k", h * P, P), XN[:, bass.ds(b * TOK + j * CH, CH)],
                                     start=True, stop=True).then_inc(k_mm, 1)
                    if u >= 1:
                        score(u - 1)
                    if u == 16:
                        turn(j)
                score(NU - 1)
            turn(NCH)
            pe.wait_ge(tr_out, NCH * 2 + 3)
            pe.wait_ge(k_up, NCH * NU + 2)

            with pe.Fori(0, NB) as b:
                with pe.Fori(0, NT // TB) as jj:
                    n0 = (b * (NT // TB) + jj) * TB
                    c0 = (b * (NT // TB) + jj) * 2

                    def values(t):
                        if t % 4 == 0:
                            pe.wait_ge(xs_up, c0 + t // 4 + 1)
                        pe.wait_ge(v_up, n0 + t + 1)
                        for half in range(2):
                            ins = nc.tensor.matmul(PS[:, (t % 2) * 6 + half, :],
                                                   XS[:, t // 4, (t % 4) * P:(t % 4 + 1) * P],
                                                   w("v", half * CH, CH), start=True, stop=True)
                        ins.then_inc(v_mm, 1)

                    def running(t):
                        pe.wait_ge(ve_up, n0 + t + 1 + 2)
                        pe.wait_ge(w_up, n0 + t + 2)
                        for half in range(2):
                            nc.tensor.matmul(PS[:, 2 + half, :], w("upto"),
                                             V[:, t % 2, 4 * half:4 * half + 4, :].rearrange("p h d -> p (h d)"),
                                             start=True, stop=False)
                            ins = nc.tensor.matmul(
                                PS[:, 2 + half, :], w("last"),
                                WP[:, (t + 1) % 2, 4 * half:4 * half + 4, :].rearrange("p h d -> p (h d)"),
                                start=False, stop=True)
                        ins.then_inc(w_mm, 1)

                    def result(t):
                        if t % 4 == 0:
                            pe.wait_ge(done, c0 + t // 4 + 1)
                        pe.wait_ge(h2_up, n0 + t + 1)
                        for half in range(2):
                            ins = nc.tensor.matmul(PS[:, 4 + t // 4, (t % 4) * P:(t % 4 + 1) * P],
                                                   H2[:, t % 2, half, :], w("ident"),
                                                   start=(half == 0), stop=(half == 1))
                        ins.then_inc(y_mm, 1)

                    values(0)
                    for t in range(TB):
                        if t + 1 < TB:
                            values(t + 1)
                        running(t)
                        if t >= 1:
                            result(t - 1)
                    result(TB - 1)

        @block.scalar
        def _(act):
            act.wait_ge(loaded, 16)
            nc.scalar.preload_act_table_set(EXP_LN)
            with act.Fori(0, NTOK // CH // 4) as g:
                norm.act(act, g * 4)
            act.wait_ge(norm.meaned, NTOK // CH)
            act.sem_inc(k_up, 2)
            act.sem_inc(v_up, 2)
            act.sem_inc(w_up, 2)
            act.sem_inc(e_up, 1)
            with act.Fori(0, NCH) as j:
                for u in range(NU):
                    act.wait_ge(k_mm, j * NU + u + 1)
                    if u >= 2:
                        act.wait_ge(s_mm, j * NU + u - 1)
                    nc.scalar.activation(KS[:, u % 2, :], PS[:, u % 2, :], ACT.Silu).then_inc(k_up, 1)
                act.wait_ge(s_mm, (j + 1) * NU)
                act.wait_ge(s_sub, j + 1)
                act.wait_ge(tr_up, j + 1)
                nc.scalar.activation(E, E, ACT.Exp).then_inc(e_up, 1)
            nc.scalar.preload_act_table_set(SILU)
            with act.Fori(0, NB) as b:
                with act.Fori(0, NT // TB) as jj:
                    n0 = (b * (NT // TB) + jj) * TB

                    def keep(t):
                        act.wait_ge(w_mm, n0 + t + 1)
                        act.wait_ge(y_up, n0 + t + 1)
                        nc.scalar.copy(WP[:, t % 2, :, :].rearrange("p h d -> p (h d)"),
                                       PS[:, 2:4, :].rearrange("p a n -> p (a n)")).then_inc(w_up, 1)

                    act.wait_ge(fresh, b + 1)
                    for t in range(TB):
                        act.wait_ge(v_mm, n0 + t + 1)
                        act.wait_ge(ve_up, n0 + t + 1)
                        nc.scalar.activation(Vs[:, t % 2, :], PS[:, (t % 2) * 6:(t % 2) * 6 + 2, :]
                                             .rearrange("p a n -> p (a n)"), ACT.Silu).then_inc(v_up, 1)
                        if t >= 1:
                            keep(t - 1)
                    keep(TB - 1)

        @block.gpsimd
        def _(pool):
            nc.gpsimd.memset(ONE[:, :], 1.0).then_inc(zeroed, 1)
            pool.wait_ge(norm.out, NTOK // CH + 4)
            with pool.Fori(0, NB) as b:
                with pool.Fori(0, NT // TB) as jj:
                    n0 = (b * (NT // TB) + jj) * TB
                    pool.wait_ge(v_up, n0 + 2)
                    for u in range(2):
                        nc.gpsimd.tensor_copy(XS[:, u, :], XN[:, bass.ds(b * TOK + (jj * 2 + u) * CH, CH)]
                                              ).then_inc(xs_up, 1)
                    for t in range(TB):
                        pool.wait_ge(y_up, n0 + t + 1 + 2)
                        nc.gpsimd.tensor_tensor(H1[:, :, :], Y[:, 0:4, :], Y[:, 4:8, :], ALU.add).then_inc(h1_up, 1)
                        pool.wait_ge(h1_up, n0 + t + 1)
                        if t >= 2:
                            pool.wait_ge(y_mm, n0 + t - 1)
                        nc.gpsimd.tensor_tensor(H2[:, t % 2, :, :], H1[:, 0:2, :], H1[:, 2:4, :],
                                                ALU.add).then_inc(h2_up, 1)
                        pool.wait_ge(h2_up, n0 + t + 1)

        @block.vector
        def _(dve):
            norm.begin(dve)
            dve.sem_inc(s_out, 1)
            dve.sem_inc(tr_out, 2)
            dve.sem_inc(ve_up, 2)
            dve.sem_inc(y_up, 2)
            dve.sem_inc(done, 2)
            nc.vector.memset(E, 0.0).then_inc(zeroed, 1)
            nc.vector.memset(RU, 0.0).then_inc(r_up, 1)
            nc.vector.memset(END[:, 0:1], -BIG).then_inc(zeroed, 1)
            nc.vector.memset(END[:, 1:2], 0.0).then_inc(zeroed, 1)
            with dve.Fori(0, NTOK // CH // 4) as g:
                norm.dve(dve, g * 4, lambda i: XN[:, bass.ds((g * 4 + i) * CH, CH)])
            dve.wait_ge(zeroed, 4)

            def take(j):
                dve.wait_ge(tr_up, j + 1)
                for dst, bank in ((ET, E_BANK), (RT, R_BANK)):
                    nc.vector.tensor_copy(dst[:, bass.ds(j * 4, 4), :, :],
                                          PS[:, bank, :].rearrange("p (t b h) -> p t b h", t=4, b=NB)[:, :, :, 0:HD]
                                          ).then_inc(tr_out, 1)

            with dve.Fori(0, NCH) as j:
                take(j)
                dve.wait_ge(s_mm, (j + 1) * NU)
                nc.vector.tensor_copy(S, PS[:, S_BANK, :]).then_inc(s_out, 1)
                dve.wait_ge(s_out, j + 2)
                nc.vector.tensor_tensor_scan(M, S, S, END[:, 0:1], ALU.max,
                                             ALU.max).then_inc(s_max, 1)
                dve.wait_ge(s_max, j * 2 + 1)
                nc.vector.tensor_copy(END[:, 0:1], M[:, CH - 1:CH]).then_inc(s_max, 1)
                nc.vector.tensor_tensor(E, S, M, ALU.subtract).then_inc(s_sub, 1)
                dve.wait_ge(e_up, j + 2)
                nc.vector.tensor_tensor_scan(U1, ONE[:, :], E, END[:, 1:2], ALU.mult,
                                             ALU.add).then_inc(u_up, 1)
                dve.wait_ge(u_up, j * 3 + 1)
                nc.vector.tensor_copy(END[:, 1:2], U1[:, CH - 1:CH]).then_inc(u_up, 1)
                nc.vector.reciprocal(RU, U1).then_inc(u_up, 1)
                dve.wait_ge(u_up, j * 3 + 3)
                nc.vector.tensor_scalar(RU, RU, 1.0 / HD, None, ALU.mult).then_inc(r_up, 1)
                dve.wait_ge(r_up, j + 2)
            take(NCH)
            dve.wait_ge(tr_out, NCH * 2 + 4)

            with dve.Fori(0, NB) as b:
                nc.vector.memset(WP[:, 1, :, :], 0.0).then_inc(fresh, 1)
                with dve.Fori(0, NT // TB) as jj:
                    n0 = (b * (NT // TB) + jj) * TB
                    c0 = (b * (NT // TB) + jj) * 2

                    def by_head(table, t):
                        return table[:, bass.ds((jj * TB + t + 4), 1), bass.ds(b, 1), :].rearrange(
                            "p t b h -> p (t b h)").unsqueeze(2).to_broadcast([P, HD, P])

                    def weigh(t):
                        dve.wait_ge(w_up, n0 + t + 1 + 2)
                        dve.wait_ge(h1_up, n0 + t) if t else None
                        nc.vector.tensor_tensor(Y[:, :, :], WP[:, t % 2, :, :], by_head(RT, t),
                                                ALU.mult).then_inc(y_up, 1)
                        if t % 4 == 3:
                            dve.wait_ge(y_mm, n0 + t + 1)
                            x = XR[:, bass.ds(b * TOK + (jj * 2 + t // 4) * CH, CH)]
                            nc.vector.tensor_tensor(x, x, PS[:, 4 + t // 4, :], ALU.add).then_inc(done, 1)

                    for t in range(TB):
                        dve.wait_ge(v_up, n0 + t + 1 + 2)
                        dve.wait_ge(w_up, n0 + t + 1)
                        nc.vector.tensor_tensor(V[:, t % 2, :, :], Vs[:, t % 2, :].rearrange("p (h d) -> p h d", h=HD),
                                                by_head(ET, t), ALU.mult).then_inc(ve_up, 1)
                        if t >= 1:
                            weigh(t - 1)
                    weigh(TB - 1)


def layer3_ffn(nc, pack, w1, w2, XR, out):
    with ExitStack() as ctx:
        def sb(name, shape, dt=F32):
            return ctx.enter_context(nc.sbuf_tensor("l3f_" + name, shape, dt))

        sem = semaphores(nc, ctx, "l3f_")

        where, width = places(PACK3F)
        W = sb("W", [P, width])

        def w(name, a=0, n=None):
            at, size = where[name]
            return W[:, at + a:at + (size if n is None else a + n)]

        QH = HID // P
        EG = 2
        XN = sb("XN", [P, 2 * TOK])
        SQ = sb("SQ", [P, 4, CH])
        RST = sb("RST", [P, 4, CH])
        PM = sb("PM", [P, 2, TOK])
        LG = sb("LG", [P, TOK])
        V4 = sb("V4", [P, 4])
        M8 = sb("M8", [P, 8])
        NIL = sb("NIL", [P, 1])
        XT = sb("XT", [P, 2, 3 * P])
        PO = sb("PO", [P, NB, NEXP3])
        W1 = sb("W1", [P, 2, EG, HID])
        W2 = sb("W2", [P, 2, EG, QH, P])
        HS = sb("HS", [P, 2, EG, QH, NB])
        OT = sb("OT", [P, NB, NEXP3])
        OE = sb("OE", [P, NB, P])
        PS = ctx.enter_context(nc.psum_tensor("l3f_PS", [P, 8, CH], F32))

        loaded = sem("loaded")
        l_mm, l_out, l_max, p_exp, p_rec, p_up = (sem(n) for n in ("l_mm", "l_out", "l_max", "p_exp", "p_rec", "p_up"))
        top, marked, chosen = sem("top"), sem("marked"), sem("chosen")
        t_mm, t_out, po_mm, po_up = sem("t_mm"), sem("t_out"), sem("po_mm"), sem("po_up")
        w1_in, w2_in = [sem("w1_in0"), sem("w1_in1")], [sem("w2_in0"), sem("w2_in1")]
        h_mm, h_b, h_up, o_mm, o_up = (sem(n) for n in ("h_mm", "h_b", "h_up", "o_mm", "o_up"))
        oe_zero, oe_mm, oe_up, y_mm, y_up, stored = (
            sem(n) for n in ("oe_zero", "oe_mm", "oe_up", "y_mm", "y_up", "stored"))
        norm = Norm(nc, sem, PS, SQ, RST, w("center"), w("ones"), w("eps"))
        NT = TOK // P
        NG = NEXP3 // EG

        block = ctx.enter_context(nc.Block())

        @block.sync
        def _(sp):
            sp.dma_start(W[:, :], pack).then_inc(loaded, 16)
            for u in range(2):
                sp.dma_start(W1[:, u, :, :], w1[:, u * EG:(u + 1) * EG, :]).then_inc(w1_in[u], 16)
                sp.dma_start(W2[:, u, :, :, :], w2[:, u * EG:(u + 1) * EG, :, :]).then_inc(w2_in[u], 16)
            with sp.Fori(1, NG // 2) as gg:
                for u in range(2):
                    at = (gg * 2 + u) * EG
                    sp.wait_ge(h_mm, (gg - 1) * 2 + u + 1)
                    sp.dma_start(W1[:, u, :, :], w1[:, bass.ds(at, EG), :]).then_inc(w1_in[u], 16)
                    sp.wait_ge(o_mm, (gg - 1) * 2 + u + 1)
                    sp.dma_start(W2[:, u, :, :, :], w2[:, bass.ds(at, EG), :, :]).then_inc(w2_in[u], 16)
            for n in range(2 * NB):
                sp.wait_ge(y_up, (n + 1) * NCH // 2 + 4)
                at = n * TOK // 2
                sp.dma_start(out[:, at:at + TOK // 2], XR[:, at:at + TOK // 2]).then_inc(stored, 16)
            sp.wait_ge(stored, 2 * NB * 16)

        @block.tensor
        def _(pe):
            pe.wait_ge(loaded, 16)
            for pr in range(2):
                for g in range(4):
                    if pr and g == 0:
                        pe.wait_ge(t_out, NT + 2)
                        pe.wait_ge(po_up, 2)
                    norm.pe(pe, pr * 16 + g * 4,
                            lambda i: XR[:, pr * 2 * TOK + (4 * g + i) * CH:pr * 2 * TOK + (4 * g + i + 1) * CH],
                            lambda i: None)
                pe.wait_ge(norm.out, pr * 16 + 16 + 4)
                for j in range(NCH):
                    pe.wait_ge(l_out, pr * NCH + j + 1)
                    for m in range(2):
                        at = m * TOK + j * CH
                        ins = nc.tensor.matmul(PS[:, j % 4, :], w("gate", m * P, P), XN[:, at:at + CH],
                                               start=(m == 0), stop=(m == 1))
                    ins.then_inc(l_mm, 1)

                def pooled(t):
                    pe.wait_ge(t_out, pr * NT + t + 1 + 2)
                    for m in range(2):
                        ins = nc.tensor.matmul(PS[:, 6 + m, 0:NEXP3], XT[:, t % 2, m * P:(m + 1) * P],
                                               XT[:, t % 2, 2 * P + m * NEXP3:2 * P + (m + 1) * NEXP3],
                                               start=(t == 0), stop=(t == NT - 1))
                    ins.then_inc(po_mm, 1)

                pe.wait_ge(chosen, pr + 1)
                for t in range(NT):
                    pe.wait_ge(t_out, pr * NT + t + 1)
                    for n, src in enumerate((XN[:, t * P:(t + 1) * P], XN[:, TOK + t * P:TOK + (t + 1) * P],
                                             PM[:, pr, t * P:(t + 1) * P])):
                        ins = nc.tensor.transpose(PS[:, 4 + t % 2, n * P:(n + 1) * P], src, w("ident"))
                    ins.then_inc(t_mm, 1)
                    if t >= 1:
                        pooled(t - 1)
                pooled(NT - 1)

            pe.wait_ge(po_up, 4)
            with pe.Fori(0, NG // 2) as gg:
                def hidden(u):
                    n = gg * 2 + u
                    pe.wait_ge(w1_in[u], (gg + 1) * 16)
                    pe.wait_ge(h_b, n + 1)
                    for e in range(EG):
                        for q in range(QH):
                            at = (e * QH + q) * NB
                            ins = nc.tensor.matmul(PS[:, u, at:at + NB], W1[:, u, e, q * P:(q + 1) * P],
                                                   PO[:, :, bass.ds(n * EG + e, 1)].rearrange("p b e -> p (b e)"),
                                                   start=True, stop=True)
                    ins.then_inc(h_mm, 1)

                def second(u):
                    n = gg * 2 + u
                    pe.wait_ge(w2_in[u], (gg + 1) * 16)
                    pe.wait_ge(h_up, n + 1)
                    pe.wait_ge(o_up, n + 1)
                    for e in range(EG):
                        for q in range(QH):
                            ins = nc.tensor.matmul(PS[:, 2 + u, e * NB:(e + 1) * NB], W2[:, u, e, q, :],
                                                   HS[:, u, e, q, :], start=(q == 0), stop=(q == QH - 1))
                    ins.then_inc(o_mm, 1)

                hidden(0)
                hidden(1)
                second(0)
                second(1)

            pe.wait_ge(o_up, NG + 2)
            for pr in range(2):
                nc.tensor.transpose(PS[:, 4 + pr, 0:P], OT[:, 2 * pr:2 * pr + 2, :].rearrange("p b e -> p (b e)"),
                                    w("ident")).then_inc(oe_mm, 1)
            pe.wait_ge(oe_up, NB)
            for n in range(NB * NCH):
                b, j = divmod(n, NCH)
                pe.wait_ge(y_up, n + 1)
                nc.tensor.matmul(PS[:, n % 4, :], OE[:, b, :], PM[:, b // 2, j * CH:(j + 1) * CH],
                                 start=True, stop=True).then_inc(y_mm, 1)

        @block.scalar
        def _(act):
            act.wait_ge(loaded, 16)
            act.sem_inc(l_out, 4)
            act.sem_inc(t_out, 2)
            nc.scalar.preload_act_table_set(EXP_LN)
            for pr in range(2):
                for g in range(4):
                    norm.act(act, pr * 16 + g * 4)
                for j in range(NCH):
                    act.wait_ge(l_mm, pr * NCH + j + 1)
                    if pr and j == 0:
                        act.wait_ge(chosen, pr)
                    nc.scalar.activation(LG[:, j * CH:(j + 1) * CH], PS[:, j % 4, :], ACT.Identity,
                                         bias=w("gate_b")).then_inc(l_out, 1)
                act.wait_ge(l_max, pr + 1)
                nc.scalar.activation(PM[:, pr, :], LG[:, :], ACT.Exp, bias=V4[:, 0:1],
                                     accum_out=V4[:, 1:2]).then_inc(p_exp, 1)
                for t in range(NT):
                    act.wait_ge(t_mm, pr * NT + t + 1)
                    if t >= 2:
                        act.wait_ge(po_mm, pr * NT + t - 1)
                    nc.scalar.copy(XT[:, t % 2, :], PS[:, 4 + t % 2, 0:3 * P]).then_inc(t_out, 1)
            nc.scalar.preload_act_table(ACT.Gelu)
            with act.Fori(0, NG // 2) as gg:
                for u in range(2):
                    act.wait_ge(h_b, gg * 2 + u + 1 + 2)
                    nc.scalar.activation(HS[:, u, :, :, :], HS[:, u, :, :, :], ACT.Gelu).then_inc(h_up, 1)

        @block.gpsimd
        def _(pool):
            nc.gpsimd.memset(OE[:, :, :], 0.0).then_inc(oe_zero, 1)

        @block.vector
        def _(dve):
            norm.begin(dve)
            dve.sem_inc(h_b, 2)
            dve.sem_inc(o_up, 2)
            dve.sem_inc(y_up, 4)
            for pr in range(2):
                for g in range(4):
                    norm.dve(dve, pr * 16 + g * 4, lambda i: XN[:, (4 * g + i) * CH:(4 * g + i + 1) * CH])
                dve.wait_ge(l_out, (pr + 1) * NCH + 4)
                nc.vector.tensor_reduce(V4[:, 0:1], LG[:, :], AX_X, ALU.max, negate=True).then_inc(l_max, 1)
                dve.wait_ge(p_exp, pr + 1)
                nc.vector.reciprocal(V4[:, 2:3], V4[:, 1:2]).then_inc(p_rec, 1)
                dve.wait_ge(p_rec, pr + 1)
                nc.vector.tensor_scalar(PM[:, pr, :], PM[:, pr, :], V4[:, 2:3], None, ALU.mult).then_inc(p_up, 1)
                dve.wait_ge(p_up, pr + 1)
                nc.vector.max(M8[:, :], PM[:, pr, :]).then_inc(top, 1)
                dve.wait_ge(top, pr + 1)
                nc.vector.match_replace(LG[:, :], M8[:, :], PM[:, pr, :], -1.0).then_inc(marked, 1)
                dve.wait_ge(marked, pr + 1)
                nc.vector.scalar_tensor_tensor(PM[:, pr, :], LG[:, :], 0.0, PM[:, pr, :], ALU.is_lt,
                                               ALU.mult).then_inc(chosen, 1)
                dve.wait_ge(po_mm, (pr + 1) * NT)
                nc.vector.tensor_copy(PO[:, 2 * pr:2 * pr + 2, :], PS[:, 6:8, 0:NEXP3]).then_inc(po_up, 2)
            with dve.Fori(0, NG // 2) as gg:
                for u in range(2):
                    n = gg * 2 + u
                    dve.wait_ge(h_mm, n + 1)
                    b1 = w("b1").rearrange("p (e q) -> p e q", q=QH)[:, bass.ds(n * EG, EG), :]
                    hid = HS[:, u, :, :, :].rearrange("p e q b -> p (e q) b")
                    nc.vector.tensor_tensor(hid, PS[:, u, 0:EG * QH * NB].rearrange("p (e b) -> p e b", b=NB),
                                            b1.rearrange("p e q -> p (e q)").unsqueeze(2)
                                            .to_broadcast([P, EG * QH, NB]), ALU.add).then_inc(h_b, 1)
                for u in range(2):
                    n = gg * 2 + u
                    dve.wait_ge(o_mm, n + 1)
                    nc.vector.tensor_tensor(OT[:, :, bass.ds(n * EG, EG)].rearrange("p b e -> p e b"),
                                            PS[:, 2 + u, 0:EG * NB].rearrange("p (e b) -> p e b", b=NB),
                                            w("b2")[:, bass.ds(n * EG, EG)].unsqueeze(2)
                                            .to_broadcast([P, EG, NB]), ALU.add).then_inc(o_up, 1)
            dve.wait_ge(oe_zero, 1)
            for b in range(NB):
                s = slice((b % 2) * HALF, (b % 2 + 1) * HALF)
                dve.wait_ge(oe_mm, b // 2 + 1)
                nc.vector.tensor_copy(OE[s, b, :], PS[s, 4 + b // 2, 0:P]).then_inc(oe_up, 1)
            for n in range(NB * NCH):
                dve.wait_ge(y_mm, n + 1)
                x = XR[:, n * CH:(n + 1) * CH]
                nc.vector.tensor_tensor(x, x, PS[:, n % 4, :], ALU.add).then_inc(y_up, 1)


def program(nc, xT, p0, sel, p1, p2, p3, p3f, w1, w2, out):
    x1 = nc.dram_tensor("layer0_out", [P, NTOK], F32).ap()
    layer0(nc, xT, p0, sel, x1)
    with nc.sbuf_tensor("XR", [P, NTOK], F32) as XR:
        layer1(nc, x1, p1, XR)
        layer2_attn(nc, p2, XR)
        layer2_ffn(nc, p2, XR)
        layer3_attn(nc, p3, XR)
        layer3_ffn(nc, p3f, w1, w2, XR, out)


def _pack(np, names, parts):
    at, width = places(names)
    out = np.zeros((P, width), np.float32)
    for name, part in parts.items():
        for row, col, a in part if isinstance(part, list) else [(0, 0, part)]:
            a = np.asarray(a)
            a = a.reshape(-1, 1) if a.ndim == 1 else a
            out[row:row + a.shape[0], at[name][0] + col:at[name][0] + col + a.shape[1]] = a
    return out


def _common(np):
    return {"ident": np.eye(P), "ones": np.full((P, P), 1.0 / P), "center": np.eye(P) - 1.0 / P,
            "eps": np.full(P, 1e-5)}


def _pack0(np, i):
    i = {k[len("L0_conv_"):]: np.asarray(v) for k, v in i.items() if k.startswith("L0_")}
    h = HALF
    shuffled = lambda a: a.reshape(2, h, -1).swapaxes(0, 1).reshape(P, -1)
    parts = dict(_common(np))
    parts["cv12"] = [(0, 0, i["cv2_w"].T), (h, h, i["cv1_w"].T)]
    for c in ("c1", "c2"):
        parts[c] = [(0, t * P, i[c + "_w"][t // 3, t % 3]) for t in range(9)]
    parts["c3"] = [(0, 0, i["c3_w"].T)]
    parts["in_xh"] = [(h, 0, i["in_proj_w"][:P].T)]
    parts["in_z"] = [(h, 0, i["in_proj_w"][P:].T)]
    xp = i["x_proj_w"]
    parts["xp_dt"] = [(0, k * P, xp[k, 0:4]) for k in range(NDIR)]
    parts["dt_w"] = [(0, k * P, i["dt_w"][k].T) for k in range(NDIR)]
    parts["bc"] = [(0, k * 96 + c * 32, xp[k, 4:].T) for k in range(NDIR) for c in range(3)]
    parts["out_proj"] = i["out_proj_w"]
    parts["cv"] = [(0, h, i["cv_w"].T)]
    parts["cv3"] = shuffled(i["cv3_w"]).T
    parts["dw"] = i["dw_w"].reshape(9, P).T
    parts["A_logs"] = i["A_logs"].reshape(NDIR, P, NST).transpose(1, 0, 2).reshape(P, -1)
    parts["Ds"] = i["Ds"].reshape(NDIR, P).T
    parts["dt_b"] = i["dt_b"].T
    parts["one"], parts["minus_one"] = np.ones((P, 1)), -np.ones((P, 1))
    for c in "gb":
        parts["cv12_" + c] = [(0, 0, i["cv2_" + c]), (h, 0, i["cv1_" + c])]
        parts["cv3_" + c] = shuffled(i["cv3_" + c])
        parts["cv_" + c] = [(h, 0, i["cv_" + c])]
        for n in ("bn0_", "bn1_", "bn2_", "ln_"):
            parts[n + c] = i[n + c]
    for n in ("c1_b", "c2_b", "c3_b", "dw_b"):
        parts[n] = i[n]
    return _pack(np, PACK0, parts)


def _selectors(np):
    out = np.zeros((96, 2 * NST, P), mybir.dt.np(BF16))
    for r in range(2 * NST):
        out[[r, 32 + r, 64 + r], r] = 1
    return out.reshape(96, -1)


def _pack1(np, i):
    i = {k[len("L1_conv_"):]: np.asarray(v) for k, v in i.items() if k.startswith("L1_")}
    parts = dict(_common(np))
    parts["group4"] = np.kron(np.eye(P // 4), np.full((4, 4), 0.25))
    names = ("a", "b", "ga", "gb")
    parts["ab"] = [(0, n * P, i["W" + s]) for n, s in enumerate(names)]
    parts["ab_b"] = [(0, n * P, np.broadcast_to(i["b" + s], (P, P))) for n, s in enumerate(names)]
    parts["g"], parts["o"] = i["Wg"], i["Wo"]
    for n in ("ln1_g", "ln1_b", "ln2_g", "ln2_b", "bg", "bo"):
        parts[n] = i[n]
    return _pack(np, PACK1, parts)


def _pack2(np, i):
    a = {k[len("L2_attn_"):]: np.asarray(v) for k, v in i.items() if k.startswith("L2_attn_")}
    f = {k[len("L2_ffn_"):]: np.asarray(v) for k, v in i.items() if k.startswith("L2_ffn_")}
    parts = dict(_common(np))
    parts["heads"] = np.kron(np.eye(4), np.full((32, 32), 32 ** -0.5))
    q, k, v = a["W_qkv"].reshape(3, P, P)
    parts["k"], parts["qv"], parts["out"] = k.T, [(0, 0, q.T), (0, P, v.T)], a["W_out"].T
    parts["b_out"], parts["gn_w"], parts["gn_b"] = a["b_out"], a["gn_w"], a["gn_b"]
    parts["router"] = f["router_w"]
    parts["router_b"] = np.broadcast_to(np.concatenate([f["router_b"]] * 4), (P, 4 * NEXP2))
    parts["experts"] = f["expert_w"].transpose(1, 0, 2).reshape(P, -1)
    parts["expert_b"] = [(0, 0, f["expert_b"])]
    return _pack(np, PACK2, parts)


def _pack3(np, i):
    a = {k[len("L3_attn_"):]: np.asarray(v) for k, v in i.items() if k.startswith("L3_attn_")}
    parts = dict(_common(np))
    parts["upto"] = np.triu(np.ones((P, P)))
    parts["last"] = [(P - 1, 0, np.ones((1, P)))]
    kv = a["W_kv"].reshape(HD, P, 2, P)
    parts["k"], parts["v"] = (kv[:, :, n].transpose(2, 0, 1).reshape(P, -1) for n in range(2))
    parts["q"] = [(0, h * (2 * P - 1) + P - 1, a["q_proj"][h]) for h in range(HD)]
    return _pack(np, PACK3, parts)


def _pack3f(np, i):
    f = {k[len("L3_ffn_"):]: np.asarray(v) for k, v in i.items() if k.startswith("L3_ffn_")}
    parts = dict(_common(np))
    parts["gate"] = [(0, 0, f["gate_w"].T), (0, P + HALF, f["gate_w"].T)]
    parts["gate_b"] = np.concatenate([f["gate_b"]] * 2)
    parts["b1"] = f["weight1"][:, P].reshape(NEXP3, HID // P, P).transpose(2, 0, 1).reshape(P, -1)
    parts["b2"] = f["weight2"][:, HID].T
    return _pack(np, PACK3F, parts)


def _experts(np, i):
    w1, w2 = np.asarray(i["L3_ffn_weight1"])[:, :P], np.asarray(i["L3_ffn_weight2"])[:, :HID]
    return {"w1": np.ascontiguousarray(w1.transpose(1, 0, 2)),
            "w2": np.ascontiguousarray(w2.reshape(NEXP3, HID // P, P, P).transpose(2, 0, 1, 3))}


def kernel(**inputs):
    import numpy as np
    import concourse.bacc as bacc
    from concourse.bass_utils import run_bass_kernel_spmd

    x = np.asarray(inputs["x"])
    arrays = {
        "xT": np.ascontiguousarray(x.reshape(NTOK, P).T),
        "p0": _pack0(np, inputs), "sel": _selectors(np), "p1": _pack1(np, inputs), "p2": _pack2(np, inputs),
        "p3": _pack3(np, inputs), "p3f": _pack3f(np, inputs), **_experts(np, inputs),
    }
    nc = bacc.Bacc("TRN2", target_bir_lowering=False, num_devices=1)
    args = {n: nc.dram_tensor(n, a.shape, mybir.dt.from_np(a.dtype), kind="ExternalInput").ap()
            for n, a in arrays.items()}
    args["out"] = nc.dram_tensor("out", (P, NTOK), F32, kind="ExternalOutput").ap()
    program(nc, **args)
    r = run_bass_kernel_spmd(nc, [arrays], core_ids=[0])
    return np.ascontiguousarray(r.results[0]["out"].T).reshape(x.shape)
```

```python
from contextlib import ExitStack

import concourse.bass as bass
from concourse import mybir

ALU = mybir.AluOpType
ACT = mybir.ActivationFunctionType
AX_X = mybir.AxisListType.X
F32 = mybir.dt.float32
BF16 = mybir.dt.bfloat16

P = 128
NB, IMG = 4, 64
TOK = IMG * IMG
NTOK = NB * TOK
CH = 512
NCH = TOK // CH
ROWS = CH // IMG
PAD = IMG + 2
HALF = P // 2
NDIR, NST = 4, 16
NEXP2, TOP2 = 8, 2
HD = 8
NEXP3, HID = 64, 512
BIG = 3.0e38
EXP_LN, SILU = "natural_log_exp_and_others", "silu_and_others"

RING, ERING = 4, 8
HRING = 8
LEAD_B, LEAD_E, LEAD_C = 4, 4, 1

PACK0 = [
    ("ident", P), ("ones", P), ("center", P), ("eps", 1), ("one", 1), ("minus_one", 1),
    ("cv12", P), ("cv2", P), ("c1", 6 * P), ("c2", 6 * P), ("c3", P), ("in_xh", P), ("in_z", P),
    ("xp_dt", NDIR * P), ("dt_w", NDIR * P), ("bc", NDIR * 96), ("out_proj", P), ("cv", P), ("cv3", P),
    ("dw", 9), ("A_logs", NDIR * NST), ("Ds", NDIR), ("dt_b", NDIR),
    ("cv12_g", 1), ("cv12_b", 1), ("cv2_g", 1), ("cv2_b", 1), ("bn0_g", 1), ("bn0_b", 1), ("bn1_g", 1), ("bn1_b", 1), ("c1_b", 1),
    ("bn2_g", 1), ("bn2_b", 1), ("c2_b", 1), ("c3_b", 1), ("dw_b", 1), ("ln_g", 1), ("ln_b", 1),
    ("cv_g", 1), ("cv_b", 1), ("cv3_g", 1), ("cv3_b", 1),
]
PACK1 = [
    ("ident", P), ("ones", P), ("center", P), ("eps", 1), ("group4", P),
    ("ab", 4 * P), ("ab_b", 4 * P), ("g", P), ("o", P),
    ("ln1_g", 1), ("ln1_b", 1), ("ln2_g", 1), ("ln2_b", 1), ("bg", 1), ("bo", 1),
]
PACK2 = [
    ("ident", P), ("ones", P), ("center", P), ("eps", 1), ("heads", P),
    ("k", P), ("qv", 2 * P), ("out", P), ("b_out", 1), ("gn_w", 1), ("gn_b", 1),
    ("router", NEXP2), ("router_b", 4 * NEXP2), ("experts", NEXP2 * P), ("expert_b", P),
]
PACK3 = [
    ("ident", P), ("ones", P), ("center", P), ("eps", 1), ("upto", P), ("last", P),
    ("k", HD * P), ("v", HD * P), ("q", HD * (2 * P - 1)),
]
PACK3F = [
    ("ident", P), ("ones", P), ("center", P), ("eps", 1),
    ("gate", 2 * P), ("gate_b", 1), ("b1", NEXP3 * 4), ("b2", NEXP3),
]


def places(pack):
    at, out = 0, {}
    for name, width in pack:
        out[name] = (at, width)
        at += width
    return out, at


def semaphores(nc, ctx, prefix):
    held = []

    def sem(name):
        held.append(nc.alloc_semaphore(name=prefix + name))
        return held[-1]

    def close():
        nc.clear_and_free_semaphores(held)
        nc.all_engine_barrier()

    ctx.callback(close)
    return sem


def layer0(nc, xT, pack, sel, x1):
    with ExitStack() as ctx:
        def sb(name, shape, dt=F32):
            return ctx.enter_context(nc.sbuf_tensor("l0_" + name, shape, dt))

        sem = semaphores(nc, ctx, "l0_")

        where, width = places(PACK0)
        W = sb("W", [P, width])

        def w(name, a=0, n=None):
            at, size = where[name]
            return W[:, at + a:at + (size if n is None else a + n)]

        SEL = sb("SEL", [96, 2 * NST * P], BF16)
        WDT = sb("WDT", [P, NDIR * P])
        WCV = sb("WCV", [P, P])
        A = sb("A", [P, NDIR * NST])
        NIL, PNIL = sb("NIL", [P, 1]), sb("PNIL", [P, 1])
        VEC = sb("VEC", [P, 4])
        LX = sb("LX", [P, TOK])
        Z = sb("Z", [P, TOK])
        YA = sb("YA", [P, PAD * PAD])
        YB = sb("YB", [P, TOK + CH])
        XH = sb("XH", [P, TOK + CH])
        XC = sb("XC", [P, TOK])
        H = sb("H", [P, (HRING + 1) * CH])
        HL = sb("HL", [P, NDIR * NST])
        BS, DBU, HC = (sb(n, [P, RING, CH]) for n in ("BS", "DBU", "HC"))
        DA = sb("DA", [P, ERING * CH])
        DL = sb("DL", [P, 2, CH])
        DU = sb("DU", [P, CH])
        S = sb("S", [96, 2, CH], BF16)
        TE, TU, TL, TP, TR = (sb(n, [P, CH]) for n in ("TE", "TU", "TL", "TP", "TR"))
        RS = H[0:HALF, HRING * CH:(HRING + 1) * CH]
        PS = ctx.enter_context(nc.psum_tensor("l0_PS", [P, 8, CH], F32))
        B_BANK, C_BANK, Y_BANK, DT_BANK, BC_BANK = 0, 2, 4, 6, 7

        X = H[:, 0:TOK]
        C2 = LX
        AB = XC
        P1 = YA[:, :].rearrange("p (h w) -> p h w", h=PAD)
        P2 = YB[:, 0:PAD * PAD].rearrange("p (h w) -> p h w", h=PAD)
        PH = H[:, 0:PAD * PAD].rearrange("p (h w) -> p h w", h=PAD)
        XCv = XC[:, 0:TOK].rearrange("p (w h) -> p h w", h=IMG)
        YBv = YB[:, 0:TOK].rearrange("p (w h) -> p h w", h=IMG)

        loaded = sem("loaded")
        x_in, r_in = sem("x_in"), sem("r_in")
        x_out = sem("x_out")
        setup_pe, setup_act, setup_dve = sem("setup_pe"), sem("setup_act"), sem("setup_dve")
        padded = sem("padded")
        bn0_done = sem("bn0_done")
        dw_up = sem("dw_up")
        dw_acc = sem("dw_acc")
        mm = sem("mm")
        ev = sem("ev")
        b_up, b_sb = sem("b_up"), sem("b_sb")
        dbu_up = sem("dbu_up")
        da_up = sem("da_up")
        scanned = sem("scanned")
        c_up = sem("c_up")
        hc_up = sem("hc_up")
        y_up = sem("y_up")
        pd_up, pb_up = sem("pd_up"), sem("pb_up")
        e_up, ln_up = sem("e_up"), sem("ln_up")
        ab_up = sem("ab_up")
        relu_up = sem("relu_up")
        u_up, t_up = sem("u_up"), sem("t_up")
        lp = sem("lp")
        dl_up, du_up = sem("dl_up"), sem("du_up")
        s_hi, s_mid, s_lo, r_up = sem("s_hi"), sem("s_mid"), sem("s_lo"), sem("r_up")
        y_out = sem("y_out")
        y_init = sem("y_init")
        hl_up = sem("hl_up")
        ln_pe, ln_act, ln_dve = sem("ln_pe"), sem("ln_act"), sem("ln_dve")
        ln_w = sem("ln_w")
        res = sem("res")

        NGA = 8 * NCH
        PREPS = NCH * NDIR + 1
        UNITS = NCH * NDIR * NST
        TAKES = NCH * NDIR + 1
        ADDS = UNITS + 2

        block = ctx.enter_context(nc.Block())

        @block.sync
        def _(sp):
            sp.dma_start(W[:, :], pack).then_inc(loaded, 16)
            sp.dma_start(SEL[:, :], sel).then_inc(loaded, 16)
            sp.sem_inc(x_out, 16)
            sp.dma_start(X, xT[:, 0:TOK]).then_inc(x_in, 16)

            def again(b):
                sp.wait_ge(ln_dve, (b + 1) * 16)
                sp.dma_start(XC[:, :], xT[:, bass.ds(b * TOK, TOK)]).then_inc(r_in, 16)

            def result(b):
                sp.wait_ge(res, (b + 1) * NCH + 1)
                sp.dma_start(x1[:, bass.ds(b * TOK, TOK)], Z[:, :]).then_inc(x_out, 16)

            with sp.Fori(0, NB - 1) as b:
                again(b)
                sp.dma_start(X, xT[:, bass.ds((b + 1) * TOK, TOK)]).then_inc(x_in, 16)
                result(b)
            again(NB - 1)
            result(NB - 1)
            sp.wait_ge(x_out, (NB + 1) * 16)

        def conv(pe, src, taps, bank, row):
            for t in range(6):
                ins = nc.tensor.matmul(PS[:, bank, :], taps[:, t * P:(t + 1) * P],
                                       src[:, bass.ds(row + t // 3 * 2, ROWS), t % 3:t % 3 + IMG],
                                       start=(t == 0), stop=(t == 5))
            return ins

        @block.tensor
        def _(pe):
            pe.wait_ge(loaded, 32)
            for k in range(NDIR):
                nc.tensor.matmul(PS[:, 0, k * P:(k + 1) * P], w("xp_dt", k * P, P)[0:4, :],
                                 w("dt_w", k * P, P)[0:4, :], start=True, stop=True)
            nc.tensor.matmul(PS[:, 1, 0:P], w("out_proj")[0:HALF, :], w("cv")[0:HALF, :],
                             start=True, stop=True).then_inc(setup_pe, 1)
            pe.wait_ge(setup_dve, 6)
            pe.wait_ge(setup_act, 3)

            with pe.Fori(0, NB) as b:
                def ring(stage, j, u):
                    pe.wait_ge(ev, b * NGA + stage * NCH + j * 2 + u + 1)

                def stage_done(stage):
                    pe.wait_ge(ev, b * NGA + stage * NCH + 2)

                with pe.Fori(0, NCH // 2) as j:
                    for u in range(2):
                        pe.wait_ge(x_in, (b + 1) * 16)
                        ring(0, j, u)
                        nc.tensor.matmul(PS[:, 2 + u, :], w("cv2"), X[:, bass.ds((j * 2 + u) * CH, CH)],
                                         start=True, stop=True)
                        nc.tensor.matmul(PS[:, u, :], w("cv12"), X[:, bass.ds((j * 2 + u) * CH, CH)],
                                         start=True, stop=True).then_inc(mm, 1)
                for stage, name in ((1, "in_xh"), (2, "in_z")):
                    with pe.Fori(0, NCH // 2) as j:
                        for u in range(2):
                            ring(stage, j, u)
                            nc.tensor.matmul(PS[:, u, :], w(name), AB[:, bass.ds((j * 2 + u) * CH, CH)],
                                             start=True, stop=True).then_inc(mm, 1)
                with pe.Fori(0, NCH // 2) as j:
                    for u in range(2):
                        pe.wait_ge(bn0_done, (b + 1) * NCH)
                        ring(3, j, u)
                        conv(pe, P1, w("c1"), u, (j * 2 + u) * ROWS).then_inc(mm, 1)
                with pe.Fori(0, NCH // 2) as j:
                    for u in range(2):
                        stage_done(4)
                        ring(4, j, u)
                        conv(pe, P2, w("c2"), u, (j * 2 + u) * ROWS).then_inc(mm, 1)
                with pe.Fori(0, NCH // 2) as j:
                    for u in range(2):
                        stage_done(5)
                        ring(5, j, u)
                        nc.tensor.matmul(PS[:, u, :], w("c3"), C2[:, bass.ds((j * 2 + u) * CH, CH)],
                                         start=True, stop=True).then_inc(mm, 1)
                stage_done(6)
                pe.wait_ge(dw_up, (b + 1) * NCH)

                def delta_arg(k, at, n):
                    nc.tensor.matmul(PS[:, DT_BANK, :], WDT[:, k * P:(k + 1) * P],
                                     (XH if k % 2 == 0 else XC)[:, bass.ds(at, CH)],
                                     start=True, stop=False)
                    nc.tensor.matmul(PS[:, DT_BANK, :], w("ident"), w("dt_b", k, 1).to_broadcast([P, CH]),
                                     start=False, stop=True).then_inc(pd_up, 1)

                def b_and_c(k, at, n):
                    nc.tensor.matmul(PS[0:96, BC_BANK, :], w("bc", k * 96, 96),
                                     (XH if k % 2 == 0 else XC)[:, bass.ds(at, CH)],
                                     start=True, stop=True).then_inc(pb_up, 1)

                def bcast_b(k, n, i):
                    pe.wait_ge(b_sb, b * (UNITS + LEAD_B) + i + 1)
                    nc.tensor.matmul(PS[:, B_BANK + n % 2, :], SEL[:, n * P:(n + 1) * P],
                                     S[:, k % 2, :], start=True, stop=True).then_inc(b_up, 1)

                def bcast_c(k, n, i):
                    pe.wait_ge(hc_up, b * UNITS + i + 1)
                    nc.tensor.matmul(PS[:, C_BANK + n % 2, :], SEL[:, (NST + n) * P:(NST + n + 1) * P],
                                     S[:, k % 2, :], start=True, stop=True).then_inc(c_up, 1)

                def add_y(k, n, it, i):
                    if n == 0:
                        pe.wait_ge(y_out, b * TAKES + it + 2)
                    pe.wait_ge(hc_up, b * UNITS + i + 1 + 2)
                    nc.tensor.matmul(PS[:, Y_BANK + k % 2, :], w("ident"), HC[:, n % RING, :],
                                     start=(n == 0), stop=(n == NST - 1)).then_inc(y_up, 1)

                delta_arg(0, 0, b * PREPS + 1)
                b_and_c(0, 0, b * PREPS + 1)
                for n in range(LEAD_B):
                    pe.wait_ge(s_lo, b * PREPS + 1)
                    bcast_b(0, n, n)
                bcast_c(0, 0, 0)
                nc.tensor.matmul(PS[:, Y_BANK + 1, :], w("ident"), HC[:, 2, :], start=True, stop=False)
                with pe.Fori(0, NCH) as c:
                    for k in range(NDIR):
                        it = c * NDIR + k
                        i0 = it * NST
                        prep = b * PREPS + c * NDIR + k + 2
                        kn, cn = (k + 1) % NDIR, (c if k < NDIR - 1 else c + 1)
                        nxt = (cn if kn < 2 else (NCH - 1) - cn) * CH
                        for n in range(NST):
                            nb, nc_ = n + LEAD_B, n + LEAD_C
                            if nb == NST:
                                pe.wait_ge(s_lo, prep)
                            bcast_b(k if nb < NST else kn, nb % NST, i0 + nb)
                            if n == 0:
                                pe.wait_ge(ab_up, prep - 1)
                                pe.wait_ge(relu_up, prep - 1)
                                pe.wait_ge(r_up, prep - 1)
                            if n >= 2:
                                add_y(k, n - 2, it, i0 + n - 2)
                            else:
                                add_y((k - 1) % NDIR, NST + n - 2, it - 1, i0 + n - 2)
                            bcast_c(k if nc_ < NST else kn, nc_ % NST, i0 + nc_)
                            if n == 0:
                                delta_arg(kn, nxt, prep)
                            if n == 4:
                                b_and_c(kn, nxt, prep)
                for n in (NST - 2, NST - 1):
                    add_y(NDIR - 1, n, NCH * NDIR - 1, UNITS - NST + n)

                for g in range(2):
                    for i in range(4):
                        pe.wait_ge(b_sb, (b + 1) * (UNITS + LEAD_B) + 2)
                        pe.wait_ge(ln_dve, b * 16 + g * 8 + i + 1)
                        nc.tensor.matmul(PS[:, i, :], w("center"), YA[:, (4 * g + i) * CH:(4 * g + i + 1) * CH],
                                         start=True, stop=True).then_inc(ln_pe, 1)
                    for i in range(4):
                        pe.wait_ge(ln_act, b * 24 + g * 12 + i + 1)
                        pe.wait_ge(r_up, (b + 1) * PREPS)
                        nc.tensor.matmul(PS[:, 4 + i, :], w("ones"), H[:, i * CH:(i + 1) * CH],
                                         start=True, stop=True).then_inc(ln_pe, 1)
                with pe.Fori(0, NCH // 2) as j:
                    for u in range(2):
                        pe.wait_ge(ln_dve, (b + 1) * 16)
                        ring(6, j, u)
                        nc.tensor.matmul(PS[:, u, :], WCV[:, :], YA[:, bass.ds((j * 2 + u) * CH, CH)],
                                         start=True, stop=True).then_inc(mm, 1)
                with pe.Fori(0, NCH // 2) as j:
                    for u in range(2):
                        stage_done(7)
                        ring(7, j, u)
                        nc.tensor.matmul(PS[:, u, :], w("cv3"), LX[:, bass.ds((j * 2 + u) * CH, CH)],
                                         start=True, stop=True).then_inc(mm, 1)
                stage_done(8)

        @block.scalar
        def _(act):
            act.wait_ge(loaded, 32)
            act.sem_inc(ev, 2)
            act.sem_inc(b_sb, 2)
            act.wait_ge(setup_pe, 1)
            nc.scalar.copy(WDT[:, :], PS[:, 0, :]).then_inc(setup_act, 1)
            nc.scalar.copy(WCV[:, :], PS[:, 1, 0:P]).then_inc(setup_act, 1)
            nc.scalar.activation(A[:, :], w("A_logs"), ACT.Exp).then_inc(setup_act, 1)
            act.wait_ge(setup_dve, 3)
            with act.Fori(0, NB) as b:
                def take(stage, body):
                    with act.Fori(0, NCH // 2) as j:
                        for u in range(2):
                            act.wait_ge(mm, b * NGA + stage * NCH + j * 2 + u + 1)
                            body(j * 2 + u, PS[:, u, :]).then_inc(ev, 1)

                def rows(ap):
                    return ap.rearrange("p (h w) -> p h w", w=IMG)

                def inner(buf, j):
                    return buf[:, bass.ds(j * ROWS + 1, ROWS), 1:1 + IMG]

                nc.scalar.preload_act_table_set(SILU)
                act.wait_ge(res, b * NCH + 1)
                with act.Fori(0, NCH // 2) as j:
                    for u in range(2):
                        at = bass.ds((j * 2 + u) * CH, CH)
                        act.wait_ge(mm, b * NGA + j * 2 + u + 1)
                        nc.scalar.activation(AB[:, at], PS[:, u, :], ACT.Silu, scale=w("cv12_g"), bias=w("cv12_b"))
                        nc.scalar.activation(LX[:, at], PS[:, 2 + u, :], ACT.Silu, scale=w("cv2_g"),
                                             bias=w("cv2_b")).then_inc(ev, 1)
                take(1, lambda j, ps: nc.scalar.copy(inner(PH, j), rows(ps)))
                act.wait_ge(x_out, (b + 1) * 16)
                take(2, lambda j, ps: nc.scalar.activation(Z[:, bass.ds(j * CH, CH)], ps, ACT.Silu))
                act.wait_ge(padded, (b + 1) * 6)
                with act.Fori(0, NCH // 2) as j:
                    for u in range(2):
                        act.wait_ge(mm, b * NGA + 3 * NCH + j * 2 + u + 1)
                        for half in range(2):
                            s = slice(half * HALF, (half + 1) * HALF)
                            ins = nc.scalar.activation(
                                P2[s, bass.ds((j * 2 + u) * ROWS + 1 - half, ROWS), 1:1 + IMG],
                                rows(PS[s, u, :]), ACT.Relu, scale=w("bn1_g")[s, :], bias=VEC[s, 0:1])
                        ins.then_inc(ev, 1)
                with act.Fori(0, NCH) as j:
                    act.wait_ge(dw_acc, (b * NCH + j + 1) * 9)
                    x = XH[:, bass.ds(j * CH, CH)]
                    nc.scalar.activation(XCv[:, bass.ds(j * ROWS, ROWS), :], rows(x), ACT.Silu, bias=w("dw_b"))
                    nc.scalar.activation(x, x, ACT.Silu, bias=w("dw_b")).then_inc(dw_up, 1)
                take(4, lambda j, ps: nc.scalar.activation(
                    C2[:, bass.ds(j * CH, CH)], ps, ACT.Relu, scale=w("bn2_g"), bias=VEC[:, 1:2]))
                take(5, lambda j, ps: nc.scalar.activation(
                    LX[0:HALF, bass.ds(j * CH, CH)], ps[0:HALF, :], ACT.Relu, bias=w("c3_b")[0:HALF, :]))

                def absolute(k, n):
                    act.wait_ge(pd_up, n)
                    act.wait_ge(dl_up, n)
                    nc.scalar.activation(TE[:, :], PS[:, DT_BANK, :], ACT.Abs).then_inc(ab_up, 1)

                def exponential(k, n):
                    act.wait_ge(ab_up, n)
                    nc.scalar.activation(TE[:, :], TE[:, :], ACT.Exp, scale=-1.0).then_inc(e_up, 1)

                def one_plus(k, n):
                    act.wait_ge(e_up, n)
                    nc.scalar.activation(TU[:, :], TE[:, :], ACT.Identity, bias=w("one")).then_inc(u_up, 1)

                def minus_one(k, n):
                    act.wait_ge(u_up, n)
                    nc.scalar.activation(TP[:, :], TU[:, :], ACT.Identity, bias=w("minus_one")).then_inc(t_up, 1)

                def logarithm(k, n):
                    act.wait_ge(u_up, n)
                    nc.scalar.activation(TL[:, :], TU[:, :], ACT.Ln).then_inc(ln_up, 1)

                def high(k, n):
                    act.wait_ge(pb_up, n)
                    nc.scalar.copy(S[:, k % 2, :], PS[0:96, BC_BANK, :]).then_inc(s_hi, 1)

                def middle(k, n):
                    act.wait_ge(r_up, n)
                    nc.scalar.copy(S[0:HALF, k % 2, :], RS).then_inc(s_mid, 1)

                def take_b(k, n, i):
                    act.wait_ge(b_up, b * (UNITS + LEAD_B) + i + 1)
                    act.wait_ge(dbu_up, b * UNITS + i + 1)
                    nc.scalar.copy(BS[:, n % RING, :], PS[:, B_BANK + n % 2, :]).then_inc(b_sb, 1)

                def exp_a(k, n, i):
                    act.wait_ge(scanned, b * UNITS + i + 1)
                    nc.scalar.activation(DA[:, n % ERING * CH:(n % ERING + 1) * CH], DL[:, k % 2, :], ACT.Exp,
                                         scale=A[:, k * NST + n:k * NST + n + 1]).then_inc(da_up, 1)

                nc.scalar.preload_act_table_set(EXP_LN)
                first = b * PREPS + 1
                absolute(0, first)
                exponential(0, first)
                one_plus(0, first)
                minus_one(0, first)
                high(0, first)
                logarithm(0, first)
                middle(0, first)
                for n in range(LEAD_B):
                    take_b(0, n, n)
                for n in range(LEAD_E):
                    act.wait_ge(dl_up, first + 1)
                    exp_a(0, n, n)
                with act.Fori(0, NCH) as c:
                    for k in range(NDIR):
                        i0 = (c * NDIR + k) * NST
                        prep = b * PREPS + c * NDIR + k + 2
                        kn = (k + 1) % NDIR
                        for n in range(NST):
                            nb = n + LEAD_B
                            take_b(k if nb < NST else kn, nb % NST, i0 + nb)
                            ne = n + LEAD_E
                            if ne == NST:
                                act.wait_ge(dl_up, prep + 1)
                            exp_a(k if ne < NST else kn, ne % NST, i0 + ne)
                            for at, work in ((1, absolute), (2, exponential), (3, one_plus), (4, minus_one),
                                             (5, high), (6, logarithm), (7, middle)):
                                if n == at:
                                    work(kn, prep)

                for g in range(2):
                    for i in range(4):
                        act.wait_ge(ln_pe, b * 16 + g * 8 + i + 1)
                        nc.scalar.activation(H[:, i * CH:(i + 1) * CH], PS[:, i, :],
                                             ACT.Square).then_inc(ln_act, 1)
                    for i in range(4):
                        act.wait_ge(ln_pe, b * 16 + g * 8 + 4 + i + 1)
                        nc.scalar.activation(H[:, (4 + i) * CH:(5 + i) * CH], PS[:, 4 + i, :], ACT.Ln,
                                             bias=w("eps")).then_inc(ln_act, 1)
                        act.wait_ge(ln_act, b * 24 + g * 12 + 4 + 2 * i + 1)
                        nc.scalar.activation(H[:, (4 + i) * CH:(5 + i) * CH], H[:, (4 + i) * CH:(5 + i) * CH],
                                             ACT.Exp, scale=-0.5).then_inc(ln_act, 1)
                nc.scalar.preload_act_table_set(SILU)
                take(6, lambda j, ps: nc.scalar.activation(
                    LX[HALF:P, bass.ds(j * CH, CH)], ps[HALF:P, :], ACT.Silu,
                    scale=w("cv_g")[HALF:P, :], bias=w("cv_b")[HALF:P, :]))
                take(7, lambda j, ps: nc.scalar.activation(
                    Z[:, bass.ds(j * CH, CH)], ps, ACT.Silu, scale=w("cv3_g"), bias=w("cv3_b")))

        @block.gpsimd
        def _(pool):
            pool.sem_inc(dbu_up, RING)
            pool.sem_inc(dl_up, 1)
            pool.wait_ge(loaded, 32)
            with pool.Fori(0, NB) as b:
                def plus_e(n):
                    pool.wait_ge(e_up, n)
                    pool.wait_ge(relu_up, n)
                    nc.gpsimd.tensor_tensor(TP[:, :], TE[:, :], TR[:, :], ALU.add).then_inc(lp, 1)

                def delta(k, n):
                    pool.wait_ge(ln_up, n)
                    pool.wait_ge(lp, n)
                    nc.gpsimd.tensor_tensor(DL[:, k % 2, :], TP[:, :], TL[:, :], ALU.add).then_inc(dl_up, 1)

                def delta_u(k, at, n):
                    pool.wait_ge(dl_up, n + 1)
                    nc.gpsimd.tensor_tensor(PNIL[:, :], w("eps"), w("eps"), ALU.mult)
                    nc.gpsimd.tensor_tensor(DU[:, :], DL[:, k % 2, :],
                                            (XH if k % 2 == 0 else XC)[:, bass.ds(at, CH)],
                                            ALU.mult).then_inc(du_up, 1)

                first = b * PREPS + 1
                plus_e(first)
                delta(0, first)
                delta_u(0, 0, first)
                with pool.Fori(0, NCH) as c:
                    for k in range(NDIR):
                        i0 = (c * NDIR + k) * NST
                        prep = b * PREPS + c * NDIR + k + 2
                        kn, cn = (k + 1) % NDIR, (c if k < NDIR - 1 else c + 1)
                        nxt = (cn if kn < 2 else (NCH - 1) - cn) * CH
                        pool.wait_ge(du_up, prep - 1)
                        for n in range(NST):
                            pool.wait_ge(b_sb, b * (UNITS + LEAD_B) + i0 + n + 1 + 2)
                            pool.wait_ge(scanned, b * UNITS + i0 + n + 1 - RING + ERING)
                            nc.gpsimd.tensor_tensor(DBU[:, n % RING, :], BS[:, n % RING, :], DU[:, :],
                                                    ALU.mult).then_inc(dbu_up, 1)
                            if n == 9:
                                plus_e(prep)
                            if n == 11:
                                delta(kn, prep)
                        pool.wait_ge(dbu_up, b * UNITS + i0 + NST + RING)
                        delta_u(kn, nxt, prep)

        @block.vector
        def _(dve):
            dve.wait_ge(loaded, 32)
            dve.sem_inc(scanned, ERING)
            dve.sem_inc(hc_up, 2)
            dve.sem_inc(res, 1)
            dve.sem_inc(y_up, RING)
            dve.sem_inc(y_out, 2)
            nc.vector.scalar_tensor_tensor(VEC[:, 0:1], w("c1_b"), w("bn1_g"), w("bn1_b"), ALU.mult,
                                           ALU.add).then_inc(setup_dve, 1)
            nc.vector.scalar_tensor_tensor(VEC[:, 1:2], w("c2_b"), w("bn2_g"), w("bn2_b"), ALU.mult,
                                           ALU.add).then_inc(setup_dve, 1)
            dve.wait_ge(setup_act, 3)
            nc.vector.tensor_scalar(A[:, :], A[:, :], -1.0, None, ALU.mult).then_inc(setup_dve, 1)
            nc.vector.tensor_reduce(VEC[:, 2:3], w("Ds"), AX_X, ALU.add).then_inc(setup_dve, 1)
            nc.vector.memset(XH[:, TOK:TOK + CH], 0.0).then_inc(setup_dve, 1)
            nc.vector.memset(HC[:, 2:4, :], 0.0).then_inc(setup_dve, 1)
            dve.wait_ge(setup_dve, 6)

            with dve.Fori(0, NB) as b:
                nc.vector.memset(YA[:, :], 0.0).then_inc(padded, 1)
                nc.vector.memset(YB[:, :], 0.0).then_inc(padded, 1)
                nc.vector.memset(HL[:, :], 0.0).then_inc(hl_up, 1)
                with dve.Fori(0, NCH) as j:
                    dve.wait_ge(padded, b * 6 + 2)
                    dve.wait_ge(ev, b * NGA + j + 1 + 2)
                    for half in range(2):
                        s = slice(half * HALF, (half + 1) * HALF)
                        ins = nc.vector.tensor_scalar(P1[s, bass.ds(j * ROWS + 1 - half, ROWS), 1:1 + IMG],
                                                      LX[s, bass.ds(j * CH, CH)].rearrange("p (h w) -> p h w", w=IMG),
                                                      w("bn0_g")[s, :], w("bn0_b")[s, :], ALU.mult, ALU.add)
                    ins.then_inc(bn0_done, 1)
                for edge in (PH[:, 0, :], PH[:, PAD - 1, :], PH[:, 1:PAD - 1, 0], PH[:, 1:PAD - 1, PAD - 1]):
                    nc.vector.memset(edge, 0.0).then_inc(padded, 1)
                with dve.Fori(0, NCH) as j:
                    acc = XH[:, bass.ds(j * CH, CH)].rearrange("p (h w) -> p h w", w=IMG)
                    n0 = (b * NCH + j) * 9
                    dve.wait_ge(padded, (b + 1) * 6)
                    dve.wait_ge(ev, b * NGA + 2 * NCH + 2)
                    for t in range(9):
                        tap = PH[:, bass.ds(j * ROWS + t // 3, ROWS), t % 3:t % 3 + IMG]
                        if t == 0:
                            ins = nc.vector.tensor_scalar(acc, tap, w("dw", t, 1), None, ALU.mult)
                        else:
                            dve.wait_ge(dw_acc, n0 + t)
                            ins = nc.vector.scalar_tensor_tensor(acc, tap, w("dw", t, 1), acc, ALU.mult, ALU.add)
                        ins.then_inc(dw_acc, 1)
                dve.wait_ge(dw_up, (b + 1) * NCH)
                nc.vector.tensor_scalar(YA[:, 0:TOK], XH[:, 0:TOK], VEC[:, 2:3], None,
                                        ALU.mult).then_inc(y_init, 1)
                dve.wait_ge(mm, b * NGA + 5 * NCH)
                nc.vector.memset(YB[:, :], 0.0).then_inc(y_init, 1)
                dve.wait_ge(y_init, (b + 1) * 2)
                dve.wait_ge(hl_up, b * (NCH * NDIR * 2 + 1) + 1)

                def relu(k, n):
                    dve.wait_ge(ab_up, n)
                    dve.wait_ge(t_up, n)
                    nc.vector.scalar_tensor_tensor(TR[:, :], PS[:, DT_BANK, :], 0.0, TP[:, :], ALU.max,
                                                   ALU.subtract).then_inc(relu_up, 1)

                def rest(k, n):
                    dve.wait_ge(pb_up, n)
                    dve.wait_ge(s_hi, n)
                    nc.vector.tensor_tensor(RS, PS[0:HALF, BC_BANK, :], S[0:HALF, k % 2, :],
                                            ALU.subtract).then_inc(r_up, 1)

                def low(k, n):
                    dve.wait_ge(s_mid, n)
                    dve.wait_ge(r_up, n)
                    nc.vector.tensor_tensor(S[0:32, k % 2, :], RS[0:32], S[0:32, k % 2, :],
                                            ALU.subtract).then_inc(s_lo, 1)

                relu(0, b * PREPS + 1)
                rest(0, b * PREPS + 1)
                low(0, b * PREPS + 1)
                with dve.Fori(0, NCH) as c:
                    for k in range(NDIR):
                        it = (b * NCH + c) * NDIR + k
                        i0 = (c * NDIR + k) * NST
                        u0 = it * NST
                        prep = b * PREPS + c * NDIR + k + 2
                        kn = (k + 1) % NDIR
                        turn = -1 if k >= 2 else 1
                        end = 0 if k >= 2 else CH - 1

                        def times_c(n):
                            dve.wait_ge(scanned, u0 + n + 1 + ERING)
                            dve.wait_ge(c_up, b * (UNITS + LEAD_C) + i0 + n + 1)
                            dve.wait_ge(y_up, b * ADDS + i0 + n + 3)
                            nc.vector.tensor_tensor(HC[:, n % RING, :], H[:, n % HRING * CH:(n % HRING + 1) * CH],
                                                    PS[:, C_BANK + n % 2, :], ALU.mult).then_inc(hc_up, 1)

                        def take_y(k, chunk, last):
                            y_sum = YA if k % 2 == 0 else YB
                            at = chunk * CH
                            dve.wait_ge(y_out, b * TAKES + last + 3)
                            dve.wait_ge(y_up, b * ADDS + 2 + (last + 1) * NST + RING)
                            nc.vector.memset(NIL[:, :], 0.0)
                            nc.vector.tensor_tensor(y_sum[:, bass.ds(at, CH)], y_sum[:, bass.ds(at, CH)],
                                                    PS[:, Y_BANK + k % 2, :], ALU.add).then_inc(y_out, 1)

                        for n in range(NST):
                            if n == 8:
                                dve.wait_ge(hl_up, it * 2 + b + 2)
                            dve.wait_ge(da_up, b * (UNITS + LEAD_E) + i0 + n + 1)
                            dve.wait_ge(dbu_up, u0 + n + 1 + RING)
                            nc.vector.tensor_tensor_scan(
                                H[:, n % HRING * CH:(n % HRING + 1) * CH][:, ::turn], DA[:, n % ERING * CH:(n % ERING + 1) * CH][:, ::turn],
                                DBU[:, n % RING, :][:, ::turn], HL[:, k * NST + n:k * NST + n + 1],
                                ALU.mult, ALU.add).then_inc(scanned, 1)
                            if n >= 1:
                                times_c(n - 1)
                            if n % HRING == HRING - 1:
                                dve.wait_ge(scanned, u0 + n + 1 + ERING)
                                nc.vector.tensor_copy(
                                    HL[:, k * NST + n + 1 - HRING:k * NST + n + 1],
                                    H[:, 0:HRING * CH].rearrange("p (n t) -> p n t", n=HRING)[:, :, end]
                                ).then_inc(hl_up, 1)
                            if n == 3:
                                k1, c1 = (k - 1) % NDIR, (c if k > 0 else c - 1)
                                take_y(k1, c1 if k1 < 2 else (NCH - 1) - c1, c * NDIR + k - 1)
                            if n == 6:
                                relu(kn, prep)
                            if n == 7:
                                rest(kn, prep)
                            if n == 11:
                                low(kn, prep)
                        times_c(NST - 1)
                        dve.wait_ge(hl_up, it * 2 + b + 3)
                take_y(NDIR - 1, 0, NCH * NDIR - 1)
                dve.wait_ge(y_out, (b + 1) * TAKES + 2)

                for g in range(2):
                    for i in range(4):
                        j = 4 * g + i
                        yj = YA[:, j * CH:(j + 1) * CH]
                        nc.vector.tensor_tensor(yj.rearrange("p (h w) -> p h w", w=IMG),
                                                yj.rearrange("p (h w) -> p h w", w=IMG),
                                                YBv[:, j * ROWS:(j + 1) * ROWS, :], ALU.add).then_inc(ln_dve, 1)
                    for i in range(4):
                        j = 4 * g + i
                        yj = YA[:, j * CH:(j + 1) * CH]
                        dve.wait_ge(ln_act, b * 24 + g * 12 + 4 + 2 * i + 2)
                        dve.wait_ge(ln_pe, b * 16 + g * 8 + 4 + i + 1)
                        nc.vector.scalar_tensor_tensor(H[:, (4 + i) * CH:(5 + i) * CH], PS[:, i, :], w("ln_g"),
                                                       H[:, (4 + i) * CH:(5 + i) * CH], ALU.mult,
                                                       ALU.mult).then_inc(ln_w, 1)
                        dve.wait_ge(ln_w, b * 8 + g * 4 + i + 1)
                        nc.vector.scalar_tensor_tensor(yj, H[:, (4 + i) * CH:(5 + i) * CH], w("ln_b"),
                                                       Z[:, j * CH:(j + 1) * CH], ALU.add,
                                                       ALU.mult).then_inc(ln_dve, 1)
                with dve.Fori(0, NCH) as j:
                    dve.wait_ge(r_in, (b + 1) * 16)
                    dve.wait_ge(ev, b * NGA + 7 * NCH + j + 1 + 2)
                    nc.vector.tensor_tensor(Z[:, bass.ds(j * CH, CH)], XC[:, bass.ds(j * CH, CH)],
                                            Z[:, bass.ds(j * CH, CH)], ALU.add).then_inc(res, 1)


class Norm:

    def __init__(self, nc, sem, PS, SQ, RST, center, ones, eps):
        self.nc, self.PS, self.SQ, self.RST = nc, PS, SQ, RST
        self.center, self.ones, self.eps = center, ones, eps
        self.centred, self.squared, self.meaned = sem("n_centred"), sem("n_squared"), sem("n_meaned")
        self.logged, self.scaled, self.out = sem("n_logged"), sem("n_scaled"), sem("n_out")

    def begin(self, dve):
        dve.sem_inc(self.out, 4)

    def pe(self, pe, n0, src, ready):
        for i in range(4):
            ready(i)
            pe.wait_ge(self.out, n0 + i + 1)
            self.nc.tensor.matmul(self.PS[:, i, :], self.center, src(i), start=True,
                                  stop=True).then_inc(self.centred, 1)
        for i in range(4):
            pe.wait_ge(self.squared, n0 + i + 1)
            self.nc.tensor.matmul(self.PS[:, 4 + i, :], self.ones, self.SQ[:, i, :], start=True,
                                  stop=True).then_inc(self.meaned, 1)

    def act(self, act, n0):
        for i in range(4):
            act.wait_ge(self.centred, n0 + i + 1)
            self.nc.scalar.activation(self.SQ[:, i, :], self.PS[:, i, :], ACT.Square).then_inc(self.squared, 1)
        for i in range(4):
            act.wait_ge(self.meaned, n0 + i + 1)
            self.nc.scalar.activation(self.RST[:, i, :], self.PS[:, 4 + i, :], ACT.Ln,
                                      bias=self.eps).then_inc(self.logged, 1)
            act.wait_ge(self.logged, n0 + i + 1)
            self.nc.scalar.activation(self.RST[:, i, :], self.RST[:, i, :], ACT.Exp,
                                      scale=-0.5).then_inc(self.scaled, 1)

    def dve(self, dve, n0, dst, gain=None):
        for i in range(4):
            dve.wait_ge(self.scaled, n0 + i + 1)
            if gain is None:
                self.nc.vector.tensor_tensor(dst(i), self.PS[:, i, :], self.RST[:, i, :],
                                             ALU.mult).then_inc(self.out, 1)
            else:
                self.nc.vector.scalar_tensor_tensor(dst(i), self.PS[:, i, :], gain, self.RST[:, i, :],
                                                    ALU.mult, ALU.mult).then_inc(self.out, 1)


def layer1(nc, x1, pack, XR):
    with ExitStack() as ctx:
        def sb(name, shape, dt=F32):
            return ctx.enter_context(nc.sbuf_tensor("l1_" + name, shape, dt))

        sem = semaphores(nc, ctx, "l1_")

        where, width = places(PACK1)
        W = sb("W", [P, width])

        def w(name, a=0, n=None):
            at, size = where[name]
            return W[:, at + a:at + (size if n is None else a + n)]

        PAIR = 2 * TOK
        G = sb("G", [P, IMG, 2, IMG])
        AB = sb("AB", [P, 2, IMG, P])
        SQ = sb("SQ", [P, 4, CH])
        RST = sb("RST", [P, 4, CH])
        OT = sb("OT", [P, 4, CH])
        T = sb("T", [P, 2, CH])
        SG = sb("SG", [P, 2, 2 * P])
        ST = sb("ST", [P, NCH, 6])
        MV = sb("MV", [P, NB, 2])
        GM = sb("GM", [P, NB, 2])
        PS = ctx.enter_context(nc.psum_tensor("l1_PS", [P, 8, CH], F32))

        x_in = [sem("x_in%d" % b) for b in range(NB)]
        loaded = sem("loaded")
        stats, group, gstat, glog = sem("stats"), sem("group"), sem("gstat"), sem("glog")
        gn_up = sem("gn_up")
        zn_up = sem("zn_up")
        ab_mm, ab_t, ab_s, ab_up = sem("ab_mm"), sem("ab_t"), sem("ab_s"), sem("ab_up")
        g_mm, g_up = sem("g_mm"), sem("g_up")
        o_mm = sem("o_mm")
        o_act, o_dve = sem("o_act"), sem("o_dve")
        t_up, t_out = sem("t_up"), sem("t_out")
        on_up, wo_mm, y_gate, y_up = sem("on_up"), sem("wo_mm"), sem("y_gate"), sem("y_up")
        norm = Norm(nc, sem, PS, SQ, RST, w("center"), w("ones"), w("eps"))

        def chunk(q):
            return G[:, :, :, :].rearrange("p i m k -> p (i m k)")[:, bass.ds(q * CH, CH)]

        NCOL = P // 8
        block = ctx.enter_context(nc.Block())

        @block.sync
        def _(sp):
            sp.dma_start(W[:, :], pack).then_inc(loaded, 16)
            if x1 is not None:
                for b in range(NB):
                    sp.dma_start(XR[:, b * TOK:(b + 1) * TOK], x1[:, b * TOK:(b + 1) * TOK]).then_inc(x_in[b], 16)

        @block.tensor
        def _(pe):
            pe.wait_ge(loaded, 16)
            pe.wait_ge(stats, NB * (NCH + 1) + 2)
            nc.tensor.matmul(PS[:, 0, 0:2 * NB], w("group4"), MV[:, :, :], start=True,
                             stop=True).then_inc(group, 1)
            for pr in range(2):
                pe.wait_ge(gn_up, 2 * (pr + 1))
                with pe.Fori(0, 4) as g:
                    norm.pe(pe, pr * 32 + g * 4, lambda i: chunk(g * 4 + i), lambda i: None)
                pe.wait_ge(zn_up, (pr + 1) * 16)
                for i in range(IMG):
                    pe.wait_ge(ab_t, pr * IMG + i + 1)
                    nc.tensor.matmul(PS[:, i % 2, :], G[:, i, :, :], w("ab"),
                                     start=True, stop=True).then_inc(ab_mm, 1)
                    if i % 4 == 3:
                        q = i // 4
                        pe.wait_ge(g_up, pr * 16 + q + 1)
                        nc.tensor.matmul(PS[:, 2 + q % 2, :], w("g"), chunk(q), start=True,
                                         stop=True).then_inc(g_mm, 1)
                pe.wait_ge(ab_up, (pr + 1) * IMG)
                for c8 in range(NCOL):
                    pe.wait_ge(o_act if c8 % 2 == 0 else o_dve, pr * (NCOL // 2) + c8 // 2 + 1)
                    for c in range(8):
                        for m in range(2):
                            s = slice(m * HALF, (m + 1) * HALF)
                            ins = nc.tensor.matmul(PS[s, 4 + c8 % 2, c * IMG:(c + 1) * IMG],
                                                   AB[s, 0, :, c8 * 8 + c], AB[s, 1, :, c8 * 8 + c],
                                                   start=True, stop=True)
                    ins.then_inc(o_mm, 1)
                pe.wait_ge(o_act, (pr + 1) * (NCOL // 2) + 1)
                pe.wait_ge(o_dve, (pr + 1) * (NCOL // 2) + 1)
                for g in range(4):
                    n0 = pr * 16 + g * 4
                    for i in range(4):
                        pe.wait_ge(y_gate, n0 + i + 1)
                        for j in range(4):
                            ins = nc.tensor.transpose(PS[:, 4 + i, j * P:(j + 1) * P],
                                                      AB[:, 0, (g * 4 + i) * 4 + j, :], w("ident"))
                        ins.then_inc(t_up, 1)
                    norm.pe(pe, pr * 32 + 16 + g * 4, lambda i: OT[:, i, :],
                            lambda i: pe.wait_ge(t_out, n0 + i + 1))
                    for i in range(4):
                        pe.wait_ge(on_up, n0 + i + 1)
                        nc.tensor.matmul(PS[:, 4 + i, :], w("o"), OT[:, i, :], start=True,
                                         stop=True).then_inc(wo_mm, 1)

        @block.scalar
        def _(act):
            act.wait_ge(loaded, 16)
            act.sem_inc(g_up, 2)
            act.sem_inc(o_act, 1)
            act.wait_ge(gstat, 2)
            nc.scalar.preload_act_table_set(EXP_LN)
            nc.scalar.activation(GM[:, :, 1], GM[:, :, 1], ACT.Ln, bias=w("eps")).then_inc(glog, 1)
            act.wait_ge(glog, 1)
            nc.scalar.activation(GM[:, :, 1], GM[:, :, 1], ACT.Exp, scale=-0.5).then_inc(glog, 1)
            with act.Fori(0, 2) as pr:
                nc.scalar.preload_act_table_set(EXP_LN)
                with act.Fori(0, 4) as g:
                    norm.act(act, pr * 32 + g * 4)
                for i in range(IMG):
                    act.wait_ge(ab_t, pr * IMG + i + 1 + 2)
                    act.wait_ge(ab_up, pr * IMG + i + 1 - 2) if i >= 2 else None
                    nc.scalar.activation(SG[:, i % 2, :], T[:, i % 2, 2 * P:], ACT.Sigmoid).then_inc(ab_s, 1)
                    if i % 4 == 3:
                        q = i // 4
                        act.wait_ge(g_mm, pr * 16 + q + 1)
                        nc.scalar.activation(chunk(q), PS[:, 2 + q % 2, :], ACT.Sigmoid, bias=w("bg")).then_inc(g_up, 1)
                for c8 in range(0, NCOL, 2):
                    act.wait_ge(o_mm, pr * NCOL + c8 + 1)
                    nc.scalar.copy(AB[:, 0, :, c8 * 8:(c8 + 1) * 8].rearrange("p j c -> p c j"),
                                   PS[:, 4 + c8 % 2, :].rearrange("p (c j) -> p c j", c=8)).then_inc(o_act, 1)
                nc.scalar.preload_act_table_set(EXP_LN)
                for g in range(4):
                    n0 = pr * 16 + g * 4
                    for i in range(4):
                        act.wait_ge(t_up, n0 + i + 1)
                        act.wait_ge(y_up, n0 + i + 1)
                        nc.scalar.copy(OT[:, i, :], PS[:, 4 + i, :]).then_inc(t_out, 1)
                    norm.act(act, pr * 32 + 16 + g * 4)

        @block.gpsimd
        def _(pool):
            with pool.Fori(0, 2) as pr:
                for i in range(IMG):
                    pool.wait_ge(ab_s, pr * IMG + i + 1)
                    nc.gpsimd.tensor_tensor(AB[:, :, i, :], T[:, i % 2, 0:2 * P].rearrange("p (m c) -> p m c", m=2),
                                            SG[:, i % 2, :].rearrange("p (m c) -> p m c", m=2),
                                            ALU.mult).then_inc(ab_up, 1)

        @block.vector
        def _(dve):
            norm.begin(dve)
            dve.sem_inc(ab_t, 2)
            dve.sem_inc(o_dve, 1)
            dve.sem_inc(y_gate, 4)
            dve.sem_inc(y_up, 4)
            for b in range(NB):
                if x1 is not None:
                    dve.wait_ge(x_in[b], 16)
                for j in range(NCH):
                    at = b * TOK + j * CH
                    if b:
                        dve.wait_ge(stats, b * (NCH + 1))
                    nc.vector.bn_stats(ST[:, j, :], XR[:, at:at + CH]).then_inc(stats, 1)
                dve.wait_ge(stats, b * (NCH + 1) + NCH)
                nc.vector.bn_aggr(MV[:, b, :], ST[:, :, :]).then_inc(stats, 1)
            dve.wait_ge(stats, NB * (NCH + 1))
            nc.vector.tensor_tensor(GM[:, :, 0], MV[:, :, 0], MV[:, :, 0], ALU.mult).then_inc(stats, 1)
            dve.wait_ge(stats, NB * (NCH + 1) + 1)
            nc.vector.tensor_tensor(MV[:, :, 1], MV[:, :, 1], GM[:, :, 0], ALU.add).then_inc(stats, 1)
            dve.wait_ge(group, 1)
            nc.vector.tensor_copy(GM[:, :, :], PS[:, 0, 0:2 * NB].rearrange("p (b s) -> p b s", s=2)
                                  ).then_inc(group, 1)
            dve.wait_ge(group, 2)
            nc.vector.tensor_tensor(MV[:, :, 0], GM[:, :, 0], GM[:, :, 0], ALU.mult).then_inc(gstat, 1)
            dve.wait_ge(gstat, 1)
            nc.vector.tensor_tensor(GM[:, :, 1], GM[:, :, 1], MV[:, :, 0], ALU.subtract).then_inc(gstat, 1)
            dve.wait_ge(glog, 2)
            nc.vector.scalar_tensor_tensor(GM[:, :, 0], GM[:, :, 0], -1.0, GM[:, :, 1], ALU.mult,
                                           ALU.mult).then_inc(gstat, 1)
            dve.wait_ge(gstat, 3)
            with dve.Fori(0, 2) as pr:
                nc.vector.tensor_copy(MV[:, 0:2, :], GM[:, bass.ds(pr * 2, 2), :]).then_inc(gstat, 1)
                dve.wait_ge(gstat, pr + 4)
                for m in range(2):
                    nc.vector.tensor_scalar(G[:, :, m, :], XR[:, bass.ds(pr * PAIR + m * TOK, TOK)]
                                            .rearrange("p (i k) -> p i k", k=IMG),
                                            MV[:, m, 1:2], MV[:, m, 0:1], ALU.mult, ALU.add).then_inc(gn_up, 1)
                with dve.Fori(0, 4) as g:
                    n0 = pr * 32 + g * 4
                    for i in range(4):
                        dve.wait_ge(norm.scaled, n0 + i + 1)
                        nc.vector.scalar_tensor_tensor(
                            chunk(g * 4 + i), PS[:, i, :], w("ln1_g"), RST[:, i, :], ALU.mult,
                            ALU.mult).then_inc(norm.out, 1)
                    for i in range(4):
                        dve.wait_ge(norm.out, n0 + i + 1 + 4)
                        nc.vector.tensor_scalar(chunk(g * 4 + i), chunk(g * 4 + i), w("ln1_b"), None,
                                                ALU.add).then_inc(zn_up, 1)
                for i in range(IMG):
                    dve.wait_ge(ab_mm, pr * IMG + i + 1)
                    dve.wait_ge(ab_up, pr * IMG + i + 1 - 2) if i >= 2 else None
                    nc.vector.tensor_tensor(T[:, i % 2, :], PS[:, i % 2, :], w("ab_b"), ALU.add).then_inc(ab_t, 1)
                for c8 in range(1, NCOL, 2):
                    dve.wait_ge(o_mm, pr * NCOL + c8 + 1)
                    nc.vector.tensor_copy(AB[:, 0, :, c8 * 8:(c8 + 1) * 8].rearrange("p j c -> p c j"),
                                          PS[:, 4 + c8 % 2, :].rearrange("p (c j) -> p c j", c=8)
                                          ).then_inc(o_dve, 1)
                for g in range(4):
                    n0 = pr * 16 + g * 4
                    norm.dve(dve, pr * 32 + 16 + g * 4, lambda i: OT[:, i, :], w("ln2_g"))
                    for i in range(4):
                        dve.wait_ge(norm.out, pr * 32 + 16 + g * 4 + i + 1 + 4)
                        nc.vector.tensor_scalar(OT[:, i, :], OT[:, i, :], w("ln2_b"), None,
                                                ALU.add).then_inc(on_up, 1)
                    for i in range(4):
                        q = g * 4 + i
                        dve.wait_ge(wo_mm, n0 + i + 1)
                        for m in range(2):
                            gate = G[:, :, m, q * 4:q * 4 + 4].rearrange("p i j -> p j i")
                            ins = nc.vector.scalar_tensor_tensor(
                                OT[:, i, :].rearrange("p (j m t) -> p j m t", j=4, m=2)[:, :, m, :],
                                PS[:, 4 + i, :].rearrange("p (j m t) -> p j m t", j=4, m=2)[:, :, m, :],
                                w("bo"), gate, ALU.add, ALU.mult)
                        ins.then_inc(y_gate, 1)
                    for i in range(4):
                        q = g * 4 + i
                        dve.wait_ge(y_gate, n0 + i + 1 + 4)
                        x = XR[:, bass.ds(pr * PAIR, PAIR)].rearrange("p (t j) -> p j t", j=IMG)[:, q * 4:q * 4 + 4, :]
                        nc.vector.tensor_tensor(x, x, OT[:, i, :].rearrange("p (j t) -> p j t", j=4),
                                                ALU.add).then_inc(y_up, 1)


def layer2_attn(nc, pack, XR):
    with ExitStack() as ctx:
        def sb(name, shape, dt=F32):
            return ctx.enter_context(nc.sbuf_tensor("l2a_" + name, shape, dt))

        sem = semaphores(nc, ctx, "l2a_")

        where, width = places(PACK2)
        W = sb("W", [P, width])

        def w(name, a=0, n=None):
            at, size = where[name]
            return W[:, at + a:at + (size if n is None else a + n)]

        XN = sb("XN", [P, TOK])
        K = sb("K", [P, TOK])
        QT = sb("QT", [P, TOK])
        SQ = sb("SQ", [P, 4, CH])
        RST = sb("RST", [P, 4, CH])
        KM = sb("KM", [P, NCH])
        KV = sb("KV", [P, 3])
        QS = sb("QS", [P, 4, 16, 32])
        MX, SM = sb("MX", [P, 2, 16]), sb("SM", [P, 2, 16])
        VS, KT = sb("VS", [P, 4, 4, P]), sb("KT", [P, 4, 4, P])
        CT, MT = sb("CT", [P, P]), sb("MT", [P, P])
        ST = sb("ST", [P, NCH, 6])
        MV, GV = sb("MV", [P, 2]), sb("GV", [P, 4])
        NIL = sb("NIL", [P, 1])
        PS = ctx.enter_context(nc.psum_tensor("l2a_PS", [P, 8, CH], F32))
        KT_BANK, QT_BANK, CTX_BANK, MISC_BANK = 4, 5, 6, 7

        loaded = sem("loaded")
        k_mm, k_out, k_max, k_top = sem("k_mm"), sem("k_out"), sem("k_max"), sem("k_top")
        k_exp, k_rec = sem("k_exp"), sem("k_rec")
        qv_mm, q_max, q_sub, q_exp = sem("qv_mm"), sem("q_max"), sem("q_sub"), sem("q_exp")
        q_sum, q_rec, q_up = sem("q_sum"), sem("q_rec"), sem("q_up")
        v_out, kt_mm, kt_out, qt_mm, qt_out = sem("v_out"), sem("kt_mm"), sem("kt_out"), sem("qt_mm"), sem("qt_out")
        c_mm, c_up, m_mm, m_up = sem("c_mm"), sem("c_up"), sem("m_mm"), sem("m_up")
        o_mm, o_out, o_stat = sem("o_mm"), sem("o_out"), sem("o_stat")
        o_gn = sem("o_gn")
        gs_mm, gs, gs_log, o_norm, done = sem("gs_mm"), sem("gs"), sem("gs_log"), sem("o_norm"), sem("done")
        norm = Norm(nc, sem, PS, SQ, RST, w("center"), w("ones"), w("eps"))

        def c(j, buf=None):
            return (XN if buf is None else buf)[:, j * CH:(j + 1) * CH]

        def qv(g):
            return PS[:, (g % 2) * 2:(g % 2) * 2 + 2, :].rearrange("p a n -> p (a n)").rearrange(
                "p (t n) -> p t n", t=4)

        def heads(ap):
            return ap.rearrange("p t (h d) -> p t h d", d=32)

        def bc(small, g):
            return small[:, g % 2, :].rearrange("p (t h) -> p t h", t=4).unsqueeze(3).to_broadcast([P, 4, 4, 32])

        block = ctx.enter_context(nc.Block())

        @block.sync
        def _(sp):
            sp.dma_start(W[:, :], pack).then_inc(loaded, 16)

        @block.tensor
        def _(pe):
            pe.wait_ge(loaded, 16)
            with pe.Fori(0, NB) as b:
                for g in range(2):
                    norm.pe(pe, b * NCH + g * 4, lambda i: XR[:, bass.ds(b * TOK + (4 * g + i) * CH, CH)],
                            lambda i: pe.wait_ge(done, b * NCH + 1))
                for j in range(NCH):
                    pe.wait_ge(norm.out, b * NCH + NCH + 4)
                    pe.wait_ge(k_out, b * NCH + j + 1)
                    nc.tensor.matmul(PS[:, j % 4, :], w("k"), c(j), start=True, stop=True).then_inc(k_mm, 1)
                pe.wait_ge(k_out, b * NCH + NCH + 4)

                def context(g):
                    pe.wait_ge(q_up, b * NCH + g + 1)
                    pe.wait_ge(qt_out, b * NCH + g + 1)
                    for t in range(4):
                        ins = nc.tensor.transpose(PS[:, QT_BANK, t * P:(t + 1) * P],
                                                  QS[:, g % 4, 4 * t:4 * t + 4, :].rearrange("p h d -> p (h d)"),
                                                  w("ident"))
                    ins.then_inc(qt_mm, 1)
                    pe.wait_ge(v_out, b * NCH + g + 1 + 2)
                    pe.wait_ge(kt_out, b * NCH + g + 1 + 1)
                    for t in range(4):
                        ins = nc.tensor.matmul(PS[:, CTX_BANK, 0:P], KT[:, g % 4, t, :], VS[:, g % 4, t, :],
                                               start=(g == 0 and t == 0), stop=(g == NCH - 1 and t == 3))
                    ins.then_inc(c_mm, 1)

                for g in range(NCH):
                    pe.wait_ge(v_out, b * NCH + g + 1)
                    for t in range(4):
                        ins = nc.tensor.matmul(qv(g)[:, t, :], XN[:, (4 * g + t) * P:(4 * g + t + 1) * P],
                                               w("qv"), start=True, stop=True)
                    ins.then_inc(qv_mm, 1)
                    pe.wait_ge(k_exp, b + 1)
                    pe.wait_ge(kt_out, b * NCH + g + 1)
                    for t in range(4):
                        ins = nc.tensor.transpose(PS[:, KT_BANK, t * P:(t + 1) * P],
                                                  K[:, (4 * g + t) * P:(4 * g + t + 1) * P], w("ident"))
                    ins.then_inc(kt_mm, 1)
                    if g >= 2:
                        context(g - 2)
                context(NCH - 2)
                context(NCH - 1)
                pe.wait_ge(c_up, b + 1)
                nc.tensor.matmul(PS[:, MISC_BANK, 0:P], CT[:, :], w("out"), start=True, stop=True).then_inc(m_mm, 1)
                pe.wait_ge(m_up, b + 1)
                pe.wait_ge(qt_out, (b + 1) * NCH + 1)
                for j in range(NCH):
                    pe.wait_ge(o_out, b * NCH + j + 1)
                    nc.tensor.matmul(PS[:, j % 4, :], MT[:, :], c(j, QT), start=True, stop=True).then_inc(o_mm, 1)
                pe.wait_ge(gs, b * 7 + 3)
                nc.tensor.matmul(PS[:, MISC_BANK, 0:2], w("ones"), MV[:, :], start=True,
                                 stop=True).then_inc(gs_mm, 1)

        @block.scalar
        def _(act):
            act.wait_ge(loaded, 16)
            act.sem_inc(k_out, 4)
            act.sem_inc(v_out, 2)
            act.sem_inc(kt_out, 1)
            act.sem_inc(o_out, 4)
            nc.scalar.preload_act_table_set(EXP_LN)
            with act.Fori(0, NB) as b:
                for g in range(2):
                    norm.act(act, b * NCH + g * 4)
                for j in range(NCH):
                    act.wait_ge(k_mm, b * NCH + j + 1)
                    nc.scalar.copy(c(j, K), PS[:, j % 4, :]).then_inc(k_out, 1)
                act.wait_ge(k_top, b + 1)
                nc.scalar.activation(K[:, :], K[:, :], ACT.Exp, bias=KV[:, 0:1],
                                     accum_out=KV[:, 1:2]).then_inc(k_exp, 1)
                for g in range(NCH):
                    act.wait_ge(kt_mm, b * NCH + g + 1)
                    if g >= 4:
                        act.wait_ge(c_mm, b * NCH + g - 3)
                    nc.scalar.copy(KT[:, g % 4, :, :], PS[:, KT_BANK, :].rearrange("p (t n) -> p t n", t=4)
                                   ).then_inc(kt_out, 1)
                    act.wait_ge(q_sub, b * NCH + g + 1)
                    nc.scalar.copy(VS[:, g % 4, :, :], qv(g)[:, :, P:2 * P]).then_inc(v_out, 1)
                    nc.scalar.activation(QS[:, g % 4, :, :], QS[:, g % 4, :, :], ACT.Exp).then_inc(q_exp, 1)
                for j in range(NCH):
                    act.wait_ge(o_mm, b * NCH + j + 1)
                    nc.scalar.activation(c(j, K), PS[:, j % 4, :], ACT.Identity, bias=w("b_out")).then_inc(o_out, 1)
                act.wait_ge(gs, b * 7 + 6)
                nc.scalar.activation(GV[:, 1:2], GV[:, 1:2], ACT.Ln, bias=w("eps")).then_inc(gs_log, 1)
                act.wait_ge(gs_log, b * 2 + 1)
                nc.scalar.activation(GV[:, 1:2], GV[:, 1:2], ACT.Exp, scale=-0.5).then_inc(gs_log, 1)
                for j in range(NCH):
                    act.wait_ge(o_norm, b * 2 + 2)
                    nc.scalar.activation(c(j, K), c(j, K), ACT.Identity, scale=GV[:, 2:3],
                                         bias=GV[:, 3:4]).then_inc(o_gn, 1)

        @block.vector
        def _(dve):
            norm.begin(dve)
            dve.sem_inc(qt_out, 1)
            dve.sem_inc(done, 1)
            with dve.Fori(0, NB) as b:
                for g in range(2):
                    norm.dve(dve, b * NCH + g * 4, lambda i: c(4 * g + i))
                for j in range(NCH):
                    dve.wait_ge(k_out, b * NCH + j + 1 + 4)
                    nc.vector.tensor_reduce(KM[:, j:j + 1], c(j, K), AX_X, ALU.max).then_inc(k_max, 1)
                dve.wait_ge(k_max, (b + 1) * NCH)
                nc.vector.tensor_reduce(KV[:, 0:1], KM[:, :], AX_X, ALU.max, negate=True).then_inc(k_top, 1)
                dve.wait_ge(k_exp, b + 1)
                nc.vector.reciprocal(KV[:, 2:3], KV[:, 1:2]).then_inc(k_rec, 1)

                def scale_q(g):
                    n = b * NCH + g + 1
                    dve.wait_ge(q_exp, n)
                    nc.vector.tensor_reduce(SM[:, g % 2, :], QS[:, g % 4, :, :], AX_X, ALU.add).then_inc(q_sum, 1)
                    dve.wait_ge(q_sum, n)
                    nc.vector.reciprocal(SM[:, g % 2, :], SM[:, g % 2, :]).then_inc(q_rec, 1)
                    dve.wait_ge(q_rec, n)
                    q4 = QS[:, g % 4, :, :].rearrange("p (t h) d -> p t h d", t=4)
                    nc.vector.tensor_tensor(q4, q4, bc(SM, g), ALU.mult).then_inc(q_up, 1)

                def take_q(g):
                    dve.wait_ge(qt_mm, b * NCH + g + 1)
                    nc.vector.tensor_copy(c(g, QT), PS[:, QT_BANK, :]).then_inc(qt_out, 1)

                for g in range(NCH):
                    n = b * NCH + g + 1
                    q = heads(qv(g)[:, :, 0:P])
                    if g >= 3:
                        take_q(g - 3)
                    dve.wait_ge(qv_mm, n)
                    nc.vector.tensor_reduce(MX[:, g % 2, :].rearrange("p (t h) -> p t h", t=4), q, AX_X,
                                            ALU.max).then_inc(q_max, 1)
                    dve.wait_ge(q_max, n)
                    if g >= 4:
                        dve.wait_ge(qt_mm, n - 4)
                    nc.vector.tensor_tensor(QS[:, g % 4, :, :].rearrange("p (t h) d -> p t h d", t=4), q,
                                            bc(MX, g), ALU.subtract).then_inc(q_sub, 1)
                    if g >= 1:
                        scale_q(g - 1)
                scale_q(NCH - 1)
                take_q(NCH - 3)
                take_q(NCH - 2)
                take_q(NCH - 1)
                dve.wait_ge(c_mm, (b + 1) * NCH)
                dve.wait_ge(k_rec, b + 1)
                nc.vector.scalar_tensor_tensor(CT[:, :], PS[:, CTX_BANK, 0:P], KV[:, 2:3], w("heads"), ALU.mult,
                                               ALU.mult).then_inc(c_up, 1)
                dve.wait_ge(m_mm, b + 1)
                nc.vector.tensor_copy(MT[:, :], PS[:, MISC_BANK, 0:P]).then_inc(m_up, 1)
                for j in range(NCH):
                    dve.wait_ge(o_out, b * NCH + j + 1 + 4)
                    nc.vector.bn_stats(ST[:, j, :], c(j, K)).then_inc(o_stat, 1)
                dve.wait_ge(o_stat, (b + 1) * NCH)
                nc.vector.memset(NIL[:, :], 0.0)
                nc.vector.bn_aggr(MV[:, :], ST[:, :, :]).then_inc(gs, 1)
                dve.wait_ge(gs, b * 7 + 1)
                nc.vector.tensor_tensor(GV[:, 0:1], MV[:, 0:1], MV[:, 0:1], ALU.mult).then_inc(gs, 1)
                dve.wait_ge(gs, b * 7 + 2)
                nc.vector.tensor_tensor(MV[:, 1:2], MV[:, 1:2], GV[:, 0:1], ALU.add).then_inc(gs, 1)
                dve.wait_ge(gs_mm, b + 1)
                nc.vector.tensor_copy(GV[:, 0:2], PS[:, MISC_BANK, 0:2]).then_inc(gs, 1)
                dve.wait_ge(gs, b * 7 + 4)
                nc.vector.tensor_tensor(GV[:, 2:3], GV[:, 0:1], GV[:, 0:1], ALU.mult).then_inc(gs, 1)
                dve.wait_ge(gs, b * 7 + 5)
                nc.vector.tensor_tensor(GV[:, 1:2], GV[:, 1:2], GV[:, 2:3], ALU.subtract).then_inc(gs, 1)
                dve.wait_ge(gs_log, b * 2 + 2)
                nc.vector.tensor_tensor(GV[:, 2:3], GV[:, 1:2], w("gn_w"), ALU.mult).then_inc(gs, 1)
                dve.wait_ge(gs, b * 7 + 7)
                nc.vector.tensor_tensor(GV[:, 3:4], GV[:, 0:1], GV[:, 2:3], ALU.mult).then_inc(o_norm, 1)
                dve.wait_ge(o_norm, b * 2 + 1)
                nc.vector.tensor_tensor(GV[:, 3:4], w("gn_b"), GV[:, 3:4], ALU.subtract).then_inc(o_norm, 1)
                for j in range(NCH):
                    dve.wait_ge(o_gn, b * NCH + j + 1)
                    x = XR[:, bass.ds(b * TOK + j * CH, CH)]
                    nc.vector.tensor_tensor(x, x, c(j, K), ALU.add).then_inc(done, 1)


def layer2_ffn(nc, pack, XR):
    with ExitStack() as ctx:
        def sb(name, shape, dt=F32):
            return ctx.enter_context(nc.sbuf_tensor("l2f_" + name, shape, dt))

        sem = semaphores(nc, ctx, "l2f_")

        where, width = places(PACK2)
        W = sb("W", [P, width])

        def w(name, a=0, n=None):
            at, size = where[name]
            return W[:, at + a:at + (size if n is None else a + n)]

        E8, SENT = NEXP2, NEXP2 - TOP2
        XN = sb("XN", [P, TOK])
        SQ = sb("SQ", [P, 4, CH])
        RST = sb("RST", [P, 4, CH])
        LG = sb("LG", [P, 4, E8 + SENT])
        FOUND = sb("FOUND", [P, 4, E8 + SENT])
        M8, TOP = sb("M8", [P, 4, 8]), sb("TOP", [P, 4, 8])
        EX = sb("EX", [P, 4, E8])
        SM = sb("SM", [P, 4])
        NIL = sb("NIL", [P, 1])
        GATE = sb("GATE", [P, 2, 4, E8])
        GT = sb("GT", [E8, CH])
        PR = sb("PR", [P, 2, E8, P])
        H1 = sb("H1", [P, 2, E8 // 2, P])
        H2 = sb("H2", [P, 2, E8 // 4, P])
        PS = ctx.enter_context(nc.psum_tensor("l2f_PS", [P, 8, CH], F32))
        R_BANK, GT_BANK, Y_BANK = 4, 5, 6

        loaded, ready = sem("loaded"), sem("ready")
        r_mm, r_step, r_exp, gate_up = sem("r_mm"), sem("r_step"), sem("r_exp"), sem("gate_up")
        gt_mm, gt_up = sem("gt_mm"), sem("gt_up")
        e_mm, pr_up, h1_up, h2_up, y_mm, done = (sem(n) for n in ("e_mm", "pr_up", "h1_up", "h2_up", "y_mm", "done"))
        norm = Norm(nc, sem, PS, SQ, RST, w("center"), w("ones"), w("eps"))
        NT = NCH * 4
        STEPS = 15

        block = ctx.enter_context(nc.Block())

        @block.sync
        def _(sp):
            sp.dma_start(W[:, :], pack).then_inc(loaded, 16)

        @block.tensor
        def _(pe):
            pe.wait_ge(loaded, 16)
            with pe.Fori(0, NB) as b:
                for g in range(2):
                    norm.pe(pe, b * NCH + g * 4, lambda i: XR[:, bass.ds(b * TOK + (4 * g + i) * CH, CH)],
                            lambda i: pe.wait_ge(done, b * NCH + 2))

                def tile(t):
                    return XN[:, t * P:(t + 1) * P]

                def router(g):
                    pe.wait_ge(r_step, (b * NCH + g) * STEPS + 1)
                    for t in range(4):
                        ins = nc.tensor.matmul(PS[:, R_BANK, t * E8:(t + 1) * E8], tile(4 * g + t), w("router"),
                                               start=True, stop=True)
                    ins.then_inc(r_mm, 1)

                def biases(g):
                    pe.wait_ge(gate_up, b * NCH + g + 1)
                    for t in range(4):
                        ins = nc.tensor.transpose(PS[0:E8, GT_BANK, t * P:(t + 1) * P], GATE[:, g % 2, t, :],
                                                  w("ident"))
                    ins.then_inc(gt_mm, 1)
                    pe.wait_ge(gt_up, b * NCH + g + 1)
                    pe.wait_ge(done, b * NCH + g + 1)
                    nc.tensor.matmul(PS[:, Y_BANK + g % 2, :], w("expert_b")[0:E8, :], GT[:, :], start=True, stop=False)

                def experts(t):
                    pe.wait_ge(pr_up, b * NT + t + 1)
                    for half in range(2):
                        ins = nc.tensor.matmul(PS[:, (t % 2) * 2 + half, :], tile(t),
                                               w("experts", half * CH, CH), start=True, stop=True)
                    ins.then_inc(e_mm, 1)

                def sums(t):
                    pe.wait_ge(h2_up, b * NT + t + 1)
                    for half in range(2):
                        ins = nc.tensor.matmul(PS[:, Y_BANK + t // 4 % 2, (t % 4) * P:(t % 4 + 1) * P], H2[:, t % 2, half, :],
                                               w("ident"), start=False, stop=(half == 1 and t % 4 == 3))
                    ins.then_inc(y_mm, 1)

                pe.wait_ge(norm.out, b * NCH + NCH + 4)
                router(0)
                for t in range(NT + 2):
                    if t < NT:
                        experts(t)
                    if t % 4 == 0 and t + 4 < NT:
                        router(t // 4 + 1)
                    if t >= 2:
                        if t % 4 == 2:
                            biases(t // 4)
                        sums(t - 2)

        @block.scalar
        def _(act):
            nc.scalar.preload_act_table_set(EXP_LN)
            with act.Fori(0, NB) as b:
                for g in range(2):
                    norm.act(act, b * NCH + g * 4)
                for g in range(NCH):
                    act.wait_ge(r_step, (b * NCH + g + 1) * STEPS + 7)
                    nc.scalar.activation(EX[:, :, :], EX[:, :, :], ACT.Exp).then_inc(r_exp, 1)
                    act.wait_ge(gt_mm, b * NCH + g + 1)
                    if g >= 1:
                        act.wait_ge(y_mm, b * NT + 4 * g - 3)
                    nc.scalar.copy(GT[:, :], PS[0:E8, GT_BANK, :]).then_inc(gt_up, 1)

        @block.gpsimd
        def _(pool):
            pool.wait_ge(loaded, 16)
            with pool.Fori(0, NB) as b:
                for t in range(NT):
                    pool.wait_ge(pr_up, b * NT + t + 1 + 2)
                    nc.gpsimd.tensor_tensor(H1[:, t % 2, :, :], PR[:, t % 2, 0:4, :], PR[:, t % 2, 4:8, :],
                                            ALU.add).then_inc(h1_up, 1)
                    pool.wait_ge(h1_up, b * NT + t + 1)
                    if t >= 2:
                        pool.wait_ge(y_mm, b * NT + t - 1)
                    nc.gpsimd.tensor_tensor(H2[:, t % 2, :, :], H1[:, t % 2, 0:2, :], H1[:, t % 2, 2:4, :],
                                            ALU.add).then_inc(h2_up, 1)

        @block.vector
        def _(dve):
            norm.begin(dve)
            dve.sem_inc(done, 2)
            dve.sem_inc(pr_up, 2)
            nc.vector.memset(LG[:, :, E8:], -BIG).then_inc(ready, 1)
            nc.vector.memset(TOP[:, :, :], -BIG).then_inc(ready, 1)
            dve.wait_ge(ready, 2)
            dve.wait_ge(loaded, 16)
            dve.sem_inc(r_step, STEPS)
            with dve.Fori(0, NB) as b:
                for g in range(2):
                    norm.dve(dve, b * NCH + g * 4, lambda i: XN[:, (4 * g + i) * CH:(4 * g + i + 1) * CH])

                def after(g, steps):
                    dve.wait_ge(r_step, (b * NCH + g + 1) * STEPS + steps)

                def largest(g):
                    dve.wait_ge(r_mm, b * NCH + g + 1)
                    nc.vector.tensor_tensor(LG[:, :, 0:E8],
                                            PS[:, R_BANK, 0:4 * E8].rearrange("p (t e) -> p t e", t=4),
                                            w("router_b").rearrange("p (t e) -> p t e", t=4),
                                            ALU.add).then_inc(r_step, 1)
                    after(g, 1)
                    nc.vector.memset(NIL[:, :], 0.0)
                    for t in range(4):
                        nc.vector.max(M8[:, t, :], LG[:, t, 0:E8]).then_inc(r_step, 1)

                def chosen(g):
                    after(g, 5)
                    nc.vector.tensor_copy(TOP[:, :, 0:TOP2], M8[:, :, 0:TOP2]).then_inc(r_step, 1)
                    nc.vector.tensor_tensor(EX[:, :, :], LG[:, :, 0:E8],
                                            M8[:, :, 0:1].to_broadcast([P, 4, E8]),
                                            ALU.subtract).then_inc(r_step, 1)
                    after(g, 7)
                    nc.vector.memset(NIL[:, :], 0.0)
                    for t in range(4):
                        nc.vector.match_replace(FOUND[:, t, :], TOP[:, t, :], LG[:, t, :],
                                                BIG).then_inc(r_step, 1)

                def weights(g):
                    after(g, 11)
                    dve.wait_ge(r_exp, b * NCH + g + 1)
                    nc.vector.scalar_tensor_tensor(EX[:, :, :], FOUND[:, :, 0:E8], BIG / 2, EX[:, :, :],
                                                   ALU.is_ge, ALU.mult).then_inc(r_step, 1)
                    after(g, 12)
                    nc.vector.tensor_reduce(SM[:, :], EX[:, :, :], AX_X, ALU.add).then_inc(r_step, 1)
                    after(g, 13)
                    nc.vector.reciprocal(SM[:, :], SM[:, :]).then_inc(r_step, 1)

                def shares(g):
                    after(g, 14)
                    if g >= 2:
                        dve.wait_ge(gt_mm, b * NCH + g - 1)
                    nc.vector.tensor_tensor(GATE[:, g % 2, :, :], EX[:, :, :],
                                            SM[:, :].unsqueeze(2).to_broadcast([P, 4, E8]),
                                            ALU.mult).then_inc(gate_up, 1)
                    dve.wait_ge(gate_up, b * NCH + g + 1)
                    dve.sem_inc(r_step, STEPS - 14)

                def add_group(g):
                    dve.wait_ge(y_mm, b * NT + 4 * g + 4)
                    x = XR[:, bass.ds(b * TOK + g * CH, CH)]
                    nc.vector.tensor_tensor(x, x, PS[:, Y_BANK + g % 2, :], ALU.add).then_inc(done, 1)

                parts = (largest, chosen, weights, shares)
                for part in parts:
                    part(0)
                for g in range(NCH):
                    for t in range(4 * g, 4 * g + 4):
                        dve.wait_ge(e_mm, b * NT + t + 1)
                        if t >= 2:
                            dve.wait_ge(h1_up, b * NT + t - 1)
                        nc.vector.tensor_tensor(
                            PR[:, t % 2, :, :],
                            PS[:, (t % 2) * 2:(t % 2) * 2 + 2, :].rearrange("p a n -> p (a n)").rearrange(
                                "p (e c) -> p e c", e=E8),
                            GATE[:, g % 2, t % 4, :].unsqueeze(2).to_broadcast([P, E8, P]),
                            ALU.mult).then_inc(pr_up, 1)
                        if g + 1 < NCH:
                            parts[t % 4](g + 1)
                        if t % 4 == 2 and g:
                            add_group(g - 1)
                add_group(NCH - 1)


def layer3_attn(nc, pack, XR):
    with ExitStack() as ctx:
        def sb(name, shape, dt=F32):
            return ctx.enter_context(nc.sbuf_tensor("l3a_" + name, shape, dt))

        sem = semaphores(nc, ctx, "l3a_")

        where, width = places(PACK3)
        W = sb("W", [P, width])

        def w(name, a=0, n=None):
            at, size = where[name]
            return W[:, at + a:at + (size if n is None else a + n)]

        XN = sb("XN", [P, NTOK + CH])
        SQ = sb("SQ", [P, 4, CH])
        RST = sb("RST", [P, 4, CH])
        KS = SQ
        SC = sb("SC", [P, 5, CH])
        S, E, M, RU, U1 = (SC[:, n, :] for n in range(5))
        ONE = sb("ONE", [P, CH])
        END = sb("END", [P, 2])
        ET = sb("ET", [P, (NCH + 1) * 4, NB, HD])
        RT = sb("RT", [P, (NCH + 1) * 4, NB, HD])
        XS = sb("XS", [P, 2, CH])
        V = SC[:, 0:4, :].rearrange("p (a c) n -> p a (c n)", a=2).rearrange("p a (h d) -> p a h d", h=HD)
        WP = sb("WP", [P, 2, HD, P])
        Vs = RST[:, :, :].rearrange("p (a c) n -> p a (c n)", a=2)
        H1 = sb("H1", [P, 4, P])
        H2 = sb("H2", [P, 2, 2, P])
        Y = SQ[:, 0:2, :].rearrange("p a n -> p (a n)").rearrange("p (h d) -> p h d", h=HD)
        PS = ctx.enter_context(nc.psum_tensor("l3a_PS", [P, 8, CH], F32))

        loaded, zeroed = sem("loaded"), sem("zeroed")
        k_mm, k_up, s_mm = sem("k_mm"), sem("k_up"), sem("s_mm")
        s_out, s_max, s_sub, e_up, u_up, r_up = (sem(n) for n in ("s_out", "s_max", "s_sub", "e_up", "u_up", "r_up"))
        tr_up, tr_out = sem("tr_up"), sem("tr_out")
        xs_up, v_mm, v_up, ve_up, w_mm, w_up = (sem(n) for n in ("xs_up", "v_mm", "v_up", "ve_up", "w_mm", "w_up"))
        y_up, h1_up, h2_up, y_mm, done, fresh = (sem(n) for n in ("y_up", "h1_up", "h2_up", "y_mm", "done", "fresh"))
        norm = Norm(nc, sem, PS, SQ, RST, w("center"), w("ones"), w("eps"))
        S_BANK, E_BANK, R_BANK = 2, 4, 5
        NU = NB * HD
        TB = 8
        NT = TOK // P

        def q_col(p, h):
            return w("q", h * (2 * P - 1) + P - 1 - p, P)

        block = ctx.enter_context(nc.Block())

        @block.sync
        def _(sp):
            sp.dma_start(W[:, :], pack).then_inc(loaded, 16)

        @block.tensor
        def _(pe):
            pe.wait_ge(loaded, 16)
            with pe.Fori(0, NTOK // CH // 4) as g:
                norm.pe(pe, g * 4, lambda i: XR[:, bass.ds((g * 4 + i) * CH, CH)], lambda i: None)
            pe.wait_ge(norm.out, NTOK // CH + 4)

            def turn(j):
                pe.wait_ge(r_up, j + 1)
                pe.wait_ge(e_up, j + 1)
                pe.wait_ge(tr_out, j * 2 + 1)
                for src, bank in ((E, E_BANK), (RU, R_BANK)):
                    for t in range(4):
                        ins = nc.tensor.transpose(PS[:, bank, t * P:(t + 1) * P], src[:, t * P:(t + 1) * P],
                                                  w("ident"))
                ins.then_inc(tr_up, 1)

            with pe.Fori(0, NCH) as j:
                def score(u):
                    b, h = divmod(u, HD)
                    if u == 0:
                        pe.wait_ge(s_out, j + 1)
                    pe.wait_ge(k_up, j * NU + u + 1 + 2)
                    nc.tensor.matmul(PS[:, S_BANK, :], q_col(32 * b + h, h), KS[:, u % 2, :], start=(u == 0),
                                     stop=(u == NU - 1)).then_inc(s_mm, 1)

                for u in range(NU):
                    b, h = divmod(u, HD)
                    pe.wait_ge(k_up, j * NU + u + 1)
                    nc.tensor.matmul(PS[:, u % 2, :], w("k", h * P, P), XN[:, bass.ds(b * TOK + j * CH, CH)],
                                     start=True, stop=True).then_inc(k_mm, 1)
                    if u >= 1:
                        score(u - 1)
                    if u == 16:
                        turn(j)
                score(NU - 1)
            turn(NCH)
            pe.wait_ge(tr_out, NCH * 2 + 3)
            pe.wait_ge(k_up, NCH * NU + 2)

            with pe.Fori(0, NB) as b:
                with pe.Fori(0, NT // TB) as jj:
                    n0 = (b * (NT // TB) + jj) * TB
                    c0 = (b * (NT // TB) + jj) * 2

                    def values(t):
                        if t % 4 == 0:
                            pe.wait_ge(xs_up, c0 + t // 4 + 1)
                        pe.wait_ge(v_up, n0 + t + 1)
                        for half in range(2):
                            ins = nc.tensor.matmul(PS[:, (t % 2) * 6 + half, :],
                                                   XS[:, t // 4, (t % 4) * P:(t % 4 + 1) * P],
                                                   w("v", half * CH, CH), start=True, stop=True)
                        ins.then_inc(v_mm, 1)

                    def running(t):
                        pe.wait_ge(ve_up, n0 + t + 1 + 2)
                        pe.wait_ge(w_up, n0 + t + 2)
                        for half in range(2):
                            nc.tensor.matmul(PS[:, 2 + half, :], w("upto"),
                                             V[:, t % 2, 4 * half:4 * half + 4, :].rearrange("p h d -> p (h d)"),
                                             start=True, stop=False)
                            ins = nc.tensor.matmul(
                                PS[:, 2 + half, :], w("last"),
                                WP[:, (t + 1) % 2, 4 * half:4 * half + 4, :].rearrange("p h d -> p (h d)"),
                                start=False, stop=True)
                        ins.then_inc(w_mm, 1)

                    def result(t):
                        if t % 4 == 0:
                            pe.wait_ge(done, c0 + t // 4 + 1)
                        pe.wait_ge(h2_up, n0 + t + 1)
                        for half in range(2):
                            ins = nc.tensor.matmul(PS[:, 4 + t // 4, (t % 4) * P:(t % 4 + 1) * P],
                                                   H2[:, t % 2, half, :], w("ident"),
                                                   start=(half == 0), stop=(half == 1))
                        ins.then_inc(y_mm, 1)

                    values(0)
                    for t in range(TB):
                        if t + 1 < TB:
                            values(t + 1)
                        running(t)
                        if t >= 1:
                            result(t - 1)
                    result(TB - 1)

        @block.scalar
        def _(act):
            act.wait_ge(loaded, 16)
            nc.scalar.preload_act_table_set(EXP_LN)
            with act.Fori(0, NTOK // CH // 4) as g:
                norm.act(act, g * 4)
            act.wait_ge(norm.meaned, NTOK // CH)
            act.sem_inc(k_up, 2)
            act.sem_inc(v_up, 2)
            act.sem_inc(w_up, 2)

            def exponentials(n):
                act.wait_ge(s_sub, n)
                nc.scalar.activation(E, E, ACT.Exp).then_inc(e_up, 1)

            with act.Fori(0, NCH) as j:
                for u in range(NU):
                    if u == 6:
                        exponentials(j + 1)
                    act.wait_ge(k_mm, j * NU + u + 1)
                    if u >= 2:
                        act.wait_ge(s_mm, j * NU + u - 1)
                    nc.scalar.activation(KS[:, u % 2, :], PS[:, u % 2, :], ACT.Silu).then_inc(k_up, 1)
            exponentials(NCH + 1)
            nc.scalar.preload_act_table_set(SILU)
            with act.Fori(0, NB) as b:
                with act.Fori(0, NT // TB) as jj:
                    n0 = (b * (NT // TB) + jj) * TB

                    def keep(t):
                        act.wait_ge(w_mm, n0 + t + 1)
                        act.wait_ge(y_up, n0 + t + 1)
                        nc.scalar.copy(WP[:, t % 2, :, :].rearrange("p h d -> p (h d)"),
                                       PS[:, 2:4, :].rearrange("p a n -> p (a n)")).then_inc(w_up, 1)

                    act.wait_ge(fresh, b + 1)
                    for t in range(TB):
                        act.wait_ge(v_mm, n0 + t + 1)
                        act.wait_ge(ve_up, n0 + t + 1)
                        nc.scalar.activation(Vs[:, t % 2, :], PS[:, (t % 2) * 6:(t % 2) * 6 + 2, :]
                                             .rearrange("p a n -> p (a n)"), ACT.Silu).then_inc(v_up, 1)
                        if t >= 1:
                            keep(t - 1)
                    keep(TB - 1)

        @block.gpsimd
        def _(pool):
            nc.gpsimd.memset(ONE[:, :], 1.0).then_inc(zeroed, 1)
            nc.gpsimd.memset(XN[:, NTOK:], 0.0).then_inc(zeroed, 1)
            pool.wait_ge(norm.out, NTOK // CH + 4)
            pool.wait_ge(zeroed, 5)

            def still(u, at):
                nc.gpsimd.tensor_copy(XS[:, u, :], XN[:, bass.ds(at, CH)]).then_inc(xs_up, 1)

            still(0, 0)
            with pool.Fori(0, NB) as b:
                with pool.Fori(0, NT // TB) as jj:
                    n0 = (b * (NT // TB) + jj) * TB
                    pool.wait_ge(v_up, n0 + 2)
                    still(1, b * TOK + (jj * 2 + 1) * CH)
                    for t in range(TB):
                        pool.wait_ge(y_up, n0 + t + 1 + 2)
                        nc.gpsimd.tensor_tensor(H1[:, :, :], Y[:, 0:4, :], Y[:, 4:8, :], ALU.add).then_inc(h1_up, 1)
                        pool.wait_ge(h1_up, n0 + t + 1)
                        if t >= 2:
                            pool.wait_ge(y_mm, n0 + t - 1)
                        nc.gpsimd.tensor_tensor(H2[:, t % 2, :, :], H1[:, 0:2, :], H1[:, 2:4, :],
                                                ALU.add).then_inc(h2_up, 1)
                        pool.wait_ge(h2_up, n0 + t + 1)
                        if t == 3:
                            pool.wait_ge(v_up, n0 + 4 + 2)
                            still(0, b * TOK + (jj * 2 + 2) * CH)

        @block.vector
        def _(dve):
            norm.begin(dve)
            dve.sem_inc(s_out, 1)
            dve.sem_inc(tr_out, 2)
            dve.sem_inc(ve_up, 2)
            dve.sem_inc(y_up, 2)
            dve.sem_inc(done, 2)
            nc.vector.memset(E, 0.0).then_inc(zeroed, 1)
            nc.vector.memset(RU, 0.0).then_inc(r_up, 1)
            nc.vector.memset(END[:, 0:1], -BIG).then_inc(zeroed, 1)
            nc.vector.memset(END[:, 1:2], 0.0).then_inc(zeroed, 1)
            with dve.Fori(0, NTOK // CH // 4) as g:
                norm.dve(dve, g * 4, lambda i: XN[:, bass.ds((g * 4 + i) * CH, CH)])
            dve.wait_ge(zeroed, 5)
            dve.sem_inc(s_sub, 1)

            def take(j):
                dve.wait_ge(tr_up, j + 1)
                for dst, bank in ((ET, E_BANK), (RT, R_BANK)):
                    nc.vector.tensor_copy(dst[:, bass.ds(j * 4, 4), :, :],
                                          PS[:, bank, :].rearrange("p (t b h) -> p t b h", t=4, b=NB)[:, :, :, 0:HD]
                                          ).then_inc(tr_out, 1)

            with dve.Fori(0, NCH) as j:
                take(j)
                dve.wait_ge(s_mm, (j + 1) * NU)
                nc.vector.tensor_copy(S, PS[:, S_BANK, :]).then_inc(s_out, 1)
                dve.wait_ge(s_out, j + 2)
                nc.vector.tensor_tensor_scan(M, S, S, END[:, 0:1], ALU.max,
                                             ALU.max).then_inc(s_max, 1)
                dve.wait_ge(s_max, j * 2 + 1)
                nc.vector.tensor_copy(END[:, 0:1], M[:, CH - 1:CH]).then_inc(s_max, 1)
                nc.vector.tensor_tensor(E, S, M, ALU.subtract).then_inc(s_sub, 1)
                dve.wait_ge(e_up, j + 2)
                nc.vector.tensor_tensor_scan(U1, ONE[:, :], E, END[:, 1:2], ALU.mult,
                                             ALU.add).then_inc(u_up, 1)
                dve.wait_ge(u_up, j * 3 + 1)
                nc.vector.tensor_copy(END[:, 1:2], U1[:, CH - 1:CH]).then_inc(u_up, 1)
                nc.vector.reciprocal(RU, U1).then_inc(u_up, 1)
                dve.wait_ge(u_up, j * 3 + 3)
                nc.vector.tensor_scalar(RU, RU, 1.0 / HD, None, ALU.mult).then_inc(r_up, 1)
                dve.wait_ge(r_up, j + 2)
            take(NCH)
            dve.wait_ge(tr_out, NCH * 2 + 4)

            with dve.Fori(0, NB) as b:
                nc.vector.memset(WP[:, 1, :, :], 0.0).then_inc(fresh, 1)
                with dve.Fori(0, NT // TB) as jj:
                    n0 = (b * (NT // TB) + jj) * TB
                    c0 = (b * (NT // TB) + jj) * 2

                    def by_head(table, t):
                        return table[:, bass.ds((jj * TB + t + 4), 1), bass.ds(b, 1), :].rearrange(
                            "p t b h -> p (t b h)").unsqueeze(2).to_broadcast([P, HD, P])

                    def weigh(t):
                        dve.wait_ge(w_up, n0 + t + 1 + 2)
                        dve.wait_ge(h1_up, n0 + t) if t else None
                        nc.vector.tensor_tensor(Y[:, :, :], WP[:, t % 2, :, :], by_head(RT, t),
                                                ALU.mult).then_inc(y_up, 1)
                        if t % 4 == 3:
                            dve.wait_ge(y_mm, n0 + t + 1)
                            x = XR[:, bass.ds(b * TOK + (jj * 2 + t // 4) * CH, CH)]
                            nc.vector.tensor_tensor(x, x, PS[:, 4 + t // 4, :], ALU.add).then_inc(done, 1)

                    for t in range(TB):
                        dve.wait_ge(v_up, n0 + t + 1 + 2)
                        dve.wait_ge(w_up, n0 + t + 1)
                        nc.vector.tensor_tensor(V[:, t % 2, :, :], Vs[:, t % 2, :].rearrange("p (h d) -> p h d", h=HD),
                                                by_head(ET, t), ALU.mult).then_inc(ve_up, 1)
                        if t >= 1:
                            weigh(t - 1)
                    weigh(TB - 1)


def layer3_ffn(nc, pack, w1, w2, XR, out):
    with ExitStack() as ctx:
        def sb(name, shape, dt=F32):
            return ctx.enter_context(nc.sbuf_tensor("l3f_" + name, shape, dt))

        sem = semaphores(nc, ctx, "l3f_")

        where, width = places(PACK3F)
        W = sb("W", [P, width])

        def w(name, a=0, n=None):
            at, size = where[name]
            return W[:, at + a:at + (size if n is None else a + n)]

        QH = HID // P
        EG = 2
        XN = sb("XN", [P, 2 * TOK])
        SQ = sb("SQ", [P, 4, CH])
        RST = sb("RST", [P, 4, CH])
        PM = sb("PM", [P, 2, TOK])
        LG = sb("LG", [P, TOK])
        V4 = sb("V4", [P, 4])
        M8 = sb("M8", [P, 8])
        XT = sb("XT", [P, 2, 3 * P])
        PO = sb("PO", [P, NB, NEXP3])
        WR = sb("WR", [P, 2 * 2 * EG * HID])
        SLOTS, SLOT = 4, 2 * EG * HID

        def slot(u, part):
            buf = WR if u < 2 else LG
            at = u % 2 * SLOT + part * EG * HID
            return buf[:, at:at + EG * HID]

        W1 = [slot(u, 0).rearrange("p (e h) -> p e h", e=EG) for u in range(SLOTS)]
        W2 = [slot(u, 1).rearrange("p (e q m) -> p e q m", e=EG, q=QH) for u in range(SLOTS)]
        HS = sb("HS", [P, 2, EG, QH, NB])
        OT = sb("OT", [P, NB, NEXP3])
        OE = sb("OE", [P, NB, P])
        PS = ctx.enter_context(nc.psum_tensor("l3f_PS", [P, 8, CH], F32))

        loaded = sem("loaded")
        l_mm, l_out, l_max, p_exp, p_rec, p_up = (sem(n) for n in ("l_mm", "l_out", "l_max", "p_exp", "p_rec", "p_up"))
        top, marked, chosen = sem("top"), sem("marked"), sem("chosen")
        t_mm, t_out, po_mm, po_up = sem("t_mm"), sem("t_out"), sem("po_mm"), sem("po_up")
        w1_in = [sem("w1_in%d" % u) for u in range(SLOTS)]
        w2_in = [sem("w2_in%d" % u) for u in range(SLOTS)]
        h_mm, h_b, h_up, o_mm, o_up = (sem(n) for n in ("h_mm", "h_b", "h_up", "o_mm", "o_up"))
        oe_zero, oe_mm, oe_up, y_mm, y_up, stored = (
            sem(n) for n in ("oe_zero", "oe_mm", "oe_up", "y_mm", "y_up", "stored"))
        norm = Norm(nc, sem, PS, SQ, RST, w("center"), w("ones"), w("eps"))
        NT = TOK // P
        NG = NEXP3 // EG

        block = ctx.enter_context(nc.Block())

        @block.sync
        def _(sp):
            sp.dma_start(W[:, :], pack).then_inc(loaded, 16)
            for u in range(SLOTS):
                if u == 2:
                    sp.wait_ge(chosen, 2)
                sp.dma_start(W1[u], w1[:, u * EG:(u + 1) * EG, :]).then_inc(w1_in[u], 16)
                sp.dma_start(W2[u], w2[:, u * EG:(u + 1) * EG, :, :]).then_inc(w2_in[u], 16)
            with sp.Fori(1, NG // SLOTS) as gg:
                for u in range(SLOTS):
                    at = (gg * SLOTS + u) * EG
                    sp.wait_ge(h_mm, (gg - 1) * SLOTS + u + 1)
                    sp.dma_start(W1[u], w1[:, bass.ds(at, EG), :]).then_inc(w1_in[u], 16)
                    sp.wait_ge(o_mm, (gg - 1) * SLOTS + u + 1)
                    sp.dma_start(W2[u], w2[:, bass.ds(at, EG), :, :]).then_inc(w2_in[u], 16)
            for n in range(2 * NB):
                sp.wait_ge(y_up, (n + 1) * NCH // 2 + 4)
                at = n * TOK // 2
                sp.dma_start(out[:, at:at + TOK // 2], XR[:, at:at + TOK // 2]).then_inc(stored, 16)
            sp.wait_ge(stored, 2 * NB * 16)

        @block.tensor
        def _(pe):
            pe.wait_ge(loaded, 16)
            for pr in range(2):
                for g in range(4):
                    if pr and g == 0:
                        pe.wait_ge(t_out, NT + 2)
                        pe.wait_ge(po_up, 2)
                    norm.pe(pe, pr * 16 + g * 4,
                            lambda i: XR[:, pr * 2 * TOK + (4 * g + i) * CH:pr * 2 * TOK + (4 * g + i + 1) * CH],
                            lambda i: None)
                pe.wait_ge(norm.out, pr * 16 + 16 + 4)
                for j in range(NCH):
                    pe.wait_ge(l_out, pr * NCH + j + 1)
                    for m in range(2):
                        at = m * TOK + j * CH
                        ins = nc.tensor.matmul(PS[:, j % 4, :], w("gate", m * P, P), XN[:, at:at + CH],
                                               start=(m == 0), stop=(m == 1))
                    ins.then_inc(l_mm, 1)

                def pooled(t):
                    pe.wait_ge(t_out, pr * NT + t + 1 + 2)
                    for m in range(2):
                        ins = nc.tensor.matmul(PS[:, 6 + m, 0:NEXP3], XT[:, t % 2, m * P:(m + 1) * P],
                                               XT[:, t % 2, 2 * P + m * NEXP3:2 * P + (m + 1) * NEXP3],
                                               start=(t == 0), stop=(t == NT - 1))
                    ins.then_inc(po_mm, 1)

                pe.wait_ge(chosen, pr + 1)
                for t in range(NT):
                    pe.wait_ge(t_out, pr * NT + t + 1)
                    for n, src in enumerate((XN[:, t * P:(t + 1) * P], XN[:, TOK + t * P:TOK + (t + 1) * P],
                                             PM[:, pr, t * P:(t + 1) * P])):
                        ins = nc.tensor.transpose(PS[:, 4 + t % 2, n * P:(n + 1) * P], src, w("ident"))
                    ins.then_inc(t_mm, 1)
                    if t >= 1:
                        pooled(t - 1)
                pooled(NT - 1)

            pe.wait_ge(po_up, 4)
            with pe.Fori(0, NG // SLOTS) as gg:
                def hidden(u):
                    n = gg * SLOTS + u
                    pe.wait_ge(w1_in[u], (gg + 1) * 16)
                    pe.wait_ge(h_b, n + 1)
                    for e in range(EG):
                        for q in range(QH):
                            at = (e * QH + q) * NB
                            ins = nc.tensor.matmul(PS[:, u % 2, at:at + NB], W1[u][:, e, q * P:(q + 1) * P],
                                                   PO[:, :, bass.ds(n * EG + e, 1)].rearrange("p b e -> p (b e)"),
                                                   start=True, stop=True)
                    ins.then_inc(h_mm, 1)

                def second(u):
                    n = gg * SLOTS + u
                    pe.wait_ge(w2_in[u], (gg + 1) * 16)
                    pe.wait_ge(h_up, n + 1)
                    pe.wait_ge(o_up, n + 1)
                    for e in range(EG):
                        for q in range(QH):
                            ins = nc.tensor.matmul(PS[:, 2 + u % 2, e * NB:(e + 1) * NB], W2[u][:, e, q, :],
                                                   HS[:, u % 2, e, q, :], start=(q == 0), stop=(q == QH - 1))
                    ins.then_inc(o_mm, 1)

                hidden(0)
                for u in range(1, SLOTS):
                    hidden(u)
                    second(u - 1)
                second(SLOTS - 1)

            pe.wait_ge(o_up, NG + 2)
            for pr in range(2):
                nc.tensor.transpose(PS[:, 4 + pr, 0:P], OT[:, 2 * pr:2 * pr + 2, :].rearrange("p b e -> p (b e)"),
                                    w("ident")).then_inc(oe_mm, 1)
            pe.wait_ge(oe_up, NB)
            for n in range(NB * NCH):
                b, j = divmod(n, NCH)
                pe.wait_ge(y_up, n + 1)
                nc.tensor.matmul(PS[:, n % 4, :], OE[:, b, :], PM[:, b // 2, j * CH:(j + 1) * CH],
                                 start=True, stop=True).then_inc(y_mm, 1)

        @block.scalar
        def _(act):
            act.wait_ge(loaded, 16)
            act.sem_inc(l_out, 4)
            act.sem_inc(t_out, 2)
            nc.scalar.preload_act_table_set(EXP_LN)
            for pr in range(2):
                for g in range(4):
                    norm.act(act, pr * 16 + g * 4)
                for j in range(NCH):
                    act.wait_ge(l_mm, pr * NCH + j + 1)
                    if pr and j == 0:
                        act.wait_ge(chosen, pr)
                    nc.scalar.activation(LG[:, j * CH:(j + 1) * CH], PS[:, j % 4, :], ACT.Identity,
                                         bias=w("gate_b")).then_inc(l_out, 1)
                act.wait_ge(l_max, pr + 1)
                nc.scalar.activation(PM[:, pr, :], LG[:, :], ACT.Exp, bias=V4[:, 0:1],
                                     accum_out=V4[:, 1:2]).then_inc(p_exp, 1)
                for t in range(NT):
                    act.wait_ge(t_mm, pr * NT + t + 1)
                    if t >= 2:
                        act.wait_ge(po_mm, pr * NT + t - 1)
                    nc.scalar.copy(XT[:, t % 2, :], PS[:, 4 + t % 2, 0:3 * P]).then_inc(t_out, 1)
            nc.scalar.preload_act_table(ACT.Gelu)
            with act.Fori(0, NG // 2) as gg:
                for u in range(2):
                    act.wait_ge(h_b, gg * 2 + u + 1 + 2)
                    nc.scalar.activation(HS[:, u, :, :, :], HS[:, u, :, :, :], ACT.Gelu).then_inc(h_up, 1)

        @block.gpsimd
        def _(pool):
            nc.gpsimd.memset(OE[:, :, :], 0.0).then_inc(oe_zero, 1)

        @block.vector
        def _(dve):
            norm.begin(dve)
            dve.sem_inc(h_b, 2)
            dve.sem_inc(o_up, 2)
            dve.sem_inc(y_up, 4)
            for pr in range(2):
                for g in range(4):
                    norm.dve(dve, pr * 16 + g * 4, lambda i: XN[:, (4 * g + i) * CH:(4 * g + i + 1) * CH])
                dve.wait_ge(l_out, (pr + 1) * NCH + 4)
                nc.vector.tensor_reduce(V4[:, 0:1], LG[:, :], AX_X, ALU.max, negate=True).then_inc(l_max, 1)
                dve.wait_ge(p_exp, pr + 1)
                nc.vector.reciprocal(V4[:, 2:3], V4[:, 1:2]).then_inc(p_rec, 1)
                dve.wait_ge(p_rec, pr + 1)
                nc.vector.tensor_scalar(PM[:, pr, :], PM[:, pr, :], V4[:, 2:3], None, ALU.mult).then_inc(p_up, 1)
                dve.wait_ge(p_up, pr + 1)
                nc.vector.max(M8[:, :], PM[:, pr, :]).then_inc(top, 1)
                dve.wait_ge(top, pr + 1)
                nc.vector.match_replace(LG[:, :], M8[:, :], PM[:, pr, :], -1.0).then_inc(marked, 1)
                dve.wait_ge(marked, pr + 1)
                nc.vector.scalar_tensor_tensor(PM[:, pr, :], LG[:, :], 0.0, PM[:, pr, :], ALU.is_lt,
                                               ALU.mult).then_inc(chosen, 1)
                dve.wait_ge(po_mm, (pr + 1) * NT)
                nc.vector.tensor_copy(PO[:, 2 * pr:2 * pr + 2, :], PS[:, 6:8, 0:NEXP3]).then_inc(po_up, 2)
            with dve.Fori(0, NG // SLOTS) as gg:
                def with_b1(u):
                    n = gg * SLOTS + u
                    dve.wait_ge(h_mm, n + 1)
                    b1 = w("b1").rearrange("p (e q) -> p e q", q=QH)[:, bass.ds(n * EG, EG), :]
                    hid = HS[:, u % 2, :, :, :].rearrange("p e q b -> p (e q) b")
                    nc.vector.tensor_tensor(hid, PS[:, u % 2, 0:EG * QH * NB].rearrange("p (e b) -> p e b", b=NB),
                                            b1.rearrange("p e q -> p (e q)").unsqueeze(2)
                                            .to_broadcast([P, EG * QH, NB]), ALU.add).then_inc(h_b, 1)

                def with_b2(u):
                    n = gg * SLOTS + u
                    dve.wait_ge(o_mm, n + 1)
                    nc.vector.tensor_tensor(OT[:, :, bass.ds(n * EG, EG)].rearrange("p b e -> p e b"),
                                            PS[:, 2 + u % 2, 0:EG * NB].rearrange("p (e b) -> p e b", b=NB),
                                            w("b2")[:, bass.ds(n * EG, EG)].unsqueeze(2)
                                            .to_broadcast([P, EG, NB]), ALU.add).then_inc(o_up, 1)

                with_b1(0)
                for u in range(1, SLOTS):
                    with_b1(u)
                    with_b2(u - 1)
                with_b2(SLOTS - 1)
            dve.wait_ge(oe_zero, 1)
            for b in range(NB):
                s = slice((b % 2) * HALF, (b % 2 + 1) * HALF)
                dve.wait_ge(oe_mm, b // 2 + 1)
                nc.vector.tensor_copy(OE[s, b, :], PS[s, 4 + b // 2, 0:P]).then_inc(oe_up, 1)
            for n in range(NB * NCH):
                dve.wait_ge(y_mm, n + 1)
                x = XR[:, n * CH:(n + 1) * CH]
                nc.vector.tensor_tensor(x, x, PS[:, n % 4, :], ALU.add).then_inc(y_up, 1)


def program(nc, xT, p0, sel, p1, p2, p3, p3f, w1, w2, out):
    x1 = nc.dram_tensor("layer0_out", [P, NTOK], F32).ap()
    layer0(nc, xT, p0, sel, x1)
    with nc.sbuf_tensor("XR", [P, NTOK], F32) as XR:
        layer1(nc, x1, p1, XR)
        layer2_attn(nc, p2, XR)
        layer2_ffn(nc, p2, XR)
        layer3_attn(nc, p3, XR)
        layer3_ffn(nc, p3f, w1, w2, XR, out)


def _pack(np, names, parts):
    at, width = places(names)
    out = np.zeros((P, width), np.float32)
    for name, part in parts.items():
        for row, col, a in part if isinstance(part, list) else [(0, 0, part)]:
            a = np.asarray(a)
            a = a.reshape(-1, 1) if a.ndim == 1 else a
            out[row:row + a.shape[0], at[name][0] + col:at[name][0] + col + a.shape[1]] = a
    return out


def _common(np):
    return {"ident": np.eye(P), "ones": np.full((P, P), 1.0 / P), "center": np.eye(P) - 1.0 / P,
            "eps": np.full(P, 1e-5)}


def _pack0(np, i):
    i = {k[len("L0_conv_"):]: np.asarray(v) for k, v in i.items() if k.startswith("L0_")}
    h = HALF
    shuffled = lambda a: a.reshape(2, h, -1).swapaxes(0, 1).reshape(P, -1)
    parts = dict(_common(np))
    parts["cv12"] = [(0, 0, i["cv2_w"].T), (h, h, i["cv1_w"].T)]
    parts["cv2"] = [(0, m, i["cv2_w"].T) for m in (0, h)]
    for c in ("c1", "c2"):
        taps = i[c + "_w"]
        cols = (0, h) if c == "c1" else (0,)
        parts[c] = [(row * h, t * P + m, taps[row, t]) for row in range(2) for t in range(3) for m in cols]
        parts[c] += [(0, (3 + t) * P + m, taps[2, t]) for t in range(3) for m in cols]
    parts["c3"] = [(0, 0, i["c3_w"].T)]
    parts["in_xh"] = [(h, 0, i["in_proj_w"][:P].T)]
    parts["in_z"] = [(h, 0, i["in_proj_w"][P:].T)]
    xp = i["x_proj_w"]
    parts["xp_dt"] = [(0, k * P, xp[k, 0:4]) for k in range(NDIR)]
    parts["dt_w"] = [(0, k * P, i["dt_w"][k].T) for k in range(NDIR)]
    parts["bc"] = [(0, k * 96 + c * 32, xp[k, 4:].T) for k in range(NDIR) for c in range(3)]
    parts["out_proj"] = i["out_proj_w"]
    parts["cv"] = [(0, h, i["cv_w"].T)]
    parts["cv3"] = shuffled(i["cv3_w"]).T
    parts["dw"] = i["dw_w"].reshape(9, P).T
    parts["A_logs"] = i["A_logs"].reshape(NDIR, P, NST).transpose(1, 0, 2).reshape(P, -1)
    parts["Ds"] = i["Ds"].reshape(NDIR, P).T
    parts["dt_b"] = i["dt_b"].T
    parts["one"], parts["minus_one"] = np.ones((P, 1)), -np.ones((P, 1))
    for c in "gb":
        parts["cv12_" + c] = [(0, 0, i["cv2_" + c]), (h, 0, i["cv1_" + c])]
        parts["cv2_" + c] = [(m, 0, i["cv2_" + c]) for m in (0, h)]
        parts["cv3_" + c] = shuffled(i["cv3_" + c])
        parts["cv_" + c] = [(h, 0, i["cv_" + c])]
        for n in ("bn2_", "ln_"):
            parts[n + c] = i[n + c]
        for n in ("bn0_", "bn1_"):
            parts[n + c] = [(m, 0, i[n + c]) for m in (0, h)]
    parts["c1_b"] = [(m, 0, i["c1_b"]) for m in (0, h)]
    for n in ("c2_b", "c3_b", "dw_b"):
        parts[n] = i[n]
    return _pack(np, PACK0, parts)


def _selectors(np):
    out = np.zeros((96, 2 * NST, P), mybir.dt.np(BF16))
    for r in range(2 * NST):
        out[[r, 32 + r, 64 + r], r] = 1
    return out.reshape(96, -1)


def _pack1(np, i):
    i = {k[len("L1_conv_"):]: np.asarray(v) for k, v in i.items() if k.startswith("L1_")}
    parts = dict(_common(np))
    parts["group4"] = np.kron(np.eye(P // 4), np.full((4, 4), 0.25))
    names = ("a", "b", "ga", "gb")
    parts["ab"] = [(0, n * P, i["W" + s]) for n, s in enumerate(names)]
    parts["ab_b"] = [(0, n * P, np.broadcast_to(i["b" + s], (P, P))) for n, s in enumerate(names)]
    parts["g"], parts["o"] = i["Wg"], i["Wo"]
    for n in ("ln1_g", "ln1_b", "ln2_g", "ln2_b", "bg", "bo"):
        parts[n] = i[n]
    return _pack(np, PACK1, parts)


def _pack2(np, i):
    a = {k[len("L2_attn_"):]: np.asarray(v) for k, v in i.items() if k.startswith("L2_attn_")}
    f = {k[len("L2_ffn_"):]: np.asarray(v) for k, v in i.items() if k.startswith("L2_ffn_")}
    parts = dict(_common(np))
    parts["heads"] = np.kron(np.eye(4), np.full((32, 32), 32 ** -0.5))
    q, k, v = a["W_qkv"].reshape(3, P, P)
    parts["k"], parts["qv"], parts["out"] = k.T, [(0, 0, q.T), (0, P, v.T)], a["W_out"].T
    parts["b_out"], parts["gn_w"], parts["gn_b"] = a["b_out"], a["gn_w"], a["gn_b"]
    parts["router"] = f["router_w"]
    parts["router_b"] = np.broadcast_to(np.concatenate([f["router_b"]] * 4), (P, 4 * NEXP2))
    parts["experts"] = f["expert_w"].transpose(1, 0, 2).reshape(P, -1)
    parts["expert_b"] = [(0, 0, f["expert_b"])]
    return _pack(np, PACK2, parts)


def _pack3(np, i):
    a = {k[len("L3_attn_"):]: np.asarray(v) for k, v in i.items() if k.startswith("L3_attn_")}
    parts = dict(_common(np))
    parts["upto"] = np.triu(np.ones((P, P)))
    parts["last"] = [(P - 1, 0, np.ones((1, P)))]
    kv = a["W_kv"].reshape(HD, P, 2, P)
    parts["k"], parts["v"] = (kv[:, :, n].transpose(2, 0, 1).reshape(P, -1) for n in range(2))
    parts["q"] = [(0, h * (2 * P - 1) + P - 1, a["q_proj"][h]) for h in range(HD)]
    return _pack(np, PACK3, parts)


def _pack3f(np, i):
    f = {k[len("L3_ffn_"):]: np.asarray(v) for k, v in i.items() if k.startswith("L3_ffn_")}
    parts = dict(_common(np))
    parts["gate"] = [(0, 0, f["gate_w"].T), (0, P + HALF, f["gate_w"].T)]
    parts["gate_b"] = np.concatenate([f["gate_b"]] * 2)
    parts["b1"] = f["weight1"][:, P].reshape(NEXP3, HID // P, P).transpose(2, 0, 1).reshape(P, -1)
    parts["b2"] = f["weight2"][:, HID].T
    return _pack(np, PACK3F, parts)


def _experts(np, i):
    w1, w2 = np.asarray(i["L3_ffn_weight1"])[:, :P], np.asarray(i["L3_ffn_weight2"])[:, :HID]
    return {"w1": np.ascontiguousarray(w1.transpose(1, 0, 2)),
            "w2": np.ascontiguousarray(w2.reshape(NEXP3, HID // P, P, P).transpose(2, 0, 1, 3))}


def kernel(**inputs):
    import numpy as np
    import concourse.bacc as bacc
    from concourse.bass_utils import run_bass_kernel_spmd

    x = np.asarray(inputs["x"])
    arrays = {
        "xT": np.ascontiguousarray(x.reshape(NTOK, P).T),
        "p0": _pack0(np, inputs), "sel": _selectors(np), "p1": _pack1(np, inputs), "p2": _pack2(np, inputs),
        "p3": _pack3(np, inputs), "p3f": _pack3f(np, inputs), **_experts(np, inputs),
    }
    nc = bacc.Bacc("TRN2", target_bir_lowering=False, num_devices=1)
    args = {n: nc.dram_tensor(n, a.shape, mybir.dt.from_np(a.dtype), kind="ExternalInput").ap()
            for n, a in arrays.items()}
    args["out"] = nc.dram_tensor("out", (P, NTOK), F32, kind="ExternalOutput").ap()
    program(nc, **args)
    r = run_bass_kernel_spmd(nc, [arrays], core_ids=[0])
    return np.ascontiguousarray(r.results[0]["out"].T).reshape(x.shape)
```
